# Optimizing a Trainium2 kernel written in Bass

```python
import numpy as np
import jax
import jax.numpy as jnp

def _softmax(x, axis=-1):
    return jax.nn.softmax(x, axis=axis)

def _gelu(x):
    return jax.nn.gelu(x, approximate=True)

def _silu(x):
    return jax.nn.silu(x)

def _sigmoid(x):
    return jax.nn.sigmoid(x)

def _layernorm(x, axis=-1, eps=1e-05):
    m = jnp.mean(x, axis=axis, keepdims=True)
    v = jnp.var(x, axis=axis, keepdims=True)
    return (x - m) / jnp.sqrt(v + eps)

def _scatter_add(tgt, idx, src, axis=0):
    return tgt.at[idx].add(src)

def _segment_sum(src, seg, n):
    return jax.ops.segment_sum(src, seg, n)
kernel_name = 'mk_sandwich_d2_jaxref_r8_0ae7ab'

def setup_inputs(seed: int=0):
    np.random.seed(seed)
    _w = jnp.asarray

    def _L0_attn_setup():
        import jax, jax.numpy as jnp
        import numpy as np
        B, S, D = (2, 512, 256)
        H, DK, DV = (16, 128, 128)
        SEG = 64
        UPDATE = 'delta'
        CAUSAL = True
        key = jax.random.key(seed)
        ks = jax.random.split(key, 6)
        s = 0.02
        return {'x': jax.random.normal(ks[0], (B, S, D), jnp.float32), 'Wq': jax.random.normal(ks[1], (D, H * DK), jnp.float32) * s, 'Wk': jax.random.normal(ks[2], (D, H * DK), jnp.float32) * s, 'Wv': jax.random.normal(ks[3], (D, H * DV), jnp.float32) * s, 'Wo': jax.random.normal(ks[4], (H * DV, D), jnp.float32) * s, 'betas': jax.random.normal(ks[5], (1, H, 1, DV), jnp.float32)}
    _L0_attn_in = _L0_attn_setup()

    def _L0_ffn_setup():
        import jax, jax.numpy as jnp
        import numpy as np
        B, S, DIM = (2, 256, 256)
        E, K = (8, 2)
        H = DIM * 4 // 3
        key = jax.random.key(seed)
        ks = jax.random.split(key, 8)
        s = 0.02
        x = jax.random.normal(ks[0], (B, S, DIM), dtype=jnp.float32)
        sw1 = jax.random.normal(ks[1], (H, DIM), dtype=jnp.float32) * s
        sw2 = jax.random.normal(ks[2], (DIM, H), dtype=jnp.float32) * s
        sw3 = jax.random.normal(ks[3], (H, DIM), dtype=jnp.float32) * s
        ew1 = jax.random.normal(ks[4], (E, H, DIM), dtype=jnp.float32) * s
        ew2 = jax.random.normal(ks[5], (E, DIM, H), dtype=jnp.float32) * s
        ew3 = jax.random.normal(ks[6], (E, H, DIM), dtype=jnp.float32) * s
        wr = jax.random.normal(ks[7], (E, DIM), dtype=jnp.float32) * s
        return {'x': x, 'sw1': sw1, 'sw2': sw2, 'sw3': sw3, 'ew1': ew1, 'ew2': ew2, 'ew3': ew3, 'wr': wr}
    _L0_ffn_in = _L0_ffn_setup()

    def _L1_attn_setup():
        import math
        import jax, jax.numpy as jnp
        import numpy as np
        EMBED_DIM = 256
        NUM_HEADS = 16
        HEAD_DIM = EMBED_DIM // NUM_HEADS
        CHUNK = 128
        RMS_EPS = 1e-05

        def _build_slopes(n):

            def pow2(n):
                start = 2.0 ** (-2.0 ** (-(math.log2(n) - 3)))
                return [start * start ** i for i in range(n)]
            if math.log2(n).is_integer():
                s = pow2(n)
            else:
                closest = 2 ** math.floor(math.log2(n))
                s = pow2(closest) + pow2(2 * closest)[0::2][:n - closest]
            return jnp.asarray(s, dtype=jnp.float32)

        def _rotary(x_BTHD, offset=0):
            T, D = (x_BTHD.shape[1], x_BTHD.shape[-1])
            freq = (1.0 / 1024.0) ** jnp.linspace(0.0, 1.0, D // 4, dtype=jnp.float32)
            freq = jnp.concatenate([freq, jnp.zeros(D // 4, dtype=jnp.float32)])
            t = jnp.arange(offset, offset + T, dtype=jnp.float32)
            theta = t[:, None] * freq[None, :]
            cos = jnp.cos(theta)[None, :, None, :]
            sin = jnp.sin(theta)[None, :, None, :]
            x1, x2 = jnp.split(x_BTHD.astype(jnp.float32), 2, axis=-1)
            y1 = x1 * cos + x2 * sin
            y2 = -x1 * sin + x2 * cos
            return jnp.concatenate([y1, y2], axis=-1).astype(x_BTHD.dtype)

        def _lightning_attn(q, k, v, slopes):
            B, H, T, D = q.shape
            C = CHUNK
            NC = T // C
            r = jnp.exp(-slopes)
            i = jnp.arange(C, dtype=jnp.float32)
            q_decay = r[:, None] ** (i[None, :] + 1.0)
            k_decay = r[:, None] ** (C - 1.0 - i[None, :])
            diff = i[:, None] - i[None, :]
            mask = diff >= 0
            dmask = jnp.where(mask[None], r[:, None, None] ** jnp.where(mask, diff, 0.0)[None], 0.0)
            r_C = r ** float(C)

            def reshape_chunks(x):
                return x.reshape(B, H, NC, C, D).transpose(2, 0, 1, 3, 4)
            qc, kc, vc = (reshape_chunks(q), reshape_chunks(k), reshape_chunks(v))

            def step(kv, qkv):
                qi, ki, vi = qkv
                inter = jnp.einsum('bhcd,bhde->bhce', qi * q_decay[None, :, :, None], kv)
                scores = jnp.einsum('bhcd,bhsd->bhcs', qi, ki) * dmask[None]
                intra = jnp.einsum('bhcs,bhse->bhce', scores, vi)
                kv_new = r_C[None, :, None, None] * kv + jnp.einsum('bhcd,bhce->bhde', ki * k_decay[None, :, :, None], vi)
                return (kv_new, inter + intra)
            kv0 = jnp.zeros((B, H, D, D), dtype=q.dtype)
            _, out = jax.lax.scan(step, kv0, (qc, kc, vc))
            return out.transpose(1, 2, 0, 3, 4).reshape(B, H, T, D)

        def _rms_norm(x, w):
            var = jnp.mean(jnp.square(x), axis=-1, keepdims=True)
            return x * jax.lax.rsqrt(var + RMS_EPS) * w
        key = jax.random.key(seed)
        ks = jax.random.split(key, 6)
        sc = 1.0 / math.sqrt(EMBED_DIM)
        return {'x': jax.random.normal(ks[0], (4, 512, EMBED_DIM), dtype=jnp.float32), 'Wq': jax.random.normal(ks[1], (EMBED_DIM, EMBED_DIM), dtype=jnp.float32) * sc, 'Wk': jax.random.normal(ks[2], (EMBED_DIM, EMBED_DIM), dtype=jnp.float32) * sc, 'Wv': jax.random.normal(ks[3], (EMBED_DIM, EMBED_DIM), dtype=jnp.float32) * sc, 'Wo': jax.random.normal(ks[4], (EMBED_DIM, EMBED_DIM), dtype=jnp.float32) * sc, 'rms_w': jnp.ones((EMBED_DIM,), dtype=jnp.float32)}
    _L1_attn_in = _L1_attn_setup()

    def _L1_ffn_setup():
        import jax, jax.numpy as jnp
        import numpy as np
        HIDDEN = 256
        INTER = 704
        B, S = (2, 256)

        def _ternary(key, shape):
            return jax.random.randint(key, shape, -1, 2).astype(jnp.float32)
        key = jax.random.key(seed)
        ks = jax.random.split(key, 7)
        x = jax.random.normal(ks[0], (B, S, HIDDEN), dtype=jnp.float32)
        gate_w = _ternary(ks[1], (INTER, HIDDEN))
        up_w = _ternary(ks[2], (INTER, HIDDEN))
        down_w = _ternary(ks[3], (HIDDEN, INTER))
        gate_s = jax.random.uniform(ks[4], (INTER,), minval=0.01, maxval=0.1, dtype=jnp.float32)
        up_s = jax.random.uniform(ks[5], (INTER,), minval=0.01, maxval=0.1, dtype=jnp.float32)
        down_s = jax.random.uniform(ks[6], (HIDDEN,), minval=0.01, maxval=0.1, dtype=jnp.float32)
        return {'x': x, 'gate_w': gate_w, 'up_w': up_w, 'down_w': down_w, 'gate_s': gate_s, 'up_s': up_s, 'down_s': down_s}
    _L1_ffn_in = _L1_ffn_setup()
    _d = {'L0_attn_x': _L0_attn_in['x'], 'L0_attn_Wq': _L0_attn_in['Wq'], 'L0_attn_Wk': _L0_attn_in['Wk'], 'L0_attn_Wv': _L0_attn_in['Wv'], 'L0_attn_Wo': _L0_attn_in['Wo'], 'L0_attn_betas': _L0_attn_in['betas'], 'L0_ffn_sw1': _L0_ffn_in['sw1'], 'L0_ffn_sw2': _L0_ffn_in['sw2'], 'L0_ffn_sw3': _L0_ffn_in['sw3'], 'L0_ffn_ew1': _L0_ffn_in['ew1'], 'L0_ffn_ew2': _L0_ffn_in['ew2'], 'L0_ffn_ew3': _L0_ffn_in['ew3'], 'L0_ffn_wr': _L0_ffn_in['wr'], 'L1_attn_Wq': _L1_attn_in['Wq'], 'L1_attn_Wk': _L1_attn_in['Wk'], 'L1_attn_Wv': _L1_attn_in['Wv'], 'L1_attn_Wo': _L1_attn_in['Wo'], 'L1_attn_rms_w': _L1_attn_in['rms_w'], 'L1_ffn_gate_w': _L1_ffn_in['gate_w'], 'L1_ffn_up_w': _L1_ffn_in['up_w'], 'L1_ffn_down_w': _L1_ffn_in['down_w'], 'L1_ffn_gate_s': _L1_ffn_in['gate_s'], 'L1_ffn_up_s': _L1_ffn_in['up_s'], 'L1_ffn_down_s': _L1_ffn_in['down_s']}
    _x0 = _d['L0_attn_x']
    _d['L0_attn_x'] = jax.random.normal(jax.random.fold_in(jax.random.key(seed), 1), (4, 512, 256), dtype=_x0.dtype)
    del _x0
    return _d

def reference(L0_attn_x, L0_attn_Wq, L0_attn_Wk, L0_attn_Wv, L0_attn_Wo, L0_attn_betas, L0_ffn_sw1, L0_ffn_sw2, L0_ffn_sw3, L0_ffn_ew1, L0_ffn_ew2, L0_ffn_ew3, L0_ffn_wr, L1_attn_Wq, L1_attn_Wk, L1_attn_Wv, L1_attn_Wo, L1_attn_rms_w, L1_ffn_gate_w, L1_ffn_up_w, L1_ffn_down_w, L1_ffn_gate_s, L1_ffn_up_s, L1_ffn_down_s):

    def _L0_attn_ref(x, Wq, Wk, Wv, Wo, betas):
        import jax, jax.numpy as jnp
        import numpy as np
        B, S, D = (2, 512, 256)
        H, DK, DV = (16, 128, 128)
        SEG = 64
        UPDATE = 'delta'
        CAUSAL = True
        Bsz, seq, _ = x.shape
        nseg = seq // SEG
        q = (x @ Wq).reshape(Bsz, seq, H, DK).transpose(0, 2, 1, 3)
        k = (x @ Wk).reshape(Bsz, seq, H, DK).transpose(0, 2, 1, 3)
        v = (x @ Wv).reshape(Bsz, seq, H, DV).transpose(0, 2, 1, 3)
        qs = q.reshape(Bsz, H, nseg, SEG, DK).transpose(2, 0, 1, 3, 4)
        ks_ = k.reshape(Bsz, H, nseg, SEG, DK).transpose(2, 0, 1, 3, 4)
        vs = v.reshape(Bsz, H, nseg, SEG, DV).transpose(2, 0, 1, 3, 4)
        causal_mask = jnp.tril(jnp.ones((SEG, SEG), bool))
        scale = DK ** 0.5
        beta = jax.nn.sigmoid(betas)

        def step(carry, seg):
            mem, z = carry
            qq, kk, vv = seg
            sigma_q = jax.nn.elu(qq) + 1.0
            scores = jnp.einsum('bhsk,bhtk->bhst', qq, kk) / scale
            if CAUSAL:
                scores = jnp.where(causal_mask, scores, -jnp.inf)
            att_dot = jax.nn.softmax(scores, axis=-1) @ vv
            att_mem = sigma_q @ mem / (sigma_q @ z)
            sigma_k = jax.nn.elu(kk) + 1.0
            if UPDATE == 'linear':
                mem_new = mem + jnp.einsum('bhsk,bhsv->bhkv', sigma_k, vv)
            else:
                delta = vv - sigma_k @ mem / (sigma_k @ z)
                mem_new = mem + jnp.einsum('bhsk,bhsv->bhkv', sigma_k, delta)
            z_new = z + sigma_k.sum(axis=-2, keepdims=True).transpose(0, 1, 3, 2)
            att = beta * att_mem + (1.0 - beta) * att_dot
            out = att.reshape(Bsz, SEG, H * DV) @ Wo
            return ((mem_new, z_new), out)
        mem0 = jnp.zeros((Bsz, H, DK, DV), x.dtype)
        z0 = jnp.ones((Bsz, H, DK, 1), x.dtype) / DK
        _, outs = jax.lax.scan(step, (mem0, z0), (qs, ks_, vs))
        return outs.transpose(1, 0, 2, 3).reshape(Bsz, seq, D)

    def _L0_ffn_ref(x, sw1, sw2, sw3, ew1, ew2, ew3, wr):
        import jax, jax.numpy as jnp
        import numpy as np
        B, S, DIM = (2, 256, 256)
        E, K = (8, 2)
        H = DIM * 4 // 3
        shared = jax.nn.silu(x @ sw1.T) * (x @ sw3.T) @ sw2.T
        logits = x @ wr.T
        probs = jax.nn.softmax(logits, axis=-1)
        top_p, top_i = jax.lax.top_k(probs, K)
        top_p = top_p / jnp.sum(top_p, axis=-1, keepdims=True)
        gates = jnp.sum(jax.nn.one_hot(top_i, E, dtype=x.dtype) * top_p[..., None], axis=-2)
        u = jnp.einsum('bsd,ehd->bseh', x, ew1)
        v = jnp.einsum('bsd,ehd->bseh', x, ew3)
        h = jax.nn.silu(u) * v
        eo = jnp.einsum('bseh,edh->bsed', h, ew2)
        return shared + jnp.einsum('bsed,bse->bsd', eo, gates)

    def _L1_attn_ref(x, Wq, Wk, Wv, Wo, rms_w):
        import math
        import jax, jax.numpy as jnp
        import numpy as np
        EMBED_DIM = 256
        NUM_HEADS = 16
        HEAD_DIM = EMBED_DIM // NUM_HEADS
        CHUNK = 128
        RMS_EPS = 1e-05

        def _build_slopes(n):

            def pow2(n):
                start = 2.0 ** (-2.0 ** (-(math.log2(n) - 3)))
                return [start * start ** i for i in range(n)]
            if math.log2(n).is_integer():
                s = pow2(n)
            else:
                closest = 2 ** math.floor(math.log2(n))
                s = pow2(closest) + pow2(2 * closest)[0::2][:n - closest]
            return jnp.asarray(s, dtype=jnp.float32)

        def _rotary(x_BTHD, offset=0):
            T, D = (x_BTHD.shape[1], x_BTHD.shape[-1])
            freq = (1.0 / 1024.0) ** jnp.linspace(0.0, 1.0, D // 4, dtype=jnp.float32)
            freq = jnp.concatenate([freq, jnp.zeros(D // 4, dtype=jnp.float32)])
            t = jnp.arange(offset, offset + T, dtype=jnp.float32)
            theta = t[:, None] * freq[None, :]
            cos = jnp.cos(theta)[None, :, None, :]
            sin = jnp.sin(theta)[None, :, None, :]
            x1, x2 = jnp.split(x_BTHD.astype(jnp.float32), 2, axis=-1)
            y1 = x1 * cos + x2 * sin
            y2 = -x1 * sin + x2 * cos
            return jnp.concatenate([y1, y2], axis=-1).astype(x_BTHD.dtype)

        def _lightning_attn(q, k, v, slopes):
            B, H, T, D = q.shape
            C = CHUNK
            NC = T // C
            r = jnp.exp(-slopes)
            i = jnp.arange(C, dtype=jnp.float32)
            q_decay = r[:, None] ** (i[None, :] + 1.0)
            k_decay = r[:, None] ** (C - 1.0 - i[None, :])
            diff = i[:, None] - i[None, :]
            mask = diff >= 0
            dmask = jnp.where(mask[None], r[:, None, None] ** jnp.where(mask, diff, 0.0)[None], 0.0)
            r_C = r ** float(C)

            def reshape_chunks(x):
                return x.reshape(B, H, NC, C, D).transpose(2, 0, 1, 3, 4)
            qc, kc, vc = (reshape_chunks(q), reshape_chunks(k), reshape_chunks(v))

            def step(kv, qkv):
                qi, ki, vi = qkv
                inter = jnp.einsum('bhcd,bhde->bhce', qi * q_decay[None, :, :, None], kv)
                scores = jnp.einsum('bhcd,bhsd->bhcs', qi, ki) * dmask[None]
                intra = jnp.einsum('bhcs,bhse->bhce', scores, vi)
                kv_new = r_C[None, :, None, None] * kv + jnp.einsum('bhcd,bhce->bhde', ki * k_decay[None, :, :, None], vi)
                return (kv_new, inter + intra)
            kv0 = jnp.zeros((B, H, D, D), dtype=q.dtype)
            _, out = jax.lax.scan(step, kv0, (qc, kc, vc))
            return out.transpose(1, 2, 0, 3, 4).reshape(B, H, T, D)

        def _rms_norm(x, w):
            var = jnp.mean(jnp.square(x), axis=-1, keepdims=True)
            return x * jax.lax.rsqrt(var + RMS_EPS) * w
        B, T, E = x.shape
        H, D = (NUM_HEADS, HEAD_DIM)
        q = (x @ Wq).reshape(B, T, H, D)
        k = (x @ Wk).reshape(B, T, H, D)
        v = (x @ Wv).reshape(B, T, H, D)
        q = _rotary(q)
        k = _rotary(k)
        q, k, v = (t.transpose(0, 2, 1, 3) for t in (q, k, v))
        slopes = _build_slopes(H)
        attn = _lightning_attn(q, k, v, slopes)
        attn = attn.transpose(0, 2, 1, 3).reshape(B, T, E)
        attn = _rms_norm(attn, rms_w)
        return attn @ Wo

    def _L1_ffn_ref(x, gate_w, up_w, down_w, gate_s, up_s, down_s):
        import jax, jax.numpy as jnp
        import numpy as np
        HIDDEN = 256
        INTER = 704
        B, S = (2, 256)

        def _ternary(key, shape):
            return jax.random.randint(key, shape, -1, 2).astype(jnp.float32)
        b, s, h = x.shape
        xf = x.reshape(b * s, h)
        g = jnp.einsum('th,ih->ti', xf, gate_w) * gate_s
        u = jnp.einsum('th,ih->ti', xf, up_w) * up_s
        hdn = jax.nn.silu(g) * u
        out = jnp.einsum('ti,hi->th', hdn, down_w) * down_s
        return out.reshape(b, s, -1)
    x = L0_attn_x
    x = x + _layernorm(_L0_attn_ref(_layernorm(x, axis=-1), L0_attn_Wq, L0_attn_Wk, L0_attn_Wv, L0_attn_Wo, L0_attn_betas), axis=-1)
    x = x + _layernorm(_L0_ffn_ref(_layernorm(x, axis=-1), L0_ffn_sw1, L0_ffn_sw2, L0_ffn_sw3, L0_ffn_ew1, L0_ffn_ew2, L0_ffn_ew3, L0_ffn_wr), axis=-1)
    x = x + _layernorm(_L1_attn_ref(_layernorm(x, axis=-1), L1_attn_Wq, L1_attn_Wk, L1_attn_Wv, L1_attn_Wo, L1_attn_rms_w), axis=-1)
    x = x + _layernorm(_L1_ffn_ref(_layernorm(x, axis=-1), L1_ffn_gate_w, L1_ffn_up_w, L1_ffn_down_w, L1_ffn_gate_s, L1_ffn_up_s, L1_ffn_down_s), axis=-1)
    return x

_drawn_inputs = setup_inputs


def setup_inputs(seed=0):
    import zlib

    import numpy as np

    out = dict(_drawn_inputs(seed))
    spreads = {'L1_attn_rms_w': (1.0, 0.2)}
    factors = {}
    for name, (base, spread) in spreads.items():
        noise = np.random.default_rng([zlib.crc32(name.encode()), seed]).standard_normal(out[name].shape)
        drawn = base * np.exp(spread * noise) if base else spread * noise
        out[name] = jnp.asarray(drawn.astype(out[name].dtype))
    for name, factor in factors.items():
        out[name] = (out[name] * factor).astype(out[name].dtype)
    return out
```

```python
from contextlib import ExitStack

import concourse.bass as bass
from concourse import mybir

ALU = mybir.AluOpType
ACT = mybir.ActivationFunctionType
AX = mybir.AxisListType
F32 = mybir.dt.float32
F16 = mybir.dt.float16
U32 = mybir.dt.uint32
ds = bass.ds

P = 128
B, S, D = 4, 512, 256
TOK = B * S
TILES = TOK // P
TPB = S // P
KC = D // P
WSCALE = 64.0
LN_EPS = 1e-5

H0, DH, SEG = 16, 128, 64
PAIRS = H0 // 2
NSEG = S // SEG
E0, HID0 = 8, D * 4 // 3
HT0 = -(-(E0 + 1) * HID0 // P)
INTER = 704
HT1 = -(-INTER // P)
H1, DH1, CHUNK = 16, 16, 128


class Phase:

    def __init__(self, nc, ctx, name):
        self.nc, self.ctx, self.name = nc, ctx, name
        self.sems = []
        ctx.callback(self.clear)

    def sb(self, name, shape, dt=F32):
        return self.ctx.enter_context(self.nc.sbuf_tensor(f"{self.name}_{name}", shape, dt))

    def ps(self, name, shape, dt=F32):
        return self.ctx.enter_context(self.nc.psum_tensor(f"{self.name}_{name}", shape, dt))

    def sem(self, name):
        self.sems.append(self.nc.alloc_semaphore(f"{self.name}_{name}"))
        return self.sems[-1]

    def clear(self):
        self.nc.clear_and_free_semaphores(self.sems)
        self.nc.all_engine_barrier()


def bcast(ap, *shape):
    return ap.to_broadcast(list(shape))


def norm_phase(nc, name, ident, x, y, xt, load_x=None, store=None):
    with ExitStack() as ctx:
        ph = Phase(nc, ctx, name)
        xh = y if y is not None else ph.sb("xh", [P, TILES, D])
        stats = ph.sb("stats", [P, 2, TILES, 6])
        mean = ph.sb("mean", [P, 2, TILES])
        var = ph.sb("var", [P, 2, TILES])
        dif = ph.sb("dif", [P, 2, TILES])
        std = ph.sb("std", [P, 2, TILES])
        rstd = ph.sb("rstd", [P, 2, TILES])
        hi = ph.sb("hi", [P, TPB, D], F16)
        lo = ph.sb("lo", [P, TPB, D], F16)
        pt = [ph.ps(f"pt{i}", [P, KC, S], F16) for i in range(2)]
        x_in = ph.sem("x_in")
        dve = ph.sem("dve")
        var_ready = ph.sem("var_ready")
        std_ready = ph.sem("std_ready")
        xh_ready = ph.sem("xh_ready")
        hi_ready = ph.sem("hi_ready")
        lo_ready = ph.sem("lo_ready")
        t_ready = ph.sem("t_ready")
        thi_out = ph.sem("thi_out")
        tlo_out = ph.sem("tlo_out")
        x_done = ph.sem("x_done")
        stored = ph.sem("stored")
        n_std = (y is not None) + (store is None)

        with nc.Block() as block:
            @block.sync
            def _(sp):
                if load_x is not None:
                    src = load_x.rearrange("b (t p) d -> p b t d", p=P)
                    for b in range(B):
                        sp.dma_start(x[:, b * TPB:(b + 1) * TPB, :], src[:, b]).then_inc(x_in, 16)
                if store is not None:
                    dst = store.rearrange("b (t p) d -> p b t d", p=P)
                    sp.wait_ge(x_done, 1)
                    for b in range(B):
                        sp.dma_start(dst[:, b], x[:, b * TPB:(b + 1) * TPB, :]).then_inc(stored, 16)
                    sp.wait_ge(stored, 16 * B)

            @block.vector
            def _(v):
                done = [0]

                def own(ins, n=1):
                    ins.then_inc(dve, 1)
                    done[0] += n
                    v.wait_ge(dve, done[0])

                def moments(src, k, n):
                    with v.Fori(0, TILES) as t:
                        v.bn_stats(stats[:, k, ds(t, 1), :], src[:, ds(t, 1), :]).then_inc(dve, 1)
                    done[0] += TILES
                    v.wait_ge(dve, done[0])
                    st = stats[:, k]
                    own(v.tensor_tensor(mean[:, k], st[:, :, 1], st[:, :, 4], ALU.add))
                    own(v.tensor_tensor(dif[:, k], st[:, :, 1], st[:, :, 4], ALU.subtract))
                    own(v.tensor_tensor(dif[:, k], dif[:, k], dif[:, k], ALU.mult))
                    own(v.tensor_tensor(var[:, k], st[:, :, 2], st[:, :, 5], ALU.add))
                    own(v.tensor_scalar(mean[:, k], mean[:, k], 0.5, None, ALU.mult))
                    own(v.tensor_scalar(var[:, k], var[:, k], 1.0 / D, LN_EPS, ALU.mult, ALU.add))
                    v.scalar_tensor_tensor(var[:, k], dif[:, k], 0.25, var[:, k],
                                           ALU.mult, ALU.add).then_inc(var_ready, 1)
                    v.wait_ge(std_ready, n)
                    own(v.reciprocal(rstd[:, k], std[:, k]))

                if load_x is not None:
                    v.wait_ge(x_in, 16 * B)
                if y is not None:
                    moments(y, 0, 1)
                    with v.Fori(0, TILES) as t:
                        v.tensor_scalar(y[:, ds(t, 1), :], y[:, ds(t, 1), :], mean[:, 0, ds(t, 1)],
                                        rstd[:, 0, ds(t, 1)], ALU.subtract, ALU.mult).then_inc(dve, 1)
                    done[0] += TILES
                    v.wait_ge(dve, done[0])
                    own(v.tensor_tensor(x[:], x[:], y[:], ALU.add))
                if store is not None:
                    v.tensor_scalar(dif[:, 0], dif[:, 0], 0.0, None, ALU.mult).then_inc(x_done, 1)
                    return
                moments(x, 1, n_std)
                with v.Fori(0, TILES) as t:
                    v.tensor_scalar(xh[:, ds(t, 1), :], x[:, ds(t, 1), :], mean[:, 1, ds(t, 1)],
                                    rstd[:, 1, ds(t, 1)], ALU.subtract, ALU.mult).then_inc(xh_ready, 1)
                v.wait_ge(xh_ready, TILES)
                with v.Fori(0, B) as b:
                    v.wait_ge(hi_ready, b + 1)
                    v.tensor_tensor(lo[:], xh[:, ds(b * TPB, TPB), :], hi[:],
                                    ALU.subtract).then_inc(lo_ready, 1)
                    v.wait_ge(t_ready, b * 2 + 2)
                    v.tensor_copy(xt[:, 1, :, ds(b * S, S)], pt[1][:]).then_inc(tlo_out, 1)

            if store is None:
                @block.tensor
                def _(pe):
                    with pe.Fori(0, B) as b:
                        for part, (src, ready) in enumerate(((hi, hi_ready), (lo, lo_ready))):
                            pe.wait_ge(ready, b + 1)
                            for kc in range(KC):
                                for t in range(TPB):
                                    last = pe.transpose(pt[part][:, kc, t * P:(t + 1) * P],
                                                        src[:, t, kc * P:(kc + 1) * P], ident[:])
                            last.then_inc(t_ready, 1)

            @block.scalar
            def _(act):
                act.preload_act_table(ACT.Sqrt)
                for k in ([0] if y is not None else []) + ([1] if store is None else []):
                    n = 1 if k == 0 or y is None else 2
                    act.wait_ge(var_ready, n)
                    act.activation(std[:, k], var[:, k], ACT.Sqrt).then_inc(std_ready, 1)
                if store is not None:
                    return
                act.wait_ge(xh_ready, TILES)
                with act.Fori(0, B) as b:
                    act.activation(hi[:], xh[:, ds(b * TPB, TPB), :], ACT.Copy).then_inc(hi_ready, 1)
                    act.wait_ge(t_ready, b * 2 + 1)
                    act.activation(xt[:, 0, :, ds(b * S, S)], pt[0][:], ACT.Copy).then_inc(thi_out, 1)
                    act.wait_ge(tlo_out, b + 1)


def ffn_phase(nc, name, w_dram, xt, y, ht_n, ident, router=None, scales=None):
    WC = 2 * KC * P + D
    with ExitStack() as ctx:
        ph = Phase(nc, ctx, name)
        wst = ph.sb("wst", [P, 2, WC])
        wsc = ph.sb("wsc", [P, 1])
        w = ph.sb("w", [P, 2, ht_n, WC], F16)
        sil = ph.sb("sil", [P, 2, S])
        hv = ph.sb("hv", [P, 2, S])
        hh = ph.sb("hh", [P, 2, S], F16)
        hl = ph.sb("hl", [P, 2, S], F16)
        zero = ph.sb("zero", [P, S], F16)
        up = [ph.ps(f"up{i}", [P, 512]) for i in range(2)]
        vp = [ph.ps(f"vp{i}", [P, 512]) for i in range(2)]
        gp = [ph.ps(f"gp{i}", [P, 512]) for i in range(2)]
        yp = [ph.ps(f"yp{i}", [P, 2, D]) for i in range(2)]
        w_in = [ph.sem(f"w_in{i}") for i in range(2)]
        w_const = ph.sem("w_const")
        w_scaled = ph.sem("w_scaled")
        w_hi = ph.sem("w_hi")
        w_ready = ph.sem("w_ready")
        const_in = ph.sem("const_in")
        zeroed = ph.sem("zeroed")
        uvg = ph.sem("uvg")
        sil_ready = ph.sem("sil_ready")
        sv = ph.sem("sv")
        h_ready = ph.sem("h_ready")
        hh_ready = ph.sem("hh_ready")
        hl_ready = ph.sem("hl_ready")
        y_part = ph.sem("y_part")
        y_out = ph.sem("y_out")
        if router is not None:
            wr_dram, expand_dram = router
            wr32 = ph.sb("wr32", [P, KC, E0])
            wrp = ph.sb("wrp", [P, 2, KC, E0], F16)
            expand = ph.sb("expand", [P, ht_n * P], F16)
            lg = ph.sb("lg", [P, TILES, E0])
            mx = ph.sb("mx", [P, TILES])
            top = ph.sb("top", [P, TILES, 8])
            topi = ph.sb("topi", [P, TILES, 8], U32)
            topf = ph.sb("topf", [P, TILES, 8])
            eid = ph.sb("eid", [P, E0])
            gates = ph.sb("gates", [P, TILES, 16])
            pick = ph.sb("pick", [P, TILES, E0])
            gt32 = ph.sb("gt32", [P, TILES, 16])
            gparts = ph.sb("gparts", [P, 2, TILES, 16], F16)
            gt = ph.sb("gt", [P, 2, TOK], F16)
            wr_in = ph.sem("wr_in")
            rsem = ph.sem("rsem")
            r_logits = ph.sem("r_logits")
            r_sub = ph.sem("r_sub")
            r_exp = ph.sem("r_exp")
            r_gates = ph.sem("r_gates")
            r_ghi = ph.sem("r_ghi")
            r_glo = ph.sem("r_glo")
            r_t = ph.sem("r_t")
            r_tout = ph.sem("r_tout")
            r_w = ph.sem("r_w")
        if scales is not None:
            scaled = ph.sem("scaled")
            s1 = ph.sb("s1", [P, ht_n])
            s3 = ph.sb("s3", [P, ht_n])
            s2 = ph.sb("s2", [P, D])
        h_scale = WSCALE if scales is None else 1.0
        tg = [[bank[:].bitcast(F16) for bank in pair] for pair in (vp, gp)]

        with nc.Block() as block:
            @block.sync
            def _(sp):
                if router is not None:
                    with nc.allow_non_contiguous_dma(reason="a small table"):
                        sp.dma_start(wr32[:], wr_dram).then_inc(wr_in, 16)
                    sp.wait_ge(rsem, 1)
                    sp.dma_start(expand[0:E0 + 1, :], expand_dram).then_inc(const_in, 16)
                if scales is not None:
                    sp.dma_start(s1[:], scales[0]).then_inc(const_in, 16)
                    sp.dma_start(s3[:], scales[1]).then_inc(const_in, 16)
                    sp.dma_start(s2[:], scales[2].to_broadcast([P, D])).then_inc(const_in, 16)
                for t in range(2):
                    sp.dma_start(wst[:, t, :], w_dram[t]).then_inc(w_in[t], 16)
                with sp.Fori(1, ht_n // 2) as k:
                    for par in range(2):
                        sp.wait_ge(w_ready, k * 2 - 1 + par)
                        sp.dma_start(wst[:, par, :], w_dram[ds(k * 2 + par, 1)].rearrange(
                            "o p c -> p (o c)")).then_inc(w_in[par], 16)

            @block.gpsimd
            def _(pool):
                pool.memset(wsc[:], WSCALE).then_inc(w_const, 1)
                pool.wait_ge(w_const, 1)
                with pool.Fori(0, ht_n // 2) as k:
                    for par in range(2):
                        pool.wait_ge(w_in[par], k * 16 + 16)
                        pool.tensor_tensor(wst[:, par, :], wst[:, par, :], bcast(wsc[:], P, WC),
                                           ALU.mult).then_inc(w_scaled, 1)
                        pool.wait_ge(w_scaled, k * 2 + par + 1)
                        pool.tensor_copy(w[:, 0, ds(k * 2 + par, 1), :],
                                         wst[:, par, :]).then_inc(w_hi, 1)
                        pool.wait_ge(w_hi, k * 2 + par + 1)
                        pool.tensor_tensor(w[:, 1, ds(k * 2 + par, 1), :], wst[:, par, :],
                                           w[:, 0, ds(k * 2 + par, 1), :],
                                           ALU.subtract).then_inc(w_ready, 1)

            def wcol(part, ht, col, n):
                return w[:, part, ds(ht, 1), col:col + n].rearrange("p o c -> p (o c)") \
                    if not isinstance(ht, int) else w[:, part, ht, col:col + n]

            @block.tensor
            def _(pe):
                def three(out, wa, xa, start, stop):
                    for n, (i, j) in enumerate(((0, 0), (0, 1), (1, 0))):
                        last = pe.matmul(out, wa(i), xa(j), start=start and n == 0,
                                         stop=stop and n == 2, skip_group_check=True)
                    return last

                if router is not None:
                    pe.wait_ge(r_w, 3)
                    for t in range(TILES):
                        for kc in range(KC):
                            last = three(up[0][:, t * E0:(t + 1) * E0],
                                         lambda i: xt[:, i, kc, t * P:(t + 1) * P],
                                         lambda j: wrp[:, j, kc, :],
                                         t == 0 and kc == 0, t == TILES - 1 and kc == KC - 1)
                    last.then_inc(r_logits, 1)
                    pe.wait_ge(r_ghi, 1)
                    pe.wait_ge(r_glo, 1)
                    for part in range(2):
                        for t in range(TILES):
                            tgt = tg[part][t // 8]
                            last = pe.transpose(tgt[0:16, (t % 8) * P:(t % 8 + 1) * P],
                                                gparts[:, part, t, :], ident[:])
                        last.then_inc(r_t, 1)
                    pe.wait_ge(r_tout, 4)

                def products(s, b, ht, par):
                    for dst, col in ((up, 0), (vp, KC * P)):
                        for kc in range(KC):
                            last = three(dst[par][:], lambda i: wcol(i, ht, col + kc * P, P),
                                         lambda j: xt[:, j, kc, ds(b * S, S)], kc == 0, kc == KC - 1)
                    if router is not None:
                        for j in range(2):
                            last = pe.matmul(gp[par][:], expand[:, ds(ht * P, P)],
                                             gt[:, j, ds(b * S, S)], start=j == 0, stop=j == 1)
                    last.then_inc(uvg, 1)

                def down(s, ht, par):
                    pe.wait_ge(hh_ready, s + 1)
                    pe.wait_ge(hl_ready, s + 1)
                    for t in range(TPB):
                        src = (hh, hl)
                        last = three(yp[t // 2][:, t % 2, :],
                                     lambda i: src[i][:, par, t * P:(t + 1) * P],
                                     lambda j: wcol(j, ht, 2 * KC * P, D), False, False)
                    last.then_inc(y_part, 1)

                pe.wait_ge(zeroed, 1)
                with pe.Fori(0, B) as b:
                    s0 = b * ht_n
                    pe.wait_ge(y_out, b * 2 + 1)
                    for bank in yp:
                        pe.matmul(bank[:].rearrange("p a d -> p (a d)"), zero[:, 0:P], zero[:],
                                  start=True, stop=False, skip_group_check=True)
                    def step(ht, par):
                        pe.wait_ge(h_ready, s0 + ht + 1)
                        pe.wait_ge(w_ready, ht + 1)
                        products(None, b, ht, par)
                    step(0, 0)
                    with pe.Fori(0, ht_n // 2 - 1) as k:
                        step(k * 2 + 1, 1)
                        down(s0 + k * 2, k * 2, 0)
                        step(k * 2 + 2, 0)
                        down(s0 + k * 2 + 1, k * 2 + 1, 1)
                    step(ht_n - 1, 1)
                    down(s0 + ht_n - 2, ht_n - 2, 0)
                    down(s0 + ht_n - 1, ht_n - 1, 1)

            @block.scalar
            def _(act):
                if router is not None:
                    act.preload_act_table(ACT.Exp)
                    act.wait_ge(wr_in, 16)
                    act.activation(wrp[:, 0], wr32[:], ACT.Copy, scale=WSCALE).then_inc(r_w, 1)
                    act.wait_ge(r_sub, 1)
                    act.activation(lg[:], lg[:], ACT.Exp).then_inc(r_exp, 1)
                    act.wait_ge(r_gates, 1)
                    act.activation(gparts[:, 0], gt32[:], ACT.Copy).then_inc(r_ghi, 1)
                    for part in range(2):
                        act.wait_ge(r_t, part + 1)
                        for i in range(2):
                            act.activation(gt[0:16, part, i * 1024:(i + 1) * 1024], tg[part][i][0:16, :],
                                           ACT.Copy).then_inc(r_tout, 1)
                act.preload_act_table(ACT.Silu)
                if scales is not None:
                    act.wait_ge(scaled, 2)
                with act.Fori(0, B) as b:
                    with act.Fori(0, ht_n // 2) as k:
                        for par in range(2):
                            s = b * ht_n + k * 2 + par
                            act.wait_ge(uvg, s + 1)
                            sc = 1.0 / WSCALE if scales is None else s1[:, ds(k * 2 + par, 1)]
                            act.activation(sil[:, par], up[par][:], ACT.Silu,
                                           scale=sc).then_inc(sil_ready, 1)
                            act.wait_ge(h_ready, s + 3)
                            act.wait_ge(y_part, s + 1)
                            act.activation(hh[:, par], hv[:, par], ACT.Copy).then_inc(hh_ready, 1)
                    act.wait_ge(y_part, b * ht_n + ht_n + 2)
                    for i in range(2):
                        act.activation(y[:, ds(b * TPB + i * 2, 2), :], yp[i][:], ACT.Copy,
                                       scale=1.0 / (WSCALE * h_scale)).then_inc(y_out, 1)
            @block.vector
            def _(v):
                done = [0]
                own_sem = rsem if router is not None else zeroed

                def own(ins):
                    ins.then_inc(own_sem, 1)
                    done[0] += 1
                    v.wait_ge(own_sem, done[0])

                if router is not None:
                    own(v.memset(expand[:], 0.0))
                    own(v.memset(gt[:], 0.0))
                    own(v.memset(gt32[:], 0.0))
                v.memset(zero[:], 0.0).then_inc(zeroed, 1)
                if router is None:
                    done[0] += 1
                if router is not None:
                    for e in range(E0):
                        own(v.memset(eid[:, e:e + 1], float(e)))
                    v.wait_ge(r_w, 1)
                    v.scalar_tensor_tensor(wrp[:, 1], wr32[:], WSCALE, wrp[:, 0], ALU.mult,
                                           ALU.subtract).then_inc(r_w, 1)
                    v.wait_ge(const_in, 16)
                    v.sem_inc(r_w, 1)
                    v.wait_ge(r_logits, 1)
                    flat = up[0][:, 0:TILES * E0].rearrange("p (t e) -> p t e", e=E0)
                    own(v.tensor_scalar(lg[:], flat, 1.0 / WSCALE, None, ALU.mult))
                    own(v.tensor_reduce(mx[:], lg[:], AX.X, ALU.max))
                    v.tensor_tensor(lg[:], lg[:], bcast(mx[:].unsqueeze(2), P, TILES, E0),
                                    ALU.subtract).then_inc(r_sub, 1)
                    v.wait_ge(r_exp, 1)
                    own(v.tensor_reduce(mx[:], lg[:], AX.X, ALU.add))
                    own(v.reciprocal(mx[:], mx[:]))
                    own(v.tensor_tensor(lg[:], lg[:], bcast(mx[:].unsqueeze(2), P, TILES, E0), ALU.mult))
                    for t in range(TILES):
                        own(v.max(top[:, t, :], lg[:, t, :]))
                        own(v.max_index(topi[:, t, :], top[:, t, :], lg[:, t, :]))
                    own(v.tensor_copy(topf[:], topi[:]))
                    own(v.tensor_tensor(mx[:], top[:, :, 0], top[:, :, 1], ALU.add))
                    own(v.reciprocal(mx[:], mx[:]))
                    own(v.tensor_tensor(top[:, :, 0:2], top[:, :, 0:2],
                                        bcast(mx[:].unsqueeze(2), P, TILES, 2), ALU.mult))
                    ids = bcast(eid[:].unsqueeze(1), P, TILES, E0)
                    for r in range(2):
                        own(v.tensor_tensor(pick[:], bcast(topf[:, :, r:r + 1], P, TILES, E0), ids,
                                            ALU.is_equal))
                        own(v.tensor_tensor(pick[:], pick[:], bcast(top[:, :, r:r + 1], P, TILES, E0),
                                            ALU.mult))
                        own(v.tensor_tensor(gt32[:, :, 1:1 + E0], gt32[:, :, 1:1 + E0], pick[:], ALU.add))
                    v.memset(gt32[:, :, 0:1], 1.0).then_inc(r_gates, 1)
                    v.wait_ge(r_ghi, 1)
                    v.tensor_tensor(gparts[:, 1], gt32[:], gparts[:, 0], ALU.subtract).then_inc(r_glo, 1)
                for n in range(2):
                    v.sem_inc(h_ready, 1)
                    v.sem_inc(y_part, 1)
                v.sem_inc(y_out, 1)
                if scales is not None:
                    v.wait_ge(const_in, 48)
                    v.tensor_scalar(s1[:], s1[:], 1.0 / WSCALE, None, ALU.mult).then_inc(scaled, 1)
                    v.tensor_scalar(s3[:], s3[:], 1.0 / WSCALE, None, ALU.mult).then_inc(scaled, 1)
                    v.wait_ge(scaled, 2)
                with v.Fori(0, B) as b:
                    with v.Fori(0, ht_n // 2) as k:
                        for par in range(2):
                            s = b * ht_n + k * 2 + par
                            v.wait_ge(uvg, s + 1)
                            v.wait_ge(sil_ready, s + 1)
                            if router is not None:
                                v.tensor_tensor(hv[:, par], vp[par][:], sil[:, par],
                                                ALU.mult).then_inc(sv, 1)
                                v.wait_ge(sv, s + 1)
                                v.tensor_tensor(hv[:, par], hv[:, par], gp[par][:],
                                                ALU.mult).then_inc(h_ready, 1)
                            else:
                                v.scalar_tensor_tensor(hv[:, par], vp[par][:], s3[:, ds(k * 2 + par, 1)],
                                                       sil[:, par], ALU.mult,
                                                       ALU.mult).then_inc(h_ready, 1)
                            v.wait_ge(hh_ready, s + 1)
                            v.tensor_tensor(hl[:, par], hv[:, par], hh[:, par],
                                            ALU.subtract).then_inc(hl_ready, 1)
                if scales is not None:
                    v.wait_ge(y_out, B * 2 + 1)
                    v.tensor_tensor(y[:], y[:], bcast(s2[:].unsqueeze(1), P, TILES, D), ALU.mult)


def attn0_phase(nc, w_dram, betas, mask_dram, xt, y, ident):
    WC = 4 * 2 * D
    QC, KC0, VC, OC = (n * 2 * D for n in range(4))
    HALF = ((slice(0, SEG), slice(SEG, P)), (slice(SEG, P), slice(0, SEG)))
    NA = 8
    ROWS16 = H0
    GROUPS = SEG // H0
    with ExitStack() as ctx:
        ph = Phase(nc, ctx, "a0")
        w = ph.sb("w", [P, 2, PAIRS, WC], F16)
        wst = ph.sb("wst", [P, WC // 2])
        wsc = ph.sb("wsc", [P, 2])
        beta = ph.sb("beta", [P, H0 * DH])
        omb = ph.sb("omb", [P, 2 * DH])
        mask = ph.sb("mask", [P, SEG])
        qs = ph.sb("qs", [P, 2, 2, S], F16)
        ks = ph.sb("ks", [P, 2, 2, S], F16)
        ee = ph.sb("ee", [P, 2, S])
        sg = ph.sb("sg", [P, 2, 2, 2, TPB, 4, SEG], F16)
        skr = ph.sb("skr", [P, 2, 2, 2, TPB, P], F16)
        v32 = ph.sb("v32", [P, 2, TPB, 2 * DH])
        vb = ph.sb("vb", [P, TPB, 2 * DH])
        vs = ph.sb("vs", [P, 2, 2, TPB, 2 * DH], F16)
        sm = ph.sb("sm", [P, 2 * TPB, SEG])
        ex = ph.sb("ex", [P, 2 * TPB, SEG])
        red = ph.sb("red", [P, 2 * TPB])
        ps = ph.sb("ps", [P, 2, 2 * TPB, SEG], F16)
        ptb = ph.sb("ptb", [P, 2, 2, 2, TPB, P], F16)
        ms = ph.sb("ms", [P, 2, 2, 2, DH + 2], F16)
        ms0 = ph.sb("ms0", [P, 2, 2, DH + 2], F16)
        d32 = ph.sb("d32", [P, 2, DH])
        dd = ph.sb("dd", [P, 2, 2, 2, DH + 2], F16)
        rd = ph.sb("rd", [P, 2])
        at = ph.sb("at", [P, TPB, 2 * DH])
        ats = ph.sb("ats", [P, 2, TPB, 2 * DH], F16)
        att = ph.sb("att", [P, 2, ROWS16, P], F16)
        yst = ph.sb("yst", [P, D])
        zi = ph.sb("zi", [P, 2, DH * 2], F16)
        ones = ph.sb("ones", [P, P], F16)
        yp = ph.ps("yp", [P, 2, D])
        mem = ph.ps("mem", [P, 2, 256])
        num = ph.ps("num", [P, 2, 256])
        pj = [ph.ps(f"pj{i}", [P, S]) for i in range(2)]
        tr = [ph.ps(f"tr{i}", [P, S]) for i in range(2)]
        tr16 = [t[:].bitcast(F16) for t in tr]

        names = ("w_in w_sc w_hi w_ready const_in beta_r init pj_full hi_r ex_r e1_r lo_r sg64 sghi sglo"
                 " skr_full skrhi skrlo v_r omb_r vb_r vhi vlo s_full sm_r mx_r sd_r pex_r sum_r ri_r pn_r"
                 " phi plo pt_full pthi ptlo num_full rd_r d_r dhi dlo a_r mem_full mhi mlo dot_full at_r"
                 " ahi alo att_full atthi attlo y_full y_out y_in yst_free").split()
        m = {n: ph.sem(n) for n in names}

        def three(pe, out, wa, xa, start=False, stop=False):
            for n, (i, j) in enumerate(((0, 0), (0, 1), (1, 0))):
                last = pe.matmul(out, wa(i), xa(j), start=start and n == 0, stop=stop and n == 2,
                                 skip_group_check=True)
            return last

        def pairs(eng, chunk, retrieve, update, tail, end):
            for c in range(NA):
                chunk(c, 0, 0, 0, 0)
            with eng.Fori(0, B) as b:
                with eng.Fori(0, PAIRS // 2) as k:
                    for par in range(2):
                        hp = k * 2 + par
                        g = b * PAIRS + hp
                        n = g + 1
                        for j in range(NSEG):
                            retrieve(j, g, hp, par)
                            chunk(j, n, (n // PAIRS) % B, n % PAIRS, 1 - par)
                            update(j, g, hp, par)
                        tail(g, hp, par)
                    end(b * (PAIRS // 2) + k, b, k)

        def keys(par, part, c):
            return sg[:, par, part, c, :, 0::3, :]

        def queries(par, part, c):
            return sg[:, par, part, c, :, 1:3, :]

        def probs_t(part, odd):
            return tr16[part][0:SEG, :].rearrange("p (c t o s) -> p c t o s", c=2, t=TPB, o=2)[:, :, :, odd, :]

        def att_from(part, c):
            return tr16[part][:, c * S:(c + 1) * S].rearrange("p (s a r) -> p s a r", a=GROUPS, r=ROWS16)

        def att_in(part, par, c):
            o = (par * 2 + c) * GROUPS
            return att[:, part].rearrange("p r (s m) -> p s m r", s=NSEG)[:, :, o:o + GROUPS, :]

        with nc.Block() as block:
            @block.sync
            def _(sp):
                sp.dma_start(mask[:], mask_dram).then_inc(m["const_in"], 16)
                sp.dma_start(beta[:], betas.to_broadcast([P, H0 * DH])).then_inc(m["const_in"], 16)
                sp.dma_start(wst[:], w_dram[0, :, 0:WC // 2]).then_inc(m["w_in"], 16)
                sp.wait_ge(m["w_ready"], 1)
                sp.dma_start(wst[:], w_dram[0, :, WC // 2:]).then_inc(m["w_in"], 16)
                with sp.Fori(1, PAIRS) as hp:
                    for half in range(2):
                        sp.wait_ge(m["w_ready"], hp * 2 + half)
                        sp.dma_start(wst[:], w_dram[ds(hp, 1), :, half * WC // 2:(half + 1) * WC // 2]
                                     .rearrange("o p c -> p (o c)")).then_inc(m["w_in"], 16)

                sp.sem_inc(m["yst_free"], 1)
                with sp.Fori(0, B) as b:
                    for k in range(PAIRS // 2):
                        sp.wait_ge(m["y_out"], b * (PAIRS // 2) + k + 1)
                        for s in range(NSEG):
                            t, odd = s // 2, 1 - s % 2
                            row = odd * SEG + k * (SEG // 4)
                            sp.dma_start(y[row:row + SEG // 4, ds(b * TPB + t, 1), :],
                                         yst[s * 16:(s + 1) * 16, :].unsqueeze(1)).then_inc(m["y_in"], 16)
                        sp.wait_ge(m["y_in"], (b * (PAIRS // 2) + k + 1) * NSEG * 16)
                        sp.sem_inc(m["yst_free"], 1)

            @block.gpsimd
            def _(pool):
                pool.memset(wsc[:, 0:1], WSCALE).then_inc(m["w_sc"], 1)
                pool.memset(wsc[:, 1:2], 1.0).then_inc(m["w_sc"], 1)
                pool.wait_ge(m["w_sc"], 2)
                with pool.Fori(0, PAIRS) as hp:
                    for half in range(2):
                        n = hp * 2 + half
                        cols = slice(half * WC // 2, (half + 1) * WC // 2)
                        pool.wait_ge(m["w_in"], n * 16 + 16)
                        pool.tensor_tensor(wst[:], wst[:], bcast(wsc[:, 0:1], P, WC // 2), ALU.mult).then_inc(m["w_sc"], 1)
                        pool.wait_ge(m["w_sc"], n + 3)
                        pool.tensor_tensor(w[:, 0, ds(hp, 1), cols], wst[:].unsqueeze(1),
                                           bcast(wsc[:, 1:2].unsqueeze(1), P, 1, WC // 2), ALU.mult).then_inc(m["w_hi"], 1)
                        pool.wait_ge(m["w_hi"], n + 1)
                        pool.tensor_tensor(w[:, 1, ds(hp, 1), cols], wst[:].unsqueeze(1), w[:, 0, ds(hp, 1), cols],
                                           ALU.subtract).then_inc(m["w_ready"], 1)

            @block.tensor
            def _(pe):
                def wcol(part, hp, col, n):
                    a = w[:, part, ds(hp, 1), col:col + n]
                    return a.rearrange("p o c -> p (o c)")

                def chunk(ci, n, b, hp, par):
                    first = ci < 4 and isinstance(n, int)
                    if ci < 4:
                        kind, c = ci // 2, ci % 2
                        if ci == 0:
                            pe.wait_ge(m["w_ready"], hp * 2 + 2)
                        if not first or ci >= 2:
                            if ci < 2:
                                pe.wait_ge(m["v_r"], n * 2 + ci - 1)
                            else:
                                pe.wait_ge(m["sg64"], n * 4 + ci - 1)
                        for kc in range(KC):
                            last = three(pe, pj[c][:],
                                         lambda i: wcol(i, hp, (QC, KC0)[kind] + kc * 2 * DH + c * DH, DH),
                                         lambda j: xt[:, j, kc, ds(b * S, S)], kc == 0, kc == KC - 1)
                        last.then_inc(m["pj_full"], 1)
                    elif ci == 4:
                        pe.wait_ge(m["sglo"], n * 4 + 4)
                        for part in range(2):
                            for c in range(2):
                                for t in range(TPB):
                                    q = (c * TPB + t) * P
                                    pe.transpose(tr16[part][:, q:q + P],
                                                 sg[:, par, part, c, t, 2:4, :].rearrange("p a s -> p (a s)"), ident[:])
                                    last = pe.transpose(tr16[part][0:SEG, q:q + P],
                                                        sg[:, par, part, c, t, 0, :], ident[:])
                            last.then_inc(m["skr_full"], 1)
                    elif ci == 5:
                        for half in range(2):
                            pe.wait_ge(m["sg64"], n * 4 + 3 + half)
                            for t in range(2):
                                for kc in range(KC):
                                    tile = half * 2 + t
                                    last = three(pe, pj[half][:, t * D:(t + 1) * D],
                                                 lambda i: xt[:, i, kc, ds(b * S + tile * P, P)],
                                                 lambda j: wcol(j, hp, VC + kc * 2 * DH, 2 * DH),
                                                 t == 0 and kc == 0, t == 1 and kc == KC - 1)
                            last.then_inc(m["pj_full"], 1)
                    elif ci == 6:
                        pe.wait_ge(m["lo_r"], n * 4 + 4)
                        pe.wait_ge(m["skrhi"], n + 1)
                        for c in range(2):
                            for t in range(TPB):
                                for odd in range(2):
                                    rows = slice(odd * SEG, odd * SEG + SEG)
                                    s0 = (2 * t + odd) * SEG
                                    col = (c * TPB + t) * SEG
                                    last = three(pe, tr[0][rows, col:col + SEG],
                                                 lambda i: qs[:, i, c, s0:s0 + SEG],
                                                 lambda j: ks[:, j, c, s0:s0 + SEG],
                                                 c == 0 and t == 0, c == 1 and t == TPB - 1)
                        last.then_inc(m["s_full"], 1)
                    else:
                        for part, (ready, free) in enumerate((("phi", "sm_r"), ("plo", "skrlo"))):
                            pe.wait_ge(m[ready], n + 1)
                            pe.wait_ge(m[free], n + 1)
                            pe.transpose(tr16[part][:, 0:P], ps[:, part, 0:2, :].rearrange("p a s -> p (a s)"), ident[:])
                            for ct in range(1, 2 * TPB):
                                last = pe.transpose(tr16[part][0:SEG, ct * P:(ct + 1) * P], ps[:, part, ct, :], ident[:])
                            last.then_inc(m["pt_full"], 1)

                def retrieve(j, g, hp, par):
                    t, odd = j // 2, j % 2
                    if j == 0:
                        pe.wait_ge(m["sglo"], g * 4 + 4)
                        pe.matmul(mem[:].rearrange("p c e -> p (c e)"), ones[:], zi[:].rearrange("p c e -> p (c e)"),
                                  start=True, stop=False, skip_group_check=True)
                    else:
                        pe.wait_ge(m["mlo"], g * 7 + j)
                    src = ms0[:] if j == 0 else ms[:, j % 2]
                    for c in range(2):
                        last = three(pe, num[:, c, 0:DH + 1],
                                     lambda i: sg[:, par, i, c, t, 2 * odd:2 * odd + 2, :].rearrange("p a s -> p (a s)"),
                                     lambda i: src[:, i, c, 0:DH + 1], c == 0, c == 1)
                    last.then_inc(m["num_full"], 1)

                def update(j, g, hp, par):
                    if j == NSEG - 1:
                        return
                    t, odd = j // 2, j % 2
                    if j == 0:
                        pe.wait_ge(m["skrlo"], g + 1)
                    pe.wait_ge(m["dlo"], g * 7 + j + 1)
                    for c in range(2):
                        last = three(pe, mem[:, c, 0:DH + 1], lambda i: skr[:, par, i, c, t, :],
                                     lambda i: dd[:, odd, i, c, 0:DH + 1])
                    last.then_inc(m["mem_full"], 1)

                def tail(g, hp, par):
                    pe.wait_ge(m["pthi"], g * 2 + 4)
                    pe.wait_ge(m["ptlo"], g * 2 + 4)
                    pe.wait_ge(m["vlo"], g + 1)
                    for half in range(2):
                        for t in range(2):
                            for c in range(2):
                                last = three(pe, tr[half][:, (t * 2 + c) * DH:(t * 2 + c + 1) * DH],
                                             lambda i: ptb[:, par, i, c, half * 2 + t, :],
                                             lambda i: vs[:, par, i, half * 2 + t, c * DH:(c + 1) * DH],
                                             t == 0 and c == 0, t == 1 and c == 1)
                        last.then_inc(m["dot_full"], 1)
                    for part, ready in enumerate(("ahi", "alo")):
                        pe.wait_ge(m[ready], g + 1)
                        for c in range(2):
                            for t in range(TPB):
                                q = (c * TPB + t) * P
                                last = pe.transpose(tr16[part][:, q:q + P], ats[:, part, t, c * DH:(c + 1) * DH], ident[:])
                        last.then_inc(m["att_full"], 1)

                def end(gi, b, k):
                    pe.wait_ge(m["w_ready"], PAIRS * 2)
                    pe.wait_ge(m["atthi"], gi * 2 + 2)
                    pe.wait_ge(m["attlo"], gi * 2 + 2)
                    for r in range(ROWS16):
                        last = three(pe, yp[:, 0, :], lambda i: att[:, i, r, :],
                                     lambda j: w[:, j, r // 2, OC + (r % 2) * D:OC + (r % 2 + 1) * D],
                                     r == 0, r == ROWS16 - 1)
                    last.then_inc(m["y_full"], 1)

                pe.wait_ge(m["init"], 11)
                pairs(pe, chunk, retrieve, update, tail, end)

            @block.scalar
            def _(act):
                act.wait_ge(m["const_in"], 32)
                act.activation(beta[:], beta[:], ACT.Sigmoid).then_inc(m["beta_r"], 1)
                act.preload_act_table(ACT.Exp)

                def chunk(ci, n, b, hp, par):
                    if ci < 4:
                        kind, c = ci // 2, ci % 2
                        dst = (qs, ks)[kind]
                        act.wait_ge(m["pj_full"], n * 6 + ci + 1)
                        act.activation(dst[:, 0, c, :], pj[c][:], ACT.Copy, scale=1 / WSCALE).then_inc(m["hi_r"], 1)
                        act.activation(ee[:, c, :], pj[c][:], ACT.Exp, scale=1 / WSCALE).then_inc(m["ex_r"], 1)
                        act.wait_ge(m["sg64"], n * 4 + ci + 1)
                        to = (queries, keys)[kind](par, 0, c)
                        act.activation(to, ee[:, c, :].rearrange("p (t o s) -> p t o s", t=TPB, o=2), ACT.Copy,
                                       scale=1 / WSCALE).then_inc(m["sghi"], 1)
                    elif ci == 4:
                        act.wait_ge(m["skr_full"], n * 2 + 1)
                        act.activation(skr[:, par, 0].rearrange("p c t d -> p (c t d)"), tr16[0], ACT.Copy).then_inc(m["skrhi"], 1)
                    elif ci == 5:
                        for half in range(2):
                            act.wait_ge(m["pj_full"], n * 6 + 5 + half)
                            act.activation(v32[:, par, half * 2:half * 2 + 2, :].rearrange("p t d -> p (t d)"),
                                           pj[half][:], ACT.Copy, scale=1 / WSCALE).then_inc(m["v_r"], 1)
                        act.wait_ge(m["vb_r"], n + 1)
                        act.activation(vs[:, par, 0], vb[:], ACT.Copy).then_inc(m["vhi"], 1)
                    elif ci == 6:
                        act.wait_ge(m["sd_r"], n + 1)
                        act.activation(ex[:], sm[:], ACT.Exp, scale=float(DH) ** -0.5).then_inc(m["pex_r"], 1)
                        act.wait_ge(m["pn_r"], n + 1)
                        act.activation(ps[:, 0], sm[:], ACT.Copy).then_inc(m["phi"], 1)
                    else:
                        act.wait_ge(m["pt_full"], n * 2 + 1)
                        for odd in range(2):
                            kr, qr = HALF[odd]
                            act.activation(ptb[kr, par, 0, :, :, qr],
                                           probs_t(0, odd),
                                           ACT.Copy).then_inc(m["pthi"], 1)

                def retrieve(j, g, hp, par):
                    if j == NSEG - 1:
                        return
                    kr = HALF[j % 2][0]
                    act.wait_ge(m["d_r"], g * 7 + j + 1)
                    act.activation(dd[kr, j % 2, 0, :, 0:DH], d32[kr], ACT.Copy).then_inc(m["dhi"], 1)

                def update(j, g, hp, par):
                    if j == NSEG - 1:
                        return
                    act.wait_ge(m["mem_full"], g * 7 + j + 1)
                    act.activation(ms[:, (j + 1) % 2, 0, :, 0:DH + 1], mem[:, :, 0:DH + 1],
                                   ACT.Copy).then_inc(m["mhi"], 1)

                def tail(g, hp, par):
                    act.wait_ge(m["at_r"], g * 2 + 2)
                    act.activation(ats[:, 0], at[:], ACT.Copy).then_inc(m["ahi"], 1)
                    act.wait_ge(m["att_full"], g * 2 + 1)
                    for c in range(2):
                        ins = act.activation(att_in(0, par, c), att_from(0, c), ACT.Copy)
                    ins.then_inc(m["atthi"], 1)

                def end(gi, b, k):
                    act.wait_ge(m["y_full"], gi + 1)
                    act.wait_ge(m["yst_free"], gi + 1)
                    act.activation(yst[:], yp[:, 0, :], ACT.Copy, scale=1 / WSCALE).then_inc(m["y_out"], 1)

                pairs(act, chunk, retrieve, update, tail, end)

            @block.vector
            def _(v):
                v.memset(ptb[:], 0.0).then_inc(m["init"], 1)
                v.memset(dd[:], 0.0).then_inc(m["init"], 1)
                v.memset(ms0[:], 0.0).then_inc(m["init"], 1)
                v.memset(zi[:], 0.0).then_inc(m["init"], 1)
                v.memset(ones[:], 1.0).then_inc(m["init"], 1)
                v.wait_ge(m["init"], 5)
                v.memset(dd[0:SEG, 0, 0, :, DH:DH + 1], 1.0).then_inc(m["init"], 1)
                v.memset(dd[SEG:P, 1, 0, :, DH:DH + 1], 1.0).then_inc(m["init"], 1)
                v.memset(ms0[:, 0, :, DH:DH + 1], 1.0 / DH).then_inc(m["init"], 1)
                v.memset(zi[0:1, :, DH:DH + 1], 1.0 / DH).then_inc(m["init"], 1)
                v.wait_ge(m["const_in"], 32)
                v.wait_ge(m["beta_r"], 1)
                v.memset(rd[:], 0.0).then_inc(m["init"], 1)
                v.memset(red[:], 0.0).then_inc(m["init"], 1)
                v.wait_ge(m["init"], 11)

                def chunk(ci, n, b, hp, par):
                    if ci < 4:
                        kind, c = ci // 2, ci % 2
                        dst = (qs, ks)[kind]
                        i = n * 4 + ci + 1
                        v.wait_ge(m["ex_r"], i)
                        v.tensor_scalar(ee[:, c, :], ee[:, c, :], 1.0, WSCALE, ALU.min, ALU.mult).then_inc(m["e1_r"], 1)
                        v.scalar_tensor_tensor(dst[:, 1, c, :], pj[c][:], 1 / WSCALE, dst[:, 0, c, :],
                                               ALU.mult, ALU.subtract).then_inc(m["lo_r"], 1)
                        v.wait_ge(m["e1_r"], i)
                        v.scalar_tensor_tensor(ee[:, c, :], pj[c][:], 0.0, ee[:, c, :], ALU.max,
                                               ALU.add).then_inc(m["sg64"], 1)
                        v.wait_ge(m["sghi"], i)
                        to = (queries, keys)[kind]
                        for t in range(TPB):
                            e = ee[:, c, t * P:(t + 1) * P].rearrange("p (o s) -> p o s", o=2)
                            ins = v.scalar_tensor_tensor(to(par, 1, c)[:, t], e, 1 / WSCALE, to(par, 0, c)[:, t],
                                                         ALU.mult, ALU.subtract)
                        ins.then_inc(m["sglo"], 1)
                    elif ci == 4:
                        v.wait_ge(m["skr_full"], n * 2 + 2)
                        v.tensor_copy(skr[:, par, 1].rearrange("p c t d -> p (c t d)"), tr16[1]).then_inc(m["skrlo"], 1)
                        v.tensor_scalar(omb[:], beta[:, ds(hp * 2 * DH, 2 * DH)], -1.0, 1.0, ALU.mult,
                                        ALU.add).then_inc(m["omb_r"], 1)
                    elif ci == 5:
                        v.wait_ge(m["omb_r"], n + 1)
                        v.wait_ge(m["v_r"], n * 2 + 2)
                        v.tensor_tensor(vb[:], v32[:, par], bcast(omb[:].unsqueeze(1), P, TPB, 2 * DH),
                                        ALU.mult).then_inc(m["vb_r"], 1)
                        v.wait_ge(m["vhi"], n + 1)
                        v.tensor_tensor(vs[:, par, 1], vb[:], vs[:, par, 0], ALU.subtract).then_inc(m["vlo"], 1)
                    elif ci == 6:
                        v.wait_ge(m["s_full"], n + 1)
                        v.tensor_tensor(sm[:], tr[0][:].rearrange("p (x s) -> p x s", s=SEG),
                                        bcast(mask[:].unsqueeze(1), P, 2 * TPB, SEG), ALU.add).then_inc(m["sm_r"], 1)
                        v.wait_ge(m["sm_r"], n + 1)
                        v.tensor_reduce(red[:], sm[:], AX.X, ALU.max).then_inc(m["mx_r"], 1)
                        v.wait_ge(m["mx_r"], n + 1)
                        v.tensor_tensor(sm[:], sm[:], bcast(red[:].unsqueeze(2), P, 2 * TPB, SEG),
                                        ALU.subtract).then_inc(m["sd_r"], 1)
                        v.wait_ge(m["pex_r"], n + 1)
                        v.tensor_reduce(red[:], ex[:], AX.X, ALU.add).then_inc(m["sum_r"], 1)
                        v.wait_ge(m["sum_r"], n + 1)
                        v.reciprocal(red[:], red[:]).then_inc(m["ri_r"], 1)
                        v.wait_ge(m["ri_r"], n + 1)
                        v.tensor_tensor(sm[:], ex[:], bcast(red[:].unsqueeze(2), P, 2 * TPB, SEG),
                                        ALU.mult).then_inc(m["pn_r"], 1)
                        v.wait_ge(m["phi"], n + 1)
                        v.tensor_tensor(ps[:, 1], sm[:], ps[:, 0], ALU.subtract).then_inc(m["plo"], 1)
                    else:
                        v.wait_ge(m["pt_full"], n * 2 + 2)
                        for odd in range(2):
                            kr, qr = HALF[odd]
                            v.tensor_copy(ptb[kr, par, 1, :, :, qr],
                                          probs_t(1, odd)).then_inc(m["ptlo"], 1)

                def retrieve(j, g, hp, par):
                    t, odd = j // 2, j % 2
                    kr, qr = HALF[odd]
                    v.wait_ge(m["num_full"], g * 8 + j + 1)
                    v.reciprocal(rd[:], num[:, :, DH]).then_inc(m["rd_r"], 1)
                    v.wait_ge(m["rd_r"], g * 8 + j + 1)
                    if j < NSEG - 1:
                        for c in range(2):
                            ins = v.scalar_tensor_tensor(d32[kr, c, :], num[kr, c, 0:DH], rd[kr, c:c + 1],
                                                         v32[kr, par, t, c * DH:(c + 1) * DH], ALU.mult,
                                                         ALU.subtract, reverse1=True)
                        ins.then_inc(m["d_r"], 1)
                    for c in range(2):
                        ins = v.scalar_tensor_tensor(at[qr, t, c * DH:(c + 1) * DH], num[qr, c, 0:DH], rd[qr, c:c + 1],
                                                     beta[qr, ds(hp * 2 * DH + c * DH, DH)], ALU.mult, ALU.mult)
                    ins.then_inc(m["a_r"], 1)
                    if j < NSEG - 1:
                        v.wait_ge(m["dhi"], g * 7 + j + 1)
                        v.tensor_tensor(dd[kr, odd, 1, :, 0:DH], d32[kr], dd[kr, odd, 0, :, 0:DH],
                                        ALU.subtract).then_inc(m["dlo"], 1)

                def update(j, g, hp, par):
                    if j == NSEG - 1:
                        return
                    i = g * 7 + j + 1
                    v.wait_ge(m["mhi"], i)
                    v.tensor_tensor(ms[:, (j + 1) % 2, 1, :, 0:DH + 1], mem[:, :, 0:DH + 1],
                                    ms[:, (j + 1) % 2, 0, :, 0:DH + 1], ALU.subtract).then_inc(m["mlo"], 1)

                def tail(g, hp, par):
                    v.wait_ge(m["a_r"], g * 8 + 8)
                    for half in range(2):
                        v.wait_ge(m["dot_full"], g * 2 + half + 1)
                        a = at[:, half * 2:half * 2 + 2, :].rearrange("p t d -> p (t d)")
                        v.tensor_tensor(a, a, tr[half][:], ALU.add).then_inc(m["at_r"], 1)
                    v.wait_ge(m["ahi"], g + 1)
                    v.tensor_tensor(ats[:, 1], at[:], ats[:, 0], ALU.subtract).then_inc(m["alo"], 1)
                    v.wait_ge(m["att_full"], g * 2 + 2)
                    for c in range(2):
                        ins = v.tensor_copy(att_in(1, par, c), att_from(1, c))
                    ins.then_inc(m["attlo"], 1)

                def end(gi, b, k):
                    pass

                pairs(v, chunk, retrieve, update, tail, end)


def attn1_phase(nc, w_dram, tabs, xt, y, ident):
    NG, HG = 4, 4
    HD = H1 * DH1
    with ExitStack() as ctx:
        ph = Phase(nc, ctx, "a1")
        w32 = ph.sb("w32", [P, KC, 4 * D])
        w = ph.sb("w", [P, 2, KC, 4 * D], F16)
        cos = ph.sb("cos", [P, TPB, DH1])
        sin = ph.sb("sin", [P, TPB, DH1])
        qdec = ph.sb("qdec", [P, H1])
        kdec = ph.sb("kdec", [P, H1])
        rc = ph.sb("rc", [P, NG])
        kvmask = ph.sb("kvmask", [P, HG * DH1])
        dmask = ph.sb("dmask", [P, HG, NG * P])
        rms_w = ph.sb("rms_w", [P, D])
        ra = ph.sb("ra", [P, 2 * H1, DH1])
        rb = ph.sb("rb", [P, 2 * H1, DH1])
        qks = ph.sb("qks", [P, 2 * H1, 2, DH1], F16)
        kx = ph.sb("kx", [P, H1, 2, DH1], F16)
        kd32 = ph.sb("kd32", [P, H1, DH1])
        kd = ph.sb("kd", [P, 2, 2, H1, 2, DH1], F16)
        vs = ph.sb("vs", [P, 2, 2, D], F16)
        qkt = ph.sb("qkt", [P, 2, 2, NG, P], F16)
        kxt = ph.sb("kxt", [P, 2, NG, P], F16)
        sd = ph.sb("sd", [P, HG, NG * P])
        sds = ph.sb("sds", [P, 2, HG, NG * P], F16)
        kv = ph.sb("kv", [P, NG, HG * DH1])
        kvu = ph.sb("kvu", [P, NG, HG * DH1])
        kvs = ph.sb("kvs", [P, 2, 2, NG, HG * DH1], F16)
        at = ph.sb("at", [P, HD])
        sq = ph.sb("sq", [P, HD])
        ss = ph.sb("ss", [P, 1])
        std = ph.sb("std", [P, 1])
        rstd = ph.sb("rstd", [P, 1])
        ats = ph.sb("ats", [P, 2, HD], F16)
        att = ph.sb("att", [P, 2, KC, P], F16)
        qkp = ph.ps("qkp", [P, 2 * D])
        vyp = ph.ps("vyp", [P, 2 * D])
        tqk = ph.ps("tqk", [P, 2, NG, P], F16)
        tx = ph.ps("tx", [P, 2, NG, P], F16)
        sp_ = [ph.ps(f"sc{i}", [P, NG * P]) for i in range(HG)]
        op, upd = sp_[0], sp_[1]

        names = ("in_ w_hi w_lo init qk_full v_full a_rot a_rb r_ready qkhi qklo kxr kd_ready kdhi kdlo vhi vlo"
                 " t_full tx_full qkt_r kxt_r sc_full sd_r sdhi sdlo out_full upd_full sc_free kvu_r kv_r"
                 " kvhi kvlo kv_reset ra_r at_r ss_r ms_r std_r rstd_r an_r anhi anlo att_full atthi attlo"
                 " y_full y_out dvo").split()
        m = {n: ph.sem(n) for n in names}

        def three(pe, out, wa, xa, start, stop):
            for n, (i, j) in enumerate(((0, 0), (0, 1), (1, 0))):
                last = pe.matmul(out, wa(i), xa(j), start=start and n == 0, stop=stop and n == 2,
                                 skip_group_check=True)
            return last

        def tiles(eng, stage_a, stage_b, reset=None):
            stage_a(0, 0, 0, 0)
            with eng.Fori(0, B) as b:
                if reset is not None:
                    reset(b)
                with eng.Fori(0, TPB // 2) as k:
                    for par in range(2):
                        t = b * TPB + k * 2 + par
                        n = t + 1
                        stage_b(b, t, par, lambda: stage_a(n, n % TILES, n % TPB, 1 - par))

        with nc.Block() as block:
            @block.sync
            def _(sp):
                sp.dma_start(w32[:], w_dram).then_inc(m["in_"], 16)
                for n, dst in (("cos", cos), ("sin", sin), ("qdec", qdec), ("kdec", kdec), ("rc", rc),
                               ("kvmask", kvmask), ("dmask", dmask)):
                    sp.dma_start(dst[:], tabs[n]).then_inc(m["in_"], 16)
                sp.dma_start(rms_w[:], tabs["rms_w"].to_broadcast([P, D])).then_inc(m["in_"], 16)
            n_in = 16 * 9

            @block.tensor
            def _(pe):
                def stage_a1(n, tile):
                    for kc in range(KC):
                        last = three(pe, qkp[:], lambda i: xt[:, i, kc, ds(tile * P, P)],
                                     lambda j: w[:, j, kc, 0:2 * D], kc == 0, kc == KC - 1)
                    last.then_inc(m["qk_full"], 1)
                    for kc in range(KC):
                        last = three(pe, vyp[:, 0:D], lambda i: xt[:, i, kc, ds(tile * P, P)],
                                     lambda j: w[:, j, kc, 2 * D:3 * D], kc == 0, kc == KC - 1)
                    last.then_inc(m["v_full"], 1)

                def stage_a2(n):
                    pe.wait_ge(m["qkhi"], n + 1)
                    pe.wait_ge(m["qklo"], n + 1)
                    flat = qks[:].rearrange("p h s d -> p (h s d)")
                    for c in range(2 * NG):
                        last = pe.transpose(tqk[:, c // NG, c % NG, :], flat[:, c * P:(c + 1) * P], ident[:])
                    last.then_inc(m["t_full"], 1)
                    pe.wait_ge(m["kxr"], n * 2 + 2)
                    flat = kx[:].rearrange("p h s d -> p (h s d)")
                    for c in range(NG):
                        last = pe.transpose(tx[:, 0, c, :], flat[:, c * P:(c + 1) * P], ident[:])
                    last.then_inc(m["tx_full"], 1)

                def a(n, tile, pos, par):
                    stage_a1(n, tile)
                    stage_a2(n)

                def b(batch, t, par, nxt):
                    n = t + 1
                    pe.wait_ge(m["ra_r"], t * 3 + 3)
                    pe.wait_ge(m["vlo"], n)
                    pe.wait_ge(m["y_out"], n)
                    stage_a1(n, n % TILES)
                    pe.wait_ge(m["qkt_r"], n)
                    pe.wait_ge(m["kxt_r"], n)
                    for g in range(NG):
                        for i in range(HG):
                            rows = slice(32 * i, 32 * i + 32)
                            pe.matmul(sp_[i][:, g * P:(g + 1) * P], qkt[rows, par, 1, g, :],
                                      qkt[rows, par, 0, g, :], start=g == 0, stop=False,
                                      skip_group_check=True)
                            last = pe.matmul(sp_[i][:, g * P:(g + 1) * P], kxt[rows, par, g, :],
                                             qkt[rows, par, 0, g, :], start=False, stop=g == NG - 1,
                                             skip_group_check=True)
                            if g == NG - 1:
                                last.then_inc(m["sc_full"], 1)
                    stage_a2(n)
                    pe.wait_ge(m["kdhi"], n)
                    pe.wait_ge(m["kdlo"], n)
                    pe.wait_ge(m["sd_r"], t * HG + 2)
                    for g in range(NG):
                        last = three(pe, upd[:, g * HG * DH1:(g + 1) * HG * DH1],
                                     lambda i: kd[:, par, i, g * HG:(g + 1) * HG].rearrange(
                                         "p h s d -> p (h s d)"),
                                     lambda j: vs[:, par, j, g * HG * DH1:(g + 1) * HG * DH1],
                                     g == 0, g == NG - 1)
                    last.then_inc(m["upd_full"], 1)
                    pe.wait_ge(m["kvlo"], n + batch)
                    for g in range(NG):
                        for j in range(2):
                            pe.matmul(op[:, HD + g * 64:HD + (g + 1) * 64], qkt[:, par, 0, g, :],
                                      kvs[:, par, j, g, :], start=g == 0 and j == 0, stop=False,
                                      skip_group_check=True)
                    for i in range(HG):
                        pe.wait_ge(m["sdhi"], t * HG + i + 1)
                        pe.wait_ge(m["sdlo"], t * HG + i + 1)
                        for g in range(NG):
                            h = HG * g + i
                            last = three(pe, op[:, h * DH1:(h + 1) * DH1],
                                         lambda j: sds[:, j, i, g * P:(g + 1) * P],
                                         lambda j: vs[:, par, j, h * DH1:(h + 1) * DH1], False, i == HG - 1)
                    last.then_inc(m["out_full"], 1)
                    pe.wait_ge(m["anhi"], n)
                    pe.wait_ge(m["anlo"], n)
                    pe.wait_ge(m["kxt_r"], n + 1)
                    for j in range(2):
                        for kc in range(KC):
                            last = pe.transpose(tx[:, 1, j * KC + kc, :], ats[:, j, kc * P:(kc + 1) * P], ident[:])
                    last.then_inc(m["att_full"], 1)
                    pe.wait_ge(m["atthi"], n)
                    pe.wait_ge(m["vlo"], n + 1)
                    for kc in range(KC):
                        last = three(pe, vyp[:, D:2 * D], lambda i: att[:, i, kc, :],
                                     lambda j: w[:, j, kc, 3 * D:4 * D], kc == 0, kc == KC - 1)
                    last.then_inc(m["y_full"], 1)

                pe.wait_ge(m["w_lo"], 1)
                tiles(pe, a, b)

            @block.scalar
            def _(act):
                act.preload_act_table(ACT.Sqrt)
                act.wait_ge(m["in_"], n_in)
                act.activation(w[:, 0], w32[:], ACT.Copy, scale=WSCALE).then_inc(m["w_hi"], 1)

                def a1(n, par):
                    act.wait_ge(m["v_full"], n + 1)
                    act.activation(vs[:, par, 0, :], vyp[:, 0:D], ACT.Copy, scale=1 / WSCALE).then_inc(m["vhi"], 1)
                    act.wait_ge(m["r_ready"], n + 1)
                    act.activation(qks[:, :, 0, :], ra[:], ACT.Copy).then_inc(m["qkhi"], 1)

                def a2(n, par):
                    act.wait_ge(m["kd_ready"], n + 1)
                    act.activation(kd[:, par, 0], bcast(kd32[:].unsqueeze(2), P, H1, 2, DH1),
                                   ACT.Copy).then_inc(m["kdhi"], 1)
                    act.wait_ge(m["t_full"], n + 1)
                    act.activation(qkt[:, par], tqk[:], ACT.Copy).then_inc(m["qkt_r"], 1)

                def a(n, tile, pos, par):
                    a1(n, par)
                    a2(n, par)

                def b(batch, t, par, nxt):
                    n = t + 1
                    a1(n, 1 - par)
                    for i in range(HG):
                        act.wait_ge(m["sd_r"], t * HG + i + 1)
                        act.activation(sds[:, 0, i, :], sd[:, i, :], ACT.Copy).then_inc(m["sdhi"], 1)
                    a2(n, 1 - par)
                    act.wait_ge(m["kv_r"], n)
                    act.activation(kvs[:, 1 - par, 0], kv[:], ACT.Copy).then_inc(m["kvhi"], 1)
                    act.wait_ge(m["at_r"], n)
                    act.activation(sq[:], at[:], ACT.Square, accum_out=ss[:]).then_inc(m["ss_r"], 1)
                    act.wait_ge(m["ms_r"], n)
                    act.activation(std[:], ss[:], ACT.Sqrt).then_inc(m["std_r"], 1)
                    act.wait_ge(m["an_r"], n)
                    act.activation(ats[:, 0, :], at[:], ACT.Copy).then_inc(m["anhi"], 1)
                    act.wait_ge(m["att_full"], n)
                    act.activation(att[:].rearrange("p a k c -> p (a k) c"), tx[:, 1], ACT.Copy).then_inc(m["atthi"], 1)
                    act.wait_ge(m["y_full"], n)
                    act.activation(y[:, ds(t, 1), :], vyp[:, D:2 * D], ACT.Copy,
                                   scale=1 / WSCALE).then_inc(m["y_out"], 1)

                tiles(act, a, b)

            @block.gpsimd
            def _(pool):
                def a(n, tile, pos, par):
                    pool.wait_ge(m["ra_r"], n * 3 + 3)
                    pool.tensor_tensor(ra[:], ra[:], rb[:], ALU.add).then_inc(m["r_ready"], 1)
                    pool.wait_ge(m["r_ready"], n + 1)
                    pool.tensor_tensor(kd32[:], ra[:, H1:2 * H1, :], bcast(kdec[:].unsqueeze(2), P, H1, DH1),
                                       ALU.mult).then_inc(m["kd_ready"], 1)
                    pool.wait_ge(m["qklo"], n + 1)
                    pool.tensor_tensor(kx[:, :, 0, :], ra[:, H1:2 * H1, :], qks[:, H1:2 * H1, 0, :],
                                       ALU.subtract).then_inc(m["kxr"], 1)
                    pool.tensor_copy(kx[:, :, 1, :], qks[:, H1:2 * H1, 0, :]).then_inc(m["kxr"], 1)

                def b(batch, t, par, nxt):
                    nxt()
                    for i in range(HG):
                        pool.wait_ge(m["sdhi"], t * HG + i + 1)
                        pool.tensor_tensor(sds[:, 1, i, :], sd[:, i, :], sds[:, 0, i, :],
                                           ALU.subtract).then_inc(m["sdlo"], 1)

                pool.wait_ge(m["in_"], n_in)
                tiles(pool, a, b)

            @block.vector
            def _(v):
                done = [0]
                v.wait_ge(m["w_hi"], 1)
                v.scalar_tensor_tensor(w[:, 1].rearrange("p k c -> p (k c)"),
                                       w32[:].rearrange("p k c -> p (k c)"), WSCALE,
                                       w[:, 0].rearrange("p k c -> p (k c)"),
                                       ALU.mult, ALU.subtract).then_inc(m["w_lo"], 1)
                v.sem_inc(m["y_out"], 1)

                def a1(n, pos):
                    v.wait_ge(m["qk_full"], n + 1)
                    q = qkp[:].rearrange("p (h d) -> p h d", d=DH1)
                    half = DH1 // 2

                    def tab(tb, lo, hi):
                        return tb[:, ds(pos, 1), lo:hi].to_broadcast([P, 2 * H1, hi - lo])
                    v.tensor_tensor(ra[:], q, tab(cos, 0, DH1), ALU.mult).then_inc(m["ra_r"], 1)
                    v.tensor_tensor(rb[:, :, 0:half], q[:, :, half:], tab(sin, 0, half),
                                    ALU.mult).then_inc(m["ra_r"], 1)
                    v.tensor_tensor(rb[:, :, half:], q[:, :, 0:half], tab(sin, half, DH1),
                                    ALU.mult).then_inc(m["ra_r"], 1)

                def a2(n, par):
                    v.wait_ge(m["vhi"], n + 1)
                    v.scalar_tensor_tensor(vs[:, par, 1, :], vyp[:, 0:D], 1 / WSCALE, vs[:, par, 0, :],
                                           ALU.mult, ALU.subtract).then_inc(m["vlo"], 1)
                    v.wait_ge(m["qkhi"], n + 1)
                    v.tensor_tensor(qks[:, :, 1, :], ra[:], qks[:, :, 0, :], ALU.subtract).then_inc(m["qklo"], 1)
                    v.wait_ge(m["kdhi"], n + 1)
                    for rep in range(2):
                        ins = v.tensor_tensor(kd[:, par, 1, :, rep], kd32[:], kd[:, par, 0, :, rep], ALU.subtract)
                    ins.then_inc(m["kdlo"], 1)

                def a3(n, par):
                    v.wait_ge(m["tx_full"], n + 1)
                    v.tensor_copy(kxt[:, par], tx[:, 0]).then_inc(m["kxt_r"], 1)

                def a(n, tile, pos, par):
                    a1(n, pos)
                    a2(n, par)
                    a3(n, par)

                def reset(b):
                    v.memset(kv[:], 0.0).then_inc(m["kv_reset"], 1)
                    v.memset(kvs[:, 0, 0], 0.0).then_inc(m["kv_reset"], 1)
                    v.wait_ge(m["kv_reset"], b * 2 + 2)
                    v.memset(kvs[:, 0, 1], 0.0).then_inc(m["kvlo"], 1)

                def b(batch, t, par, nxt):
                    n = t + 1
                    a1(n, n % TPB)
                    for i in range(HG):
                        v.wait_ge(m["sc_full"], t * HG + i + 1)
                        v.tensor_tensor(sd[:, i, :], sp_[i][:], dmask[:, i, :], ALU.mult).then_inc(m["sd_r"], 1)
                    a2(n, 1 - par)
                    a3(n, 1 - par)
                    v.wait_ge(m["upd_full"], n)
                    v.tensor_tensor(kvu[:], upd[:, 0:HD].rearrange("p (g e) -> p g e", g=NG),
                                    bcast(kvmask[:].unsqueeze(1), P, NG, HG * DH1), ALU.mult).then_inc(m["dvo"], 1)
                    v.tensor_tensor(kv[:], kv[:], bcast(rc[:].unsqueeze(2), P, NG, HG * DH1),
                                    ALU.mult).then_inc(m["dvo"], 1)
                    v.wait_ge(m["dvo"], t * 4 + 2)
                    v.tensor_tensor(kv[:], kv[:], kvu[:], ALU.add).then_inc(m["kv_r"], 1)
                    v.wait_ge(m["out_full"], n)
                    v.tensor_tensor(at[:].rearrange("p (h e) -> p h e", h=H1),
                                    op[:, HD:].rearrange("p (h e) -> p h e", h=H1),
                                    bcast(qdec[:].unsqueeze(2), P, H1, DH1), ALU.mult).then_inc(m["dvo"], 1)
                    v.wait_ge(m["dvo"], t * 4 + 3)
                    v.tensor_tensor(at[:], at[:], op[:, 0:HD], ALU.add).then_inc(m["at_r"], 1)
                    v.wait_ge(m["kvhi"], n)
                    v.tensor_tensor(kvs[:, 1 - par, 1], kv[:], kvs[:, 1 - par, 0],
                                    ALU.subtract).then_inc(m["kvlo"], 1)
                    v.wait_ge(m["ss_r"], n)
                    v.tensor_scalar(ss[:], ss[:], 1.0 / HD, LN_EPS, ALU.mult, ALU.add).then_inc(m["ms_r"], 1)
                    v.wait_ge(m["std_r"], n)
                    v.reciprocal(rstd[:], std[:]).then_inc(m["dvo"], 1)
                    v.wait_ge(m["dvo"], t * 4 + 4)
                    v.scalar_tensor_tensor(at[:], at[:], rstd[:], rms_w[:], ALU.mult,
                                           ALU.mult).then_inc(m["an_r"], 1)
                    v.wait_ge(m["anhi"], n)
                    v.tensor_tensor(ats[:, 1, :], at[:], ats[:, 0, :], ALU.subtract).then_inc(m["anlo"], 1)

                tiles(v, a, b, reset)


def _pack_ffn(w1, w3, w2, ht_n):
    import numpy as np
    rows = ht_n * P
    out = np.zeros((ht_n, P, 2 * KC * P + D), np.float32)
    for n, w in enumerate((w1, w3)):
        full = np.zeros((rows, D), np.float32)
        full[:w.shape[0]] = w
        out[:, :, n * D:(n + 1) * D] = full.reshape(ht_n, P, KC, P).transpose(0, 3, 2, 1).reshape(ht_n, P, D)
    full = np.zeros((rows, D), np.float32)
    full[:w2.shape[0]] = w2
    out[:, :, 2 * D:] = full.reshape(ht_n, P, D)
    return out


def _by_kc(w):
    return w.reshape(KC, P, -1).transpose(1, 0, 2)


def _pack_attn0(wq, wk, wv, wo):
    import numpy as np
    parts = [w.reshape(KC, P, PAIRS, 2 * DH).transpose(2, 1, 0, 3).reshape(PAIRS, P, -1) for w in (wq, wk, wv)]
    parts.append(wo.reshape(PAIRS, 2, DH, D).transpose(0, 2, 1, 3).reshape(PAIRS, P, -1))
    return np.ascontiguousarray(np.concatenate(parts, axis=2))


def _rows(v, ht_n):
    import numpy as np
    out = np.zeros(ht_n * P, np.float32)
    out[:v.shape[0]] = v
    return np.ascontiguousarray(out.reshape(ht_n, P).T)


def _expand():
    import numpy as np
    e = np.zeros((E0 + 1, HT0 * P), np.float16)
    for n in range(E0 + 1):
        e[n, n * HID0:(n + 1) * HID0] = 1
    return e


def _tables():
    import numpy as np
    f = np.float32
    quarter = DH1 // 4
    freq = np.concatenate([(f(1) / f(1024)) ** np.linspace(0, 1, quarter, dtype=f), np.zeros(quarter, f)])
    theta = (np.arange(S, dtype=f)[:, None] * freq[None, :]).astype(f)
    cos, sin = np.cos(theta), np.sin(theta)
    by_tile = lambda a: (a / WSCALE).reshape(TPB, P, DH1).transpose(1, 0, 2).astype(f)
    slopes = (2.0 ** -0.5) ** np.arange(1, H1 + 1)
    r = np.exp(-slopes)
    i = np.arange(CHUNK)
    head = np.arange(P)[:, None] // 32 + 4 * np.arange(4)[None, :]
    diff = i[None, :] - i[:, None]
    dm = np.where(diff[:, None] >= 0, r[None, :, None] ** np.maximum(diff, 0)[:, None], 0)
    return {
        "cos": by_tile(np.concatenate([cos, cos], 1)), "sin": by_tile(np.concatenate([sin, -sin], 1)),
        "qdec": (r[None] ** (i[:, None] + 1.0)).astype(f), "kdec": (r[None] ** (CHUNK - 1.0 - i[:, None])).astype(f),
        "rc": (r[head] ** CHUNK).astype(f),
        "kvmask": (np.arange(P)[:, None] // 32 == np.arange(64)[None, :] // DH1).astype(f),
        "dmask": dm.reshape(P, 4, 4, P).transpose(0, 2, 1, 3).reshape(P, 4, 4 * P).astype(f),
    }


def prepare(inputs):
    import numpy as np
    i = {k: np.asarray(v) for k, v in inputs.items()}
    a = {"x": i["L0_attn_x"]}
    a["eye"] = np.eye(P, dtype=np.float16)
    a["w_attn0"] = _pack_attn0(i["L0_attn_Wq"], i["L0_attn_Wk"], i["L0_attn_Wv"], i["L0_attn_Wo"])
    a["betas"] = i["L0_attn_betas"].reshape(1, H0 * DH)
    flat = lambda w: w.reshape(-1, w.shape[-1])
    a["w_ffn0"] = _pack_ffn(np.concatenate([i["L0_ffn_sw1"], flat(i["L0_ffn_ew1"])]),
                            np.concatenate([i["L0_ffn_sw3"], flat(i["L0_ffn_ew3"])]),
                            np.concatenate([i["L0_ffn_sw2"].T, flat(i["L0_ffn_ew2"].transpose(0, 2, 1))]), HT0)
    a["wr"] = np.ascontiguousarray(_by_kc(i["L0_ffn_wr"].T))
    a["expand"] = _expand()
    a["w_ffn1"] = _pack_ffn(i["L1_ffn_gate_w"], i["L1_ffn_up_w"], i["L1_ffn_down_w"].T, HT1)
    a["gate_s"] = _rows(i["L1_ffn_gate_s"], HT1)
    a["up_s"] = _rows(i["L1_ffn_up_s"], HT1)
    a["down_s"] = i["L1_ffn_down_s"].reshape(1, D)
    a["w_attn1"] = np.concatenate([_by_kc(i["L1_attn_W" + n]) for n in "qkvo"], axis=2)
    a["mask"] = np.where(np.arange(SEG)[None] <= np.arange(P)[:, None] % SEG, 0, -1e30).astype(np.float32)
    a["rms_w"] = i["L1_attn_rms_w"].reshape(1, D)
    a.update(_tables())
    return {k: np.ascontiguousarray(v) for k, v in a.items()}


def network(nc, t, out):
    with ExitStack() as ctx:
        xt = ctx.enter_context(nc.sbuf_tensor("xt", [P, 2, KC, TOK], F16))
        y = ctx.enter_context(nc.sbuf_tensor("y", [P, TILES, D], F32))
        ident = ctx.enter_context(nc.sbuf_tensor("ident", [P, P], F16))
        loaded = ctx.enter_context(nc.semaphore("ident_loaded"))
        with nc.Block() as block:
            @block.sync
            def _(sp):
                sp.dma_start(ident[:], t["eye"]).then_inc(loaded, 16)
                sp.wait_ge(loaded, 16)
        with ExitStack() as first:
            x = first.enter_context(nc.sbuf_tensor("x_first", [P, TILES, D], F32))
            norm_phase(nc, "n0", ident, x, None, xt, load_x=t["x"])
        attn0_phase(nc, t["w_attn0"], t["betas"], t["mask"], xt, y, ident)
        x = ctx.enter_context(nc.sbuf_tensor("x_sb", [P, TILES, D], F32))
        norm_phase(nc, "n1", ident, x, y, xt, load_x=t["x"])
        ffn_phase(nc, "f0", t["w_ffn0"], xt, y, HT0, ident, router=(t["wr"], t["expand"]))
        norm_phase(nc, "n2", ident, x, y, xt)
        attn1_phase(nc, t["w_attn1"], t, xt, y, ident)
        norm_phase(nc, "n3", ident, x, y, xt)
        ffn_phase(nc, "f1", t["w_ffn1"], xt, y, HT1, ident, scales=(t["gate_s"], t["up_s"], t["down_s"]))
        norm_phase(nc, "n4", ident, x, y, None, store=out)


def kernel(**inputs):
    import concourse.bacc as _bacc
    from concourse.bass_utils import run_bass_kernel_spmd as _run

    arrays = prepare(inputs)
    nc = _bacc.Bacc("TRN2", target_bir_lowering=False, num_devices=1)
    tensors = {name: nc.dram_tensor(name, a.shape, mybir.dt.from_np(a.dtype), kind="ExternalInput").ap()
               for name, a in arrays.items()}
    out = nc.dram_tensor("out", (B, S, D), F32, kind="ExternalOutput").ap()
    network(nc, tensors, out)
    r = _run(nc, [arrays], core_ids=[0])
    return r.results[0]["out"]
```

```python
from contextlib import ExitStack

import concourse.bass as bass
from concourse import mybir

ALU = mybir.AluOpType
ACT = mybir.ActivationFunctionType
AX = mybir.AxisListType
F32 = mybir.dt.float32
F16 = mybir.dt.float16
U32 = mybir.dt.uint32
ds = bass.ds

P = 128
B, S, D = 4, 512, 256
TOK = B * S
TILES = TOK // P
TPB = S // P
KC = D // P
WSCALE = 64.0
LN_EPS = 1e-5

H0, DH, SEG = 16, 128, 64
NSEG = S // SEG
HG = 4
GROUPS = H0 // HG
ROWS16 = H0
E0, HID0 = 8, D * 4 // 3
HT0 = -(-(E0 + 1) * HID0 // P)
INTER = 704
HT1 = -(-INTER // P)
H1, DH1, CHUNK = 16, 16, 128


class Phase:

    def __init__(self, nc, ctx, name):
        self.nc, self.ctx, self.name = nc, ctx, name
        self.sems = []
        ctx.callback(self.clear)

    def sb(self, name, shape, dt=F32):
        return self.ctx.enter_context(self.nc.sbuf_tensor(f"{self.name}_{name}", shape, dt))

    def ps(self, name, shape, dt=F32):
        return self.ctx.enter_context(self.nc.psum_tensor(f"{self.name}_{name}", shape, dt))

    def sem(self, name):
        self.sems.append(self.nc.alloc_semaphore(f"{self.name}_{name}"))
        return self.sems[-1]

    def clear(self):
        self.nc.clear_and_free_semaphores(self.sems)
        self.nc.all_engine_barrier()


def bcast(ap, *shape):
    return ap.to_broadcast(list(shape))


def norm_phase(nc, name, ident, x, y, xt, load_x=None, load_y=None, store=None):
    with ExitStack() as ctx:
        ph = Phase(nc, ctx, name)
        xh = y if y is not None else ph.sb("xh", [P, TILES, D])
        stats = ph.sb("stats", [P, 2, TILES, 6])
        mean = ph.sb("mean", [P, 2, TILES])
        var = ph.sb("var", [P, 2, TILES])
        dif = ph.sb("dif", [P, 2, TILES])
        std = ph.sb("std", [P, 2, TILES])
        rstd = ph.sb("rstd", [P, 2, TILES])
        hi = ph.sb("hi", [P, TPB, D], F16)
        lo = ph.sb("lo", [P, TPB, D], F16)
        pt = [ph.ps(f"pt{i}", [P, KC, S], F16) for i in range(2)]
        x_in = ph.sem("x_in")
        dve = ph.sem("dve")
        var_ready = ph.sem("var_ready")
        std_ready = ph.sem("std_ready")
        xh_ready = ph.sem("xh_ready")
        hi_ready = ph.sem("hi_ready")
        lo_ready = ph.sem("lo_ready")
        t_ready = ph.sem("t_ready")
        thi_out = ph.sem("thi_out")
        tlo_out = ph.sem("tlo_out")
        x_done = ph.sem("x_done")
        stored = ph.sem("stored")
        n_std = (y is not None) + (store is None)

        with nc.Block() as block:
            @block.sync
            def _(sp):
                if load_x is not None:
                    src = load_x.rearrange("b (t p) d -> p b t d", p=P)
                    for b in range(B):
                        sp.dma_start(x[:, b * TPB:(b + 1) * TPB, :], src[:, b]).then_inc(x_in, 16)
                if load_y is not None:
                    src = load_y.rearrange("b (t p) d -> p b t d", p=P)
                    for b in range(B):
                        sp.dma_start(y[:, b * TPB:(b + 1) * TPB, :], src[:, b]).then_inc(x_in, 16)
                if store is not None:
                    dst = store.rearrange("b (t p) d -> p b t d", p=P)
                    sp.wait_ge(x_done, 1)
                    for b in range(B):
                        sp.dma_start(dst[:, b], x[:, b * TPB:(b + 1) * TPB, :]).then_inc(stored, 16)
                    sp.wait_ge(stored, 16 * B)

            @block.vector
            def _(v):
                done = [0]

                def own(ins, n=1):
                    ins.then_inc(dve, 1)
                    done[0] += n
                    v.wait_ge(dve, done[0])

                def moments(src, k, n):
                    with v.Fori(0, TILES) as t:
                        v.bn_stats(stats[:, k, ds(t, 1), :], src[:, ds(t, 1), :]).then_inc(dve, 1)
                    done[0] += TILES
                    v.wait_ge(dve, done[0])
                    st = stats[:, k]
                    own(v.tensor_tensor(mean[:, k], st[:, :, 1], st[:, :, 4], ALU.add))
                    own(v.tensor_tensor(dif[:, k], st[:, :, 1], st[:, :, 4], ALU.subtract))
                    own(v.tensor_tensor(dif[:, k], dif[:, k], dif[:, k], ALU.mult))
                    own(v.tensor_tensor(var[:, k], st[:, :, 2], st[:, :, 5], ALU.add))
                    own(v.tensor_scalar(mean[:, k], mean[:, k], 0.5, None, ALU.mult))
                    own(v.tensor_scalar(var[:, k], var[:, k], 1.0 / D, LN_EPS, ALU.mult, ALU.add))
                    v.scalar_tensor_tensor(var[:, k], dif[:, k], 0.25, var[:, k],
                                           ALU.mult, ALU.add).then_inc(var_ready, 1)
                    v.wait_ge(std_ready, n)
                    own(v.reciprocal(rstd[:, k], std[:, k]))

                if load_x is not None:
                    v.wait_ge(x_in, 16 * B * (1 if load_y is None else 2))
                if y is not None:
                    moments(y, 0, 1)
                    with v.Fori(0, TILES) as t:
                        v.tensor_scalar(y[:, ds(t, 1), :], y[:, ds(t, 1), :], mean[:, 0, ds(t, 1)],
                                        rstd[:, 0, ds(t, 1)], ALU.subtract, ALU.mult).then_inc(dve, 1)
                    done[0] += TILES
                    v.wait_ge(dve, done[0])
                    own(v.tensor_tensor(x[:], x[:], y[:], ALU.add))
                if store is not None:
                    v.tensor_scalar(dif[:, 0], dif[:, 0], 0.0, None, ALU.mult).then_inc(x_done, 1)
                    return
                moments(x, 1, n_std)
                with v.Fori(0, TILES) as t:
                    v.tensor_scalar(xh[:, ds(t, 1), :], x[:, ds(t, 1), :], mean[:, 1, ds(t, 1)],
                                    rstd[:, 1, ds(t, 1)], ALU.subtract, ALU.mult).then_inc(xh_ready, 1)
                v.wait_ge(xh_ready, TILES)
                with v.Fori(0, B) as b:
                    v.wait_ge(hi_ready, b + 1)
                    v.tensor_tensor(lo[:], xh[:, ds(b * TPB, TPB), :], hi[:],
                                    ALU.subtract).then_inc(lo_ready, 1)
                    v.wait_ge(t_ready, b * 2 + 2)
                    v.tensor_copy(xt[:, 1, :, ds(b * S, S)], pt[1][:]).then_inc(tlo_out, 1)

            if store is None:
                @block.tensor
                def _(pe):
                    with pe.Fori(0, B) as b:
                        for part, (src, ready) in enumerate(((hi, hi_ready), (lo, lo_ready))):
                            pe.wait_ge(ready, b + 1)
                            for kc in range(KC):
                                for t in range(TPB):
                                    last = pe.transpose(pt[part][:, kc, t * P:(t + 1) * P],
                                                        src[:, t, kc * P:(kc + 1) * P], ident[:])
                            last.then_inc(t_ready, 1)

            @block.scalar
            def _(act):
                act.preload_act_table(ACT.Sqrt)
                for k in ([0] if y is not None else []) + ([1] if store is None else []):
                    n = 1 if k == 0 or y is None else 2
                    act.wait_ge(var_ready, n)
                    act.activation(std[:, k], var[:, k], ACT.Sqrt).then_inc(std_ready, 1)
                if store is not None:
                    return
                act.wait_ge(xh_ready, TILES)
                with act.Fori(0, B) as b:
                    act.activation(hi[:], xh[:, ds(b * TPB, TPB), :], ACT.Copy).then_inc(hi_ready, 1)
                    act.wait_ge(t_ready, b * 2 + 1)
                    act.activation(xt[:, 0, :, ds(b * S, S)], pt[0][:], ACT.Copy).then_inc(thi_out, 1)
                    act.wait_ge(tlo_out, b + 1)


def ffn_phase(nc, name, w_dram, xt, y, ht_n, ident, router=None, scales=None):
    WC = 2 * KC * P + D
    with ExitStack() as ctx:
        ph = Phase(nc, ctx, name)
        wst = ph.sb("wst", [P, 2, WC])
        wsc = ph.sb("wsc", [P, 1])
        w = ph.sb("w", [P, 2, ht_n, WC], F16)
        sil = ph.sb("sil", [P, 2, S])
        hv = ph.sb("hv", [P, 2, S])
        hh = ph.sb("hh", [P, 2, S], F16)
        hl = ph.sb("hl", [P, 2, S], F16)
        zero = ph.sb("zero", [P, S], F16)
        up = [ph.ps(f"up{i}", [P, 512]) for i in range(2)]
        vp = [ph.ps(f"vp{i}", [P, 512]) for i in range(2)]
        gp = [ph.ps(f"gp{i}", [P, 512]) for i in range(2)]
        yp = [ph.ps(f"yp{i}", [P, 2, D]) for i in range(2)]
        w_in = [ph.sem(f"w_in{i}") for i in range(2)]
        w_const = ph.sem("w_const")
        w_scaled = ph.sem("w_scaled")
        w_hi = ph.sem("w_hi")
        w_ready = ph.sem("w_ready")
        const_in = ph.sem("const_in")
        zeroed = ph.sem("zeroed")
        uvg = ph.sem("uvg")
        sil_ready = ph.sem("sil_ready")
        sv = ph.sem("sv")
        h_ready = ph.sem("h_ready")
        hh_ready = ph.sem("hh_ready")
        hl_ready = ph.sem("hl_ready")
        y_part = ph.sem("y_part")
        y_out = ph.sem("y_out")
        if router is not None:
            wr_dram, expand_dram = router
            wr32 = ph.sb("wr32", [P, KC, E0])
            wrp = ph.sb("wrp", [P, 2, KC, E0], F16)
            expand = ph.sb("expand", [P, ht_n * P], F16)
            lg = ph.sb("lg", [P, TILES, E0])
            mx = ph.sb("mx", [P, TILES])
            top = ph.sb("top", [P, TILES, 8])
            topi = ph.sb("topi", [P, TILES, 8], U32)
            topf = ph.sb("topf", [P, TILES, 8])
            eid = ph.sb("eid", [P, E0])
            gates = ph.sb("gates", [P, TILES, 16])
            pick = ph.sb("pick", [P, TILES, E0])
            gt32 = ph.sb("gt32", [P, TILES, 16])
            gparts = ph.sb("gparts", [P, 2, TILES, 16], F16)
            gt = ph.sb("gt", [P, 2, TOK], F16)
            wr_in = ph.sem("wr_in")
            rsem = ph.sem("rsem")
            r_logits = ph.sem("r_logits")
            r_sub = ph.sem("r_sub")
            r_exp = ph.sem("r_exp")
            r_gates = ph.sem("r_gates")
            r_ghi = ph.sem("r_ghi")
            r_glo = ph.sem("r_glo")
            r_t = ph.sem("r_t")
            r_tout = ph.sem("r_tout")
            r_w = ph.sem("r_w")
        if scales is not None:
            scaled = ph.sem("scaled")
            s1 = ph.sb("s1", [P, ht_n])
            s3 = ph.sb("s3", [P, ht_n])
            s2 = ph.sb("s2", [P, D])
        h_scale = WSCALE if scales is None else 1.0
        tg = [[bank[:].bitcast(F16) for bank in pair] for pair in (vp, gp)]

        with nc.Block() as block:
            @block.sync
            def _(sp):
                if router is not None:
                    with nc.allow_non_contiguous_dma(reason="a small table"):
                        sp.dma_start(wr32[:], wr_dram).then_inc(wr_in, 16)
                    sp.wait_ge(rsem, 1)
                    sp.dma_start(expand[0:E0 + 1, :], expand_dram).then_inc(const_in, 16)
                if scales is not None:
                    sp.dma_start(s1[:], scales[0]).then_inc(const_in, 16)
                    sp.dma_start(s3[:], scales[1]).then_inc(const_in, 16)
                    sp.dma_start(s2[:], scales[2].to_broadcast([P, D])).then_inc(const_in, 16)
                for t in range(2):
                    sp.dma_start(wst[:, t, :], w_dram[t]).then_inc(w_in[t], 16)
                with sp.Fori(1, ht_n // 2) as k:
                    for par in range(2):
                        sp.wait_ge(w_ready, k * 2 - 1 + par)
                        sp.dma_start(wst[:, par, :], w_dram[ds(k * 2 + par, 1)].rearrange(
                            "o p c -> p (o c)")).then_inc(w_in[par], 16)

            @block.gpsimd
            def _(pool):
                pool.memset(wsc[:], WSCALE).then_inc(w_const, 1)
                pool.wait_ge(w_const, 1)
                with pool.Fori(0, ht_n // 2) as k:
                    for par in range(2):
                        pool.wait_ge(w_in[par], k * 16 + 16)
                        pool.tensor_tensor(wst[:, par, :], wst[:, par, :], bcast(wsc[:], P, WC),
                                           ALU.mult).then_inc(w_scaled, 1)
                        pool.wait_ge(w_scaled, k * 2 + par + 1)
                        pool.tensor_copy(w[:, 0, ds(k * 2 + par, 1), :],
                                         wst[:, par, :]).then_inc(w_hi, 1)
                        pool.wait_ge(w_hi, k * 2 + par + 1)
                        pool.tensor_tensor(w[:, 1, ds(k * 2 + par, 1), :], wst[:, par, :],
                                           w[:, 0, ds(k * 2 + par, 1), :],
                                           ALU.subtract).then_inc(w_ready, 1)

            def wcol(part, ht, col, n):
                return w[:, part, ds(ht, 1), col:col + n].rearrange("p o c -> p (o c)") \
                    if not isinstance(ht, int) else w[:, part, ht, col:col + n]

            @block.tensor
            def _(pe):
                def three(out, wa, xa, start, stop):
                    for n, (i, j) in enumerate(((0, 0), (0, 1), (1, 0))):
                        last = pe.matmul(out, wa(i), xa(j), start=start and n == 0,
                                         stop=stop and n == 2, skip_group_check=True)
                    return last

                if router is not None:
                    pe.wait_ge(r_w, 3)
                    for t in range(TILES):
                        for kc in range(KC):
                            last = three(up[0][:, t * E0:(t + 1) * E0],
                                         lambda i: xt[:, i, kc, t * P:(t + 1) * P],
                                         lambda j: wrp[:, j, kc, :],
                                         t == 0 and kc == 0, t == TILES - 1 and kc == KC - 1)
                    last.then_inc(r_logits, 1)
                    pe.wait_ge(r_ghi, 1)
                    pe.wait_ge(r_glo, 1)
                    for part in range(2):
                        for t in range(TILES):
                            tgt = tg[part][t // 8]
                            last = pe.transpose(tgt[0:16, (t % 8) * P:(t % 8 + 1) * P],
                                                gparts[:, part, t, :], ident[:])
                        last.then_inc(r_t, 1)
                    pe.wait_ge(r_tout, 4)

                def products(s, b, ht, par):
                    for dst, col in ((up, 0), (vp, KC * P)):
                        for kc in range(KC):
                            last = three(dst[par][:], lambda i: wcol(i, ht, col + kc * P, P),
                                         lambda j: xt[:, j, kc, ds(b * S, S)], kc == 0, kc == KC - 1)
                    if router is not None:
                        for j in range(2):
                            last = pe.matmul(gp[par][:], expand[:, ds(ht * P, P)],
                                             gt[:, j, ds(b * S, S)], start=j == 0, stop=j == 1)
                    last.then_inc(uvg, 1)

                def down(s, ht, par):
                    pe.wait_ge(hh_ready, s + 1)
                    pe.wait_ge(hl_ready, s + 1)
                    for t in range(TPB):
                        src = (hh, hl)
                        last = three(yp[t // 2][:, t % 2, :],
                                     lambda i: src[i][:, par, t * P:(t + 1) * P],
                                     lambda j: wcol(j, ht, 2 * KC * P, D), False, False)
                    last.then_inc(y_part, 1)

                pe.wait_ge(zeroed, 1)
                with pe.Fori(0, B) as b:
                    s0 = b * ht_n
                    pe.wait_ge(y_out, b * 2 + 1)
                    for bank in yp:
                        pe.matmul(bank[:].rearrange("p a d -> p (a d)"), zero[:, 0:P], zero[:],
                                  start=True, stop=False, skip_group_check=True)
                    def step(ht, par):
                        pe.wait_ge(h_ready, s0 + ht + 1)
                        pe.wait_ge(w_ready, ht + 1)
                        products(None, b, ht, par)
                    step(0, 0)
                    with pe.Fori(0, ht_n // 2 - 1) as k:
                        step(k * 2 + 1, 1)
                        down(s0 + k * 2, k * 2, 0)
                        step(k * 2 + 2, 0)
                        down(s0 + k * 2 + 1, k * 2 + 1, 1)
                    step(ht_n - 1, 1)
                    down(s0 + ht_n - 2, ht_n - 2, 0)
                    down(s0 + ht_n - 1, ht_n - 1, 1)

            @block.scalar
            def _(act):
                if router is not None:
                    act.preload_act_table(ACT.Exp)
                    act.wait_ge(wr_in, 16)
                    act.activation(wrp[:, 0], wr32[:], ACT.Copy, scale=WSCALE).then_inc(r_w, 1)
                    act.wait_ge(r_sub, 1)
                    act.activation(lg[:], lg[:], ACT.Exp).then_inc(r_exp, 1)
                    act.wait_ge(r_gates, 1)
                    act.activation(gparts[:, 0], gt32[:], ACT.Copy).then_inc(r_ghi, 1)
                    for part in range(2):
                        act.wait_ge(r_t, part + 1)
                        for i in range(2):
                            act.activation(gt[0:16, part, i * 1024:(i + 1) * 1024], tg[part][i][0:16, :],
                                           ACT.Copy).then_inc(r_tout, 1)
                act.preload_act_table(ACT.Silu)
                if scales is not None:
                    act.wait_ge(scaled, 2)
                with act.Fori(0, B) as b:
                    with act.Fori(0, ht_n // 2) as k:
                        for par in range(2):
                            s = b * ht_n + k * 2 + par
                            act.wait_ge(uvg, s + 1)
                            sc = 1.0 / WSCALE if scales is None else s1[:, ds(k * 2 + par, 1)]
                            act.activation(sil[:, par], up[par][:], ACT.Silu,
                                           scale=sc).then_inc(sil_ready, 1)
                            act.wait_ge(h_ready, s + 3)
                            act.wait_ge(y_part, s + 1)
                            act.activation(hh[:, par], hv[:, par], ACT.Copy).then_inc(hh_ready, 1)
                    act.wait_ge(y_part, b * ht_n + ht_n + 2)
                    for i in range(2):
                        act.activation(y[:, ds(b * TPB + i * 2, 2), :], yp[i][:], ACT.Copy,
                                       scale=1.0 / (WSCALE * h_scale)).then_inc(y_out, 1)
            @block.vector
            def _(v):
                done = [0]
                own_sem = rsem if router is not None else zeroed

                def own(ins):
                    ins.then_inc(own_sem, 1)
                    done[0] += 1
                    v.wait_ge(own_sem, done[0])

                if router is not None:
                    own(v.memset(expand[:], 0.0))
                    own(v.memset(gt[:], 0.0))
                    own(v.memset(gt32[:], 0.0))
                v.memset(zero[:], 0.0).then_inc(zeroed, 1)
                if router is None:
                    done[0] += 1
                if router is not None:
                    for e in range(E0):
                        own(v.memset(eid[:, e:e + 1], float(e)))
                    v.wait_ge(r_w, 1)
                    v.scalar_tensor_tensor(wrp[:, 1], wr32[:], WSCALE, wrp[:, 0], ALU.mult,
                                           ALU.subtract).then_inc(r_w, 1)
                    v.wait_ge(const_in, 16)
                    v.sem_inc(r_w, 1)
                    v.wait_ge(r_logits, 1)
                    flat = up[0][:, 0:TILES * E0].rearrange("p (t e) -> p t e", e=E0)
                    own(v.tensor_scalar(lg[:], flat, 1.0 / WSCALE, None, ALU.mult))
                    own(v.tensor_reduce(mx[:], lg[:], AX.X, ALU.max))
                    v.tensor_tensor(lg[:], lg[:], bcast(mx[:].unsqueeze(2), P, TILES, E0),
                                    ALU.subtract).then_inc(r_sub, 1)
                    v.wait_ge(r_exp, 1)
                    own(v.tensor_reduce(mx[:], lg[:], AX.X, ALU.add))
                    own(v.reciprocal(mx[:], mx[:]))
                    own(v.tensor_tensor(lg[:], lg[:], bcast(mx[:].unsqueeze(2), P, TILES, E0), ALU.mult))
                    for t in range(TILES):
                        own(v.max(top[:, t, :], lg[:, t, :]))
                        own(v.max_index(topi[:, t, :], top[:, t, :], lg[:, t, :]))
                    own(v.tensor_copy(topf[:], topi[:]))
                    own(v.tensor_tensor(mx[:], top[:, :, 0], top[:, :, 1], ALU.add))
                    own(v.reciprocal(mx[:], mx[:]))
                    own(v.tensor_tensor(top[:, :, 0:2], top[:, :, 0:2],
                                        bcast(mx[:].unsqueeze(2), P, TILES, 2), ALU.mult))
                    ids = bcast(eid[:].unsqueeze(1), P, TILES, E0)
                    for r in range(2):
                        own(v.tensor_tensor(pick[:], bcast(topf[:, :, r:r + 1], P, TILES, E0), ids,
                                            ALU.is_equal))
                        own(v.tensor_tensor(pick[:], pick[:], bcast(top[:, :, r:r + 1], P, TILES, E0),
                                            ALU.mult))
                        own(v.tensor_tensor(gt32[:, :, 1:1 + E0], gt32[:, :, 1:1 + E0], pick[:], ALU.add))
                    v.memset(gt32[:, :, 0:1], 1.0).then_inc(r_gates, 1)
                    v.wait_ge(r_ghi, 1)
                    v.tensor_tensor(gparts[:, 1], gt32[:], gparts[:, 0], ALU.subtract).then_inc(r_glo, 1)
                for n in range(2):
                    v.sem_inc(h_ready, 1)
                    v.sem_inc(y_part, 1)
                v.sem_inc(y_out, 1)
                if scales is not None:
                    v.wait_ge(const_in, 48)
                    v.tensor_scalar(s1[:], s1[:], 1.0 / WSCALE, None, ALU.mult).then_inc(scaled, 1)
                    v.tensor_scalar(s3[:], s3[:], 1.0 / WSCALE, None, ALU.mult).then_inc(scaled, 1)
                    v.wait_ge(scaled, 2)
                with v.Fori(0, B) as b:
                    with v.Fori(0, ht_n // 2) as k:
                        for par in range(2):
                            s = b * ht_n + k * 2 + par
                            v.wait_ge(uvg, s + 1)
                            v.wait_ge(sil_ready, s + 1)
                            if router is not None:
                                v.tensor_tensor(hv[:, par], vp[par][:], sil[:, par],
                                                ALU.mult).then_inc(sv, 1)
                                v.wait_ge(sv, s + 1)
                                v.tensor_tensor(hv[:, par], hv[:, par], gp[par][:],
                                                ALU.mult).then_inc(h_ready, 1)
                            else:
                                v.scalar_tensor_tensor(hv[:, par], vp[par][:], s3[:, ds(k * 2 + par, 1)],
                                                       sil[:, par], ALU.mult,
                                                       ALU.mult).then_inc(h_ready, 1)
                            v.wait_ge(hh_ready, s + 1)
                            v.tensor_tensor(hl[:, par], hv[:, par], hh[:, par],
                                            ALU.subtract).then_inc(hl_ready, 1)
                if scales is not None:
                    v.wait_ge(y_out, B * 2 + 1)
                    v.tensor_tensor(y[:], y[:], bcast(s2[:].unsqueeze(1), P, TILES, D), ALU.mult)


BESIDE = (
    (("own_dot 0", "project 0 0", "past_att_hi 3", "past_att_lo 3", "own_prob_hi 1", "own_prob_lo 1"),
     ("own_dot_out 0", "project 0 1", "past_att_turn 3"),
     ("split 0 0", "past_att_out 3", "sigma 0 0", "low 0 0")),
    (("past_output 0", "split 0 1", "sigma_hi 0 0", "sigma_lo 0 0", "sigma 0 1", "low 0 1"),
     ("past_output 1", "past_output_out", "project 0 2", "own_prob_turn 1"),
     ("own_pt_hi 1", "own_pt_lo 1", "sigma_hi 0 1", "sigma_lo 0 1", "split 0 2")),
    (("project 0 3", "own_dot 1", "sigma 0 2", "low 0 2"),
     ("own_dot_out 1", "sigma_hi 0 2", "sigma_lo 0 2", "value 0 0"),
     ("split 0 3", "own_add 0", "sigma 0 3", "low 0 3", "weights 0")),
    (("value 0 1", "own_att_hi 0", "own_att_lo 0", "sigma_hi 0 3", "sigma_lo 0 3", "value_out 0 0"),
     ("score 0", "project 1 0", "own_att_turn 0", "value_lo 0 0"),
     ("value_out 0 1", "row_max 0", "own_att_out 0", "value_lo 0 1", "subtract_max 0", "own_add 1")),
    (("project 1 1", "key_turn 0", "split 1 0", "exponent 0"),
     ("project 1 2", "key_lo 0", "sigma 1 0", "low 1 0", "own_att_hi 1", "own_att_lo 1"),
     ("key_hi 0", "split 1 1", "sigma_hi 1 0", "sigma_lo 1 0", "row_sum 0", "normalise 0", "sigma 1 1", "low 1 1")),
    (("project 1 3", "own_att_turn 1", "sigma_hi 1 1", "sigma_lo 1 1", "split 1 2"),
     ("value 1 0", "sigma 1 2", "low 1 2", "own_att_out 1"),
     ("prob_hi 0", "prob_lo 0", "split 1 3", "sigma_hi 1 2", "sigma_lo 1 2", "sigma 1 3", "low 1 3", "own_add 2",
      "weights 1")),
    (("value 1 1", "prob_turn 0", "sigma_hi 1 3", "sigma_lo 1 3", "value_out 1 0"),
     ("pt_lo 0", "own_att_hi 2", "own_att_lo 2", "value_lo 1 0"),
     ("pt_hi 0", "value_out 1 1", "value_lo 1 1")),
    (("key_turn 1", "key_hi 1", "key_lo 1"),
     ("score 1", "own_att_turn 2"),
     ("row_max 1", "own_att_out 2", "subtract_max 1", "exponent 1", "row_sum 1", "normalise 1", "own_add 3")),
)


class Unit:

    def __init__(self, n, par):
        self.n, self.par = n, par
        self.b, self.k = n % B, (n // B) % GROUPS


def attn0_phase(nc, w_dram, wo_dram, betas, mask_dram, xt, y_dram, ident):
    KQV = 2 * HG * DH
    WC = 3 * KQV
    EIGHTH = WC // 8
    HALF = ((slice(0, SEG), slice(SEG, P)), (slice(SEG, P), slice(0, SEG)))
    with ExitStack() as ctx:
        ph = Phase(nc, ctx, "a0")
        w = ph.sb("w", [P, 2, 2, WC], F16)
        wo = ph.sb("wo", [P, 2, H0 * D], F16)
        wst = ph.sb("wst", [P, EIGHTH])
        wsc = ph.sb("wsc", [P, 2])
        beta = ph.sb("beta", [P, H0 * DH])
        omb = ph.sb("omb", [P, HG * DH])
        mask = ph.sb("mask", [P, SEG])
        qs = ph.sb("qs", [P, 2, 2, S], F16)
        ks = ph.sb("ks", [P, 2, 2, S], F16)
        x32 = ph.sb("x32", [P, 2, S])
        ee = ph.sb("ee", [P, 2, S])
        sg = ph.sb("sg", [P, 2, 2, HG, TPB, 4, SEG], F16)
        skr = ph.sb("skr", [P, 2, 2, HG, TPB, P], F16)
        v32 = ph.sb("v32", [P, 2, TPB, HG * DH])
        vs = ph.sb("vs", [P, 2, TPB, HG * DH], F16)
        sm = ph.sb("sm", [P, 2 * TPB, SEG])
        red = ph.sb("red", [P, 2, 2 * TPB])
        ps = ph.sb("ps", [P, 2, 2 * TPB, SEG], F16)
        ptb = ph.sb("ptb", [P, 2, 2, TPB, P], F16)
        ms = ph.sb("ms", [P, 2, 2, HG, DH + 2], F16)
        ms0 = ph.sb("ms0", [P, 2, DH + 2], F16)
        dd = ph.sb("dd", [P, 2, 2, HG, DH + 2], F16)
        rd = ph.sb("rd", [P, HG])
        tq = ph.sb("tq", [P, 2, HG, DH])
        am = ph.sb("am", [P, 2, HG * DH])
        at = ph.sb("at", [P, 2, TPB, HG * DH])
        ats = ph.sb("ats", [P, 2, HG * DH], F16)
        att = ph.sb("att", [P, 2, ROWS16, P], F16)
        yst = ph.sb("yst", [P, D])
        mem = ph.ps("mem", [P, HG, 256])
        num = ph.ps("num", [P, HG, 256])
        pj = [ph.ps(f"pj{i}", [P, S]) for i in range(2)]
        tr = [ph.ps(f"tr{i}", [P, S]) for i in range(2)]
        tr16 = [t[:].bitcast(F16) for t in tr]

        names = ("w0_in wo_in w0_hi w0_lo wo_hi wo_lo w_in w_sc w_hi w_ready const_in beta_r init pj_full x32_r"
                 " hi_r ex_r e1_r lo_r sg_r sghi sglo skr_full skrhi skrlo v_r omb_r vlo s_full sm_r mx_r"
                 " sd_r pex_r sum_r ri_r pn_r phi plo pt_full pthi ptlo num_full rd_r t_r d_r dhi dlo am_r"
                 " mem_full mhi mlo dot_full dot_r at_r ahi alo att_full att_r y_full y_out y_stored yst_free").split()
        m = {n: ph.sem(n) for n in names}

        def three(pe, out, wa, xa, start=False, stop=False):
            for n, (i, j) in enumerate(((0, 0), (0, 1), (1, 0))):
                last = pe.matmul(out, wa(i), xa(j), start=start and n == 0, stop=stop and n == 2,
                                 skip_group_check=True)
            return last

        def units(eng, steps, retrieve, update, split):
            def beside(names, plain, own, past):
                for text in names:
                    name, *args = text.split()
                    unit = {"own": own, "past": past}.get(name.split("_")[0], plain)
                    name = name.removeprefix("own_").removeprefix("past_")
                    if unit is not None and name in steps:
                        steps[name](unit, *[int(a) for a in args])

            def segment(j, plain, own, past):
                retrieve(own, j)
                beside(BESIDE[j][0], plain, own, past)
                if j < NSEG - 1:
                    update(own, j)
                beside(BESIDE[j][1], plain, own, past)
                if j < NSEG - 1:
                    split(own, j)
                beside(BESIDE[j][2], plain, own, past)

            for row in BESIDE:
                for names in row:
                    beside(names, Unit(0, 0), None, None)
            for j in range(2):
                segment(j, Unit(1, 1), Unit(0, 0), None)
            with eng.Fori(0, GROUPS) as k:
                with eng.Fori(0, B // 2) as bb:
                    for par in range(2):
                        n = k * B + bb * 2 + par
                        cur, new, after = Unit(n, par), Unit(n + 1, 1 - par), Unit(n + 2, par)
                        for j in range(2, NSEG):
                            segment(j, new, cur, None)
                        for j in range(2):
                            segment(j, after, new, cur)

        def later(unit):
            return not isinstance(unit.n, int) or unit.n > 0

        def keys(par, part, c):
            return sg[:, par, part, c, :, 0::3, :]

        def queries(par, part, c):
            return sg[:, par, part, c, :, 1:3, :]

        def probs_t(part, odd):
            return tr16[part][0:SEG, :].rearrange("p (c t o s) -> p c t o s", c=2, t=TPB, o=2)[:, :, :, odd, :]

        with nc.Block() as block:
            @block.sync
            def _(sp):
                sp.dma_start(mask[:], mask_dram).then_inc(m["const_in"], 16)
                sp.dma_start(beta[:], betas.to_broadcast([P, H0 * DH])).then_inc(m["const_in"], 16)
                sp.dma_start(v32[:].rearrange("p a t e -> p (a t e)")[:, 0:WC], w_dram[0]).then_inc(m["w0_in"], 16)
                sp.dma_start(at[:].rearrange("p a t e -> p (a t e)"), wo_dram).then_inc(m["wo_in"], 16)

                def weights(new, half):
                    if later(new) or half:
                        sp.wait_ge(m["w_ready"], new.n * 2 + half)
                    grp, e = (new.n // B + 1) % GROUPS, new.b * 2 + half
                    src = w_dram.rearrange("g p (e c) -> g e p c", e=8)[ds(grp, 1), ds(e, 1)]
                    sp.dma_start(wst[:], src.rearrange("g e p c -> p (g e c)")).then_inc(m["w_in"], 16)

                def output_out(u):
                    sp.wait_ge(m["y_out"], u.n + 1)
                    rows = y_dram.rearrange("b (s k m) d -> b k s m d", s=NSEG, k=GROUPS)[ds(u.b, 1), ds(u.k, 1)]
                    for s in range(NSEG):
                        sp.dma_start(rows[:, :, s].rearrange("x y m d -> (x y m) d"),
                                     yst[s * 16:(s + 1) * 16, :]).then_inc(m["y_stored"], 16)
                    sp.wait_ge(m["y_stored"], (u.n + 1) * NSEG * 16)
                    sp.sem_inc(m["yst_free"], 1)

                sp.sem_inc(m["yst_free"], 1)

                def nothing(u, j):
                    pass
                units(sp, dict(weights=weights, output_out=output_out), nothing, nothing, nothing)

            @block.gpsimd
            def _(pool):
                def weights(new, half):
                    n = new.n * 2 + half
                    if later(new):
                        pool.wait_ge(m["pj_full"], new.n * 12)
                    pool.wait_ge(m["w_in"], n * 16 + 16)
                    pool.tensor_tensor(wst[:], wst[:], bcast(wsc[:, 0:1], P, EIGHTH), ALU.mult).then_inc(m["w_sc"], 1)
                    pool.wait_ge(m["w_sc"], n + 3)
                    buf, cols = (new.n // B + 1) % 2, (new.b * 2 + half) * EIGHTH

                    def to(part):
                        return w[:].rearrange("p a q c -> p (a q c)")[:, ds(buf * (2 * WC) + part * WC + cols, EIGHTH)]
                    pool.tensor_tensor(to(0), wst[:], bcast(wsc[:, 1:2], P, EIGHTH), ALU.mult).then_inc(m["w_hi"], 1)
                    pool.wait_ge(m["w_hi"], n + 1)
                    pool.tensor_tensor(to(1), wst[:], to(0), ALU.subtract).then_inc(m["w_ready"], 1)

                def low(new, h, ci):
                    c, dst = ci % 2, (qs, ks)[ci // 2]
                    pool.wait_ge(m["hi_r"], (new.n * 2 + h) * 4 + ci + 1)
                    pool.tensor_tensor(dst[:, 1, c, :], x32[:, c, :], dst[:, 0, c, :], ALU.subtract).then_inc(m["lo_r"], 1)

                def sigma_lo(new, h, ci):
                    c, to = ci % 2, (queries, keys)[ci // 2]
                    pool.wait_ge(m["sghi"], (new.n * 2 + h) * 4 + ci + 1)
                    head = h * 2 + c
                    pool.tensor_tensor(to(new.par, 1, head), ee[:, c, :].rearrange("p (t o s) -> p t o s", t=TPB, o=2),
                                       to(new.par, 0, head), ALU.subtract).then_inc(m["sglo"], 1)

                def value_lo(new, h, i):
                    cols = slice(h * 2 * DH, (h + 1) * 2 * DH)
                    pool.wait_ge(m["v_r"], (new.n * 2 + h) * 2 + i + 1)
                    pool.tensor_tensor(vs[:, 1, i * 2:i * 2 + 2, cols], v32[:, new.par, i * 2:i * 2 + 2, cols],
                                       vs[:, 0, i * 2:i * 2 + 2, cols], ALU.subtract).then_inc(m["vlo"], 1)

                def subtract_max(new, h):
                    pool.wait_ge(m["mx_r"], new.n * 2 + h + 1)
                    pool.tensor_tensor(sm[:], sm[:], bcast(red[:, 0].unsqueeze(2), P, 2 * TPB, SEG),
                                       ALU.subtract).then_inc(m["sd_r"], 1)

                def normalise(new, h):
                    pool.wait_ge(m["ri_r"], new.n * 2 + h + 1)
                    pool.tensor_tensor(sm[:], sm[:], bcast(red[:, 1].unsqueeze(2), P, 2 * TPB, SEG),
                                       ALU.mult).then_inc(m["pn_r"], 1)

                def prob_lo(new, h):
                    pool.wait_ge(m["phi"], new.n * 2 + h + 1)
                    pool.tensor_tensor(ps[:, 1], sm[:], ps[:, 0], ALU.subtract).then_inc(m["plo"], 1)

                def add(u, t):
                    pool.wait_ge(m["dot_r"], u.n * 4 + 4)
                    pool.wait_ge(m["am_r"], u.n * NSEG + 2 * t + 2)
                    pool.tensor_tensor(at[:, u.par, t], at[:, u.par, t], am[:, t % 2], ALU.add).then_inc(m["at_r"], 1)

                def att_lo(u, t):
                    pool.wait_ge(m["ahi"], u.n * TPB + t + 1)
                    pool.tensor_tensor(ats[:, 1], at[:, u.par, t], ats[:, 0], ALU.subtract).then_inc(m["alo"], 1)

                def nothing(u, j):
                    pass

                pool.memset(wsc[:, 0:1], WSCALE).then_inc(m["w_sc"], 1)
                pool.memset(wsc[:, 1:2], 1.0).then_inc(m["w_sc"], 1)
                pool.wait_ge(m["w_sc"], 2)
                units(pool, dict(weights=weights, low=low, sigma_lo=sigma_lo, value_lo=value_lo,
                                 subtract_max=subtract_max, normalise=normalise, prob_lo=prob_lo, add=add,
                                 att_lo=att_lo), nothing, nothing, nothing)

            @block.tensor
            def _(pe):
                def wcol(part, k, col, n):
                    if isinstance(k, int):
                        return w[:, k % 2, part, col:col + n]
                    return w[:].rearrange("p a q c -> p (a q c)")[:, ds((k % 2) * (2 * WC) + (part * WC + col), n)]

                def project(new, h, ci):
                    i = new.n * 2 + h
                    kind, c = ci // 2, ci % 2
                    if ci == 0 and h == 0:
                        if later(new):
                            pe.wait_ge(m["w_ready"], new.n * 2)
                        else:
                            pe.wait_ge(m["w0_lo"], 3)
                    if ci >= 2:
                        pe.wait_ge(m["ex_r"], i * 4 + ci - 1)
                    elif later(new) or h:
                        pe.wait_ge(m["v_r"], i * 2 + ci - 1)
                    for kc in range(KC):
                        last = three(pe, pj[c][:],
                                     lambda p: wcol(p, new.k, kind * KQV + kc * HG * DH + (h * 2 + c) * DH, DH),
                                     lambda p: xt[:, p, kc, ds(new.b * S, S)], kc == 0, kc == KC - 1)
                    last.then_inc(m["pj_full"], 1)

                def value(new, h, i):
                    pe.wait_ge(m["ex_r"], (new.n * 2 + h) * 4 + 3 + i)
                    for t in range(2):
                        for kc in range(KC):
                            last = three(pe, pj[i][:, t * D:(t + 1) * D],
                                         lambda p: xt[:, p, kc, ds(new.b * S + (i * 2 + t) * P, P)],
                                         lambda p: wcol(p, new.k, 2 * KQV + kc * HG * DH + h * 2 * DH, 2 * DH),
                                         t == 0 and kc == 0, t == 1 and kc == KC - 1)
                    last.then_inc(m["pj_full"], 1)

                def score(new, h):
                    i = new.n * 2 + h
                    if h:
                        pe.wait_ge(m["skrhi"], new.n * 2 + 2)
                    elif later(new):
                        pe.wait_ge(m["dot_r"], new.n * 4)
                    pe.wait_ge(m["lo_r"], i * 4 + 4)
                    for c in range(2):
                        for t in range(TPB):
                            for odd in range(2):
                                rows = slice(odd * SEG, odd * SEG + SEG)
                                s0 = (2 * t + odd) * SEG
                                col = (c * TPB + t) * SEG
                                last = three(pe, tr[0][rows, col:col + SEG],
                                             lambda p: qs[:, p, c, s0:s0 + SEG],
                                             lambda p: ks[:, p, c, s0:s0 + SEG],
                                             c == 0 and t == 0, c == 1 and t == TPB - 1)
                    last.then_inc(m["s_full"], 1)

                def key_turn(new, h):
                    i = new.n * 2 + h
                    pe.wait_ge(m["sglo"], i * 4 + 4)
                    for part in range(2):
                        if part == 0:
                            pe.wait_ge(m["sm_r"] if h == 0 else m["pthi"], new.n * 2 + 1)
                        elif h:
                            pe.wait_ge(m["ptlo"], new.n * 2 + 1)
                        elif later(new):
                            pe.wait_ge(m["att_r"], new.n * 4 - 3)
                        for c in range(2):
                            for t in range(TPB):
                                q = (c * TPB + t) * P
                                pe.transpose(tr16[part][:, q:q + P],
                                             sg[:, new.par, part, h * 2 + c, t, 2:4, :].rearrange("p a s -> p (a s)"),
                                             ident[:])
                                last = pe.transpose(tr16[part][0:SEG, q:q + P],
                                                    sg[:, new.par, part, h * 2 + c, t, 0, :], ident[:])
                        last.then_inc(m["skr_full"], 1)

                def prob_turn(new, h):
                    i = new.n * 2 + h
                    for part, ready in enumerate(("phi", "plo")):
                        pe.wait_ge(m[ready], i + 1)
                        if h == 0 and part == 0:
                            pe.wait_ge(m["skrhi"], new.n * 2 + 1)
                        elif later(new):
                            if part == 0:
                                pe.wait_ge(m["y_out"], new.n)
                            else:
                                pe.wait_ge(m["att_r"], new.n * 4 - 2 + 2 * h)
                        else:
                            pe.wait_ge(m["dot_r" if h else "skrlo"], 2 if h else 1)
                        pe.transpose(tr16[part][:, 0:P], ps[:, part, 0:2, :].rearrange("p a s -> p (a s)"), ident[:])
                        for ct in range(1, 2 * TPB):
                            last = pe.transpose(tr16[part][0:SEG, ct * P:(ct + 1) * P], ps[:, part, ct, :], ident[:])
                        last.then_inc(m["pt_full"], 1)

                def dot(new, h):
                    i = new.n * 2 + h
                    pe.wait_ge(m["pthi"], i + 1)
                    pe.wait_ge(m["ptlo"], i + 1)
                    pe.wait_ge(m["vlo"], i * 2 + 2)
                    for half in range(2):
                        if h == 0 and half == 0:
                            pe.wait_ge(m["sm_r"], new.n * 2 + 2)
                        elif h == 0 and later(new):
                            pe.wait_ge(m["att_r"], new.n * 4 - 1)
                        elif h == 0:
                            pe.wait_ge(m["skrlo"], 2)
                        for t in range(2):
                            for c in range(2):
                                cols = slice((h * 2 + c) * DH, (h * 2 + c + 1) * DH)
                                last = three(pe, tr[half][:, (t * 2 + c) * DH:(t * 2 + c + 1) * DH],
                                             lambda p: ptb[:, p, c, half * 2 + t, :],
                                             lambda p: vs[:, p, half * 2 + t, cols],
                                             t == 0 and c == 0, t == 1 and c == 1)
                        last.then_inc(m["dot_full"], 1)

                def retrieve(u, j):
                    t, odd = j // 2, j % 2
                    if j == 0:
                        pe.wait_ge(m["sglo"], u.n * 8 + 8)
                        if later(u):
                            pe.wait_ge(m["t_r"], u.n * NSEG)
                        for c in range(HG):
                            pe.matmul(mem[:, c, 0:DH + 1], ident[:], ms0[:, 0, 0:DH + 1], start=c % 2 == 0, stop=False,
                                      skip_group_check=True)
                    else:
                        pe.wait_ge(m["mlo"], u.n * 7 + j)
                    for c in range(HG):
                        last = three(pe, num[:, c, 0:DH + 1],
                                     lambda p: sg[:, u.par, p, c, t, 2 * odd:2 * odd + 2, :].rearrange("p a s -> p (a s)"),
                                     lambda p: ms0[:, p, 0:DH + 1] if j == 0 else ms[:, j % 2, p, c, 0:DH + 1],
                                     c % 2 == 0, c % 2 == 1)
                    last.then_inc(m["num_full"], 1)

                def update(u, j):
                    t, odd = j // 2, j % 2
                    if j == 0:
                        pe.wait_ge(m["skrhi"], u.n * 2 + 2)
                        pe.wait_ge(m["skrlo"], u.n * 2 + 2)
                    pe.wait_ge(m["dlo"], u.n * 7 + j + 1)
                    for c in range(HG):
                        last = three(pe, mem[:, c, 0:DH + 1], lambda p: skr[:, u.par, p, c, t, :],
                                     lambda p: dd[:, odd, p, c, 0:DH + 1])
                    last.then_inc(m["mem_full"], 1)

                def split(u, j):
                    pass

                def att_turn(u, t):
                    n = u.n + 1
                    pe.wait_ge(m["alo"], u.n * TPB + t + 1)
                    if t == 0:
                        pe.wait_ge(m["dot_r"], u.n * 4 + 4)
                    elif t < 3:
                        pe.wait_ge(m["skrlo"], n * 2 + t)
                    else:
                        pe.wait_ge(m["dot_r"], n * 4 + 2)
                    for part in range(2):
                        for c in range(HG):
                            q = (part * HG + c) * P
                            last = pe.transpose(tr16[1][:, q:q + P], ats[:, part, c * DH:(c + 1) * DH], ident[:])
                    last.then_inc(m["att_full"], 1)

                def output(u, part):
                    if part == 0:
                        pe.wait_ge(m["att_r"], u.n * TPB + TPB)
                        pe.wait_ge(m["dot_r"], u.n * 4 + 6)
                    for r in range(part * 8, part * 8 + 8):
                        last = three(pe, tr[0][:, 0:D], lambda p: att[:, p, r, :],
                                     lambda p: wo[:, p, r * D:(r + 1) * D], r == 0, r == ROWS16 - 1)
                    if part:
                        last.then_inc(m["y_full"], 1)

                pe.wait_ge(m["init"], 9)
                pe.wait_ge(m["wo_lo"], 4)
                units(pe, dict(project=project, value=value, score=score, key_turn=key_turn, prob_turn=prob_turn,
                               dot=dot, att_turn=att_turn, output=output), retrieve, update, split)

            @block.scalar
            def _(act):
                act.wait_ge(m["const_in"], 32)
                act.activation(beta[:], beta[:], ACT.Sigmoid).then_inc(m["beta_r"], 1)
                act.preload_act_table(ACT.Exp)
                act.wait_ge(m["w0_in"], 16)
                for i in range(3):
                    act.activation(w[:, 0, 0, i * KQV:(i + 1) * KQV],
                                   v32[:].rearrange("p a t e -> p (a t e)")[:, i * KQV:(i + 1) * KQV], ACT.Copy,
                                   scale=WSCALE).then_inc(m["w0_hi"], 1)
                act.wait_ge(m["wo_in"], 16)
                for i in range(4):
                    act.activation(wo[:, 0, i * 1024:(i + 1) * 1024],
                                   at[:].rearrange("p a t e -> p (a t e)")[:, i * 1024:(i + 1) * 1024], ACT.Copy,
                                   scale=WSCALE).then_inc(m["wo_hi"], 1)

                def split(new, h, ci):
                    c, dst = ci % 2, (qs, ks)[ci // 2]
                    i = new.n * 2 + h
                    act.wait_ge(m["pj_full"], i * 6 + ci + 1)
                    if later(new) or h or ci >= 2:
                        act.wait_ge(m["sglo"], i * 4 + ci - 1)
                    if ci == 0 and (later(new) or h):
                        act.wait_ge(m["s_full"], i)
                    act.activation(x32[:, c, :], pj[c][:], ACT.Copy, scale=1 / WSCALE).then_inc(m["x32_r"], 1)
                    act.activation(dst[:, 0, c, :], pj[c][:], ACT.Copy, scale=1 / WSCALE).then_inc(m["hi_r"], 1)
                    act.activation(ee[:, c, :], pj[c][:], ACT.Exp, scale=1 / WSCALE).then_inc(m["ex_r"], 1)

                def sigma_hi(new, h, ci):
                    c, to = ci % 2, (queries, keys)[ci // 2]
                    act.wait_ge(m["sg_r"], (new.n * 2 + h) * 4 + ci + 1)
                    act.activation(to(new.par, 0, h * 2 + c), ee[:, c, :].rearrange("p (t o s) -> p t o s", t=TPB, o=2),
                                   ACT.Copy).then_inc(m["sghi"], 1)

                def value_out(new, h, i):
                    cols = slice(h * 2 * DH, (h + 1) * 2 * DH)
                    src = pj[i][:].rearrange("p (t e) -> p t e", t=2)
                    act.wait_ge(m["pj_full"], (new.n * 2 + h) * 6 + 5 + i)
                    act.activation(vs[:, 0, i * 2:i * 2 + 2, cols], src, ACT.Copy, scale=1 / WSCALE)
                    act.activation(v32[:, new.par, i * 2:i * 2 + 2, cols], src, ACT.Copy,
                                   scale=1 / WSCALE).then_inc(m["v_r"], 1)

                def key_hi(new, h):
                    act.wait_ge(m["skr_full"], (new.n * 2 + h) * 2 + 1)
                    act.activation(skr[:, new.par, 0, h * 2:h * 2 + 2].rearrange("p c t d -> p (c t d)"), tr16[0],
                                   ACT.Copy).then_inc(m["skrhi"], 1)

                def exponent(new, h):
                    act.wait_ge(m["sd_r"], new.n * 2 + h + 1)
                    act.activation(sm[:], sm[:], ACT.Exp, scale=float(DH) ** -0.5).then_inc(m["pex_r"], 1)

                def prob_hi(new, h):
                    act.wait_ge(m["pn_r"], new.n * 2 + h + 1)
                    act.activation(ps[:, 0], sm[:], ACT.Copy).then_inc(m["phi"], 1)

                def pt_hi(new, h):
                    act.wait_ge(m["pt_full"], (new.n * 2 + h) * 2 + 1)
                    for odd in range(2):
                        kr, qr = HALF[odd]
                        last = act.activation(ptb[kr, 0, :, :, qr], probs_t(0, odd), ACT.Copy)
                    last.then_inc(m["pthi"], 1)

                def retrieve(u, j):
                    if j == NSEG - 1:
                        return
                    kr, odd = HALF[j % 2][0], j % 2
                    act.wait_ge(m["d_r"], u.n * 7 + j + 1)
                    act.activation(dd[kr, odd, 0, :, 0:DH], tq[kr, odd], ACT.Copy).then_inc(m["dhi"], 1)

                def update(u, j):
                    pass

                def split_mem(u, j):
                    act.wait_ge(m["mem_full"], u.n * 7 + j + 1)
                    act.activation(ms[:, (j + 1) % 2, 0, :, 0:DH + 1], mem[:, :, 0:DH + 1],
                                   ACT.Copy).then_inc(m["mhi"], 1)

                def att_hi(u, t):
                    act.wait_ge(m["at_r"], u.n * TPB + t + 1)
                    act.activation(ats[:, 0], at[:, u.par, t], ACT.Copy).then_inc(m["ahi"], 1)

                def att_out(u, t):
                    act.wait_ge(m["att_full"], u.n * TPB + t + 1)
                    for part in range(2):
                        src = tr16[1][:, part * 512:(part + 1) * 512].rearrange("p (c o a r) -> p c o a r", c=HG, o=2,
                                                                               r=ROWS16)
                        for blk in range(2):
                            m0 = (2 * t + 1 - blk) * 16
                            dst = att[:, part, :, m0:m0 + 16].rearrange("p r (c a) -> p c a r", c=HG)
                            last = act.activation(dst, src[:, :, blk], ACT.Copy)
                    last.then_inc(m["att_r"], 1)

                def output_out(u):
                    act.wait_ge(m["yst_free"], u.n + 1)
                    act.wait_ge(m["y_full"], u.n + 1)
                    act.activation(yst[:], tr[0][:, 0:D], ACT.Copy, scale=1 / WSCALE).then_inc(m["y_out"], 1)

                act.wait_ge(m["w0_lo"], 3)
                act.wait_ge(m["wo_lo"], 4)
                act.wait_ge(m["init"], 9)
                units(act, dict(split=split, sigma_hi=sigma_hi, value_out=value_out, key_hi=key_hi, exponent=exponent,
                                prob_hi=prob_hi, pt_hi=pt_hi, att_hi=att_hi, att_out=att_out, output_out=output_out),
                      retrieve, update, split_mem)

            @block.vector
            def _(v):
                v.memset(ptb[:], 0.0).then_inc(m["init"], 1)
                v.memset(dd[:], 0.0).then_inc(m["init"], 1)
                v.memset(ms0[:], 0.0).then_inc(m["init"], 1)
                v.memset(rd[:], 0.0).then_inc(m["init"], 1)
                v.memset(red[:], 0.0).then_inc(m["init"], 1)
                v.memset(am[:], 0.0).then_inc(m["init"], 1)
                v.wait_ge(m["init"], 6)
                v.memset(dd[0:SEG, 0, 0, :, DH:DH + 1], 1.0).then_inc(m["init"], 1)
                v.memset(dd[SEG:P, 1, 0, :, DH:DH + 1], 1.0).then_inc(m["init"], 1)
                v.memset(ms0[:, 0, DH:DH + 1], 1.0 / DH).then_inc(m["init"], 1)
                v.wait_ge(m["init"], 9)
                for i in range(3):
                    cols = slice(i * KQV, (i + 1) * KQV)
                    v.wait_ge(m["w0_hi"], i + 1)
                    v.scalar_tensor_tensor(w[:, 0, 1, cols], v32[:].rearrange("p a t e -> p (a t e)")[:, cols], WSCALE,
                                           w[:, 0, 0, cols], ALU.mult, ALU.subtract).then_inc(m["w0_lo"], 1)
                for i in range(4):
                    cols = slice(i * 1024, (i + 1) * 1024)
                    v.wait_ge(m["wo_hi"], i + 1)
                    v.scalar_tensor_tensor(wo[:, 1, cols], at[:].rearrange("p a t e -> p (a t e)")[:, cols], WSCALE,
                                           wo[:, 0, cols], ALU.mult, ALU.subtract).then_inc(m["wo_lo"], 1)

                def sigma(new, h, ci):
                    c = ci % 2
                    i = (new.n * 2 + h) * 4 + ci + 1
                    v.wait_ge(m["ex_r"], i)
                    v.tensor_scalar(ee[:, c, :], ee[:, c, :], 1.0, None, ALU.min).then_inc(m["e1_r"], 1)
                    v.wait_ge(m["e1_r"], i)
                    v.scalar_tensor_tensor(ee[:, c, :], x32[:, c, :], 0.0, ee[:, c, :], ALU.max,
                                           ALU.add).then_inc(m["sg_r"], 1)

                def key_lo(new, h):
                    v.wait_ge(m["skr_full"], (new.n * 2 + h) * 2 + 2)
                    v.tensor_copy(skr[:, new.par, 1, h * 2:h * 2 + 2].rearrange("p c t d -> p (c t d)"),
                                  tr16[1]).then_inc(m["skrlo"], 1)

                def row_max(new, h):
                    i = new.n * 2 + h
                    v.wait_ge(m["s_full"], i + 1)
                    if later(new) or h:
                        v.wait_ge(m["plo"], i)
                    v.tensor_tensor(sm[:], tr[0][:].rearrange("p (x s) -> p x s", s=SEG),
                                    bcast(mask[:].unsqueeze(1), P, 2 * TPB, SEG), ALU.add).then_inc(m["sm_r"], 1)
                    v.wait_ge(m["sm_r"], i + 1)
                    v.tensor_reduce(red[:, 0], sm[:], AX.X, ALU.max).then_inc(m["mx_r"], 1)

                def row_sum(new, h):
                    i = new.n * 2 + h
                    v.wait_ge(m["pex_r"], i + 1)
                    v.tensor_reduce(red[:, 1], sm[:], AX.X, ALU.add).then_inc(m["sum_r"], 1)
                    v.wait_ge(m["sum_r"], i + 1)
                    v.reciprocal(red[:, 1], red[:, 1]).then_inc(m["ri_r"], 1)

                def pt_lo(new, h):
                    v.wait_ge(m["pt_full"], (new.n * 2 + h) * 2 + 2)
                    for odd in range(2):
                        kr, qr = HALF[odd]
                        last = v.tensor_copy(ptb[kr, 1, :, :, qr], probs_t(1, odd))
                    last.then_inc(m["ptlo"], 1)

                def dot_out(new, h):
                    i = new.n * 2 + h
                    if h == 0:
                        v.tensor_scalar(omb[:], beta[:, ds(new.k * (HG * DH), HG * DH)], -1.0, 1.0, ALU.mult,
                                        ALU.add).then_inc(m["omb_r"], 1)
                        v.wait_ge(m["omb_r"], new.n + 1)
                    for half in range(2):
                        cols = slice(h * 2 * DH, (h + 1) * 2 * DH)
                        v.wait_ge(m["dot_full"], i * 2 + half + 1)
                        v.tensor_tensor(at[:, new.par, half * 2:half * 2 + 2, cols],
                                        tr[half][:].rearrange("p (t e) -> p t e", t=2),
                                        bcast(omb[:, cols].unsqueeze(1), P, 2, 2 * DH), ALU.mult).then_inc(m["dot_r"], 1)

                def retrieve(u, j):
                    t, odd = j // 2, j % 2
                    kr, qr = HALF[odd]
                    v.wait_ge(m["num_full"], u.n * NSEG + j + 1)
                    v.reciprocal(rd[:], num[:, :, DH]).then_inc(m["rd_r"], 1)
                    v.wait_ge(m["rd_r"], u.n * NSEG + j + 1)
                    v.tensor_tensor(tq[:, odd], num[:, :, 0:DH], bcast(rd[:].unsqueeze(2), P, HG, DH),
                                    ALU.mult).then_inc(m["t_r"], 1)
                    v.wait_ge(m["t_r"], u.n * NSEG + j + 1)
                    if j < NSEG - 1:
                        v.tensor_tensor(tq[kr, odd], v32[kr, u.par, t].rearrange("p (c e) -> p c e", c=HG), tq[kr, odd],
                                        ALU.subtract).then_inc(m["d_r"], 1)
                    if j == NSEG - 1:
                        beta_times(u, j)

                def beta_times(u, j):
                    t, odd = j // 2, j % 2
                    qr = HALF[odd][1]
                    v.tensor_tensor(am[qr, t % 2], tq[qr, odd].rearrange("p c e -> p (c e)"),
                                    beta[qr, ds(u.k * (HG * DH), HG * DH)], ALU.mult).then_inc(m["am_r"], 1)

                def update(u, j):
                    kr, odd = HALF[j % 2][0], j % 2
                    v.wait_ge(m["dhi"], u.n * 7 + j + 1)
                    v.tensor_tensor(dd[kr, odd, 1, :, 0:DH], tq[kr, odd], dd[kr, odd, 0, :, 0:DH],
                                    ALU.subtract).then_inc(m["dlo"], 1)
                    beta_times(u, j)

                def split(u, j):
                    v.wait_ge(m["mhi"], u.n * 7 + j + 1)
                    v.tensor_tensor(ms[:, (j + 1) % 2, 1, :, 0:DH + 1], mem[:, :, 0:DH + 1],
                                    ms[:, (j + 1) % 2, 0, :, 0:DH + 1], ALU.subtract).then_inc(m["mlo"], 1)

                v.wait_ge(m["const_in"], 32)
                v.wait_ge(m["beta_r"], 1)
                units(v, dict(sigma=sigma, key_lo=key_lo, row_max=row_max, row_sum=row_sum, pt_lo=pt_lo,
                              dot_out=dot_out), retrieve, update, split)


def attn1_phase(nc, w_dram, tabs, xt, y, ident):
    NG, HG = 4, 4
    HD = H1 * DH1
    with ExitStack() as ctx:
        ph = Phase(nc, ctx, "a1")
        w32 = ph.sb("w32", [P, KC, 4 * D])
        w = ph.sb("w", [P, 2, KC, 4 * D], F16)
        cos = ph.sb("cos", [P, TPB, DH1])
        sin = ph.sb("sin", [P, TPB, DH1])
        qdec = ph.sb("qdec", [P, H1])
        kdec = ph.sb("kdec", [P, H1])
        rc = ph.sb("rc", [P, NG])
        kvmask = ph.sb("kvmask", [P, HG * DH1])
        dmask = ph.sb("dmask", [P, HG, NG * P])
        rms_w = ph.sb("rms_w", [P, D])
        ra = ph.sb("ra", [P, 2 * H1, DH1])
        rb = ph.sb("rb", [P, 2 * H1, DH1])
        qks = ph.sb("qks", [P, 2 * H1, 2, DH1], F16)
        kx = ph.sb("kx", [P, H1, 2, DH1], F16)
        kd32 = ph.sb("kd32", [P, H1, DH1])
        kd = ph.sb("kd", [P, 2, 2, H1, 2, DH1], F16)
        vs = ph.sb("vs", [P, 2, 2, D], F16)
        qkt = ph.sb("qkt", [P, 2, 2, NG, P], F16)
        kxt = ph.sb("kxt", [P, 2, NG, P], F16)
        sd = ph.sb("sd", [P, HG, NG * P])
        sds = ph.sb("sds", [P, 2, HG, NG * P], F16)
        kv = ph.sb("kv", [P, NG, HG * DH1])
        kvu = ph.sb("kvu", [P, NG, HG * DH1])
        kvs = ph.sb("kvs", [P, 2, 2, NG, HG * DH1], F16)
        at = ph.sb("at", [P, HD])
        sq = ph.sb("sq", [P, HD])
        ss = ph.sb("ss", [P, 1])
        std = ph.sb("std", [P, 1])
        rstd = ph.sb("rstd", [P, 1])
        ats = ph.sb("ats", [P, 2, HD], F16)
        att = ph.sb("att", [P, 2, KC, P], F16)
        qkp = ph.ps("qkp", [P, 2 * D])
        vyp = ph.ps("vyp", [P, 2 * D])
        tqk = ph.ps("tqk", [P, 2, NG, P], F16)
        tx = ph.ps("tx", [P, 2, NG, P], F16)
        sp_ = [ph.ps(f"sc{i}", [P, NG * P]) for i in range(HG)]
        op, upd = sp_[0], sp_[1]

        names = ("in_ w_hi w_lo init qk_full v_full a_rot a_rb r_ready qkhi qklo kxr kd_ready kdhi kdlo vhi vlo"
                 " t_full tx_full qkt_r kxt_r sc_full sd_r sdhi sdlo out_full upd_full sc_free kvu_r kv_r"
                 " kvhi kvlo kv_reset ra_r at_r ss_r ms_r std_r rstd_r an_r anhi anlo att_full atthi attlo"
                 " y_full y_out dvo").split()
        m = {n: ph.sem(n) for n in names}

        def three(pe, out, wa, xa, start, stop):
            for n, (i, j) in enumerate(((0, 0), (0, 1), (1, 0))):
                last = pe.matmul(out, wa(i), xa(j), start=start and n == 0, stop=stop and n == 2,
                                 skip_group_check=True)
            return last

        def tiles(eng, stage_a, stage_b, reset=None):
            stage_a(0, 0, 0, 0)
            with eng.Fori(0, B) as b:
                if reset is not None:
                    reset(b)
                with eng.Fori(0, TPB // 2) as k:
                    for par in range(2):
                        t = b * TPB + k * 2 + par
                        n = t + 1
                        stage_b(b, t, par, lambda: stage_a(n, n % TILES, n % TPB, 1 - par))

        with nc.Block() as block:
            @block.sync
            def _(sp):
                sp.dma_start(w32[:], w_dram).then_inc(m["in_"], 16)
                for n, dst in (("cos", cos), ("sin", sin), ("qdec", qdec), ("kdec", kdec), ("rc", rc),
                               ("kvmask", kvmask), ("dmask", dmask)):
                    sp.dma_start(dst[:], tabs[n]).then_inc(m["in_"], 16)
                sp.dma_start(rms_w[:], tabs["rms_w"].to_broadcast([P, D])).then_inc(m["in_"], 16)
            n_in = 16 * 9

            @block.tensor
            def _(pe):
                def stage_a1(n, tile):
                    for kc in range(KC):
                        last = three(pe, qkp[:], lambda i: xt[:, i, kc, ds(tile * P, P)],
                                     lambda j: w[:, j, kc, 0:2 * D], kc == 0, kc == KC - 1)
                    last.then_inc(m["qk_full"], 1)
                    for kc in range(KC):
                        last = three(pe, vyp[:, 0:D], lambda i: xt[:, i, kc, ds(tile * P, P)],
                                     lambda j: w[:, j, kc, 2 * D:3 * D], kc == 0, kc == KC - 1)
                    last.then_inc(m["v_full"], 1)

                def stage_a2(n):
                    pe.wait_ge(m["qkhi"], n + 1)
                    pe.wait_ge(m["qklo"], n + 1)
                    flat = qks[:].rearrange("p h s d -> p (h s d)")
                    for c in range(2 * NG):
                        last = pe.transpose(tqk[:, c // NG, c % NG, :], flat[:, c * P:(c + 1) * P], ident[:])
                    last.then_inc(m["t_full"], 1)
                    pe.wait_ge(m["kxr"], n * 2 + 2)
                    flat = kx[:].rearrange("p h s d -> p (h s d)")
                    for c in range(NG):
                        last = pe.transpose(tx[:, 0, c, :], flat[:, c * P:(c + 1) * P], ident[:])
                    last.then_inc(m["tx_full"], 1)

                def a(n, tile, pos, par):
                    stage_a1(n, tile)
                    stage_a2(n)

                def b(batch, t, par, nxt):
                    n = t + 1
                    pe.wait_ge(m["ra_r"], t * 3 + 3)
                    pe.wait_ge(m["vlo"], n)
                    pe.wait_ge(m["y_out"], n)
                    stage_a1(n, n % TILES)
                    pe.wait_ge(m["qkt_r"], n)
                    pe.wait_ge(m["kxt_r"], n)
                    for g in range(NG):
                        for i in range(HG):
                            rows = slice(32 * i, 32 * i + 32)
                            pe.matmul(sp_[i][:, g * P:(g + 1) * P], qkt[rows, par, 1, g, :],
                                      qkt[rows, par, 0, g, :], start=g == 0, stop=False,
                                      skip_group_check=True)
                            last = pe.matmul(sp_[i][:, g * P:(g + 1) * P], kxt[rows, par, g, :],
                                             qkt[rows, par, 0, g, :], start=False, stop=g == NG - 1,
                                             skip_group_check=True)
                            if g == NG - 1:
                                last.then_inc(m["sc_full"], 1)
                    stage_a2(n)
                    pe.wait_ge(m["kdhi"], n)
                    pe.wait_ge(m["kdlo"], n)
                    pe.wait_ge(m["sd_r"], t * HG + 2)
                    for g in range(NG):
                        last = three(pe, upd[:, g * HG * DH1:(g + 1) * HG * DH1],
                                     lambda i: kd[:, par, i, g * HG:(g + 1) * HG].rearrange(
                                         "p h s d -> p (h s d)"),
                                     lambda j: vs[:, par, j, g * HG * DH1:(g + 1) * HG * DH1],
                                     g == 0, g == NG - 1)
                    last.then_inc(m["upd_full"], 1)
                    pe.wait_ge(m["kvlo"], n + batch)
                    for g in range(NG):
                        for j in range(2):
                            pe.matmul(op[:, HD + g * 64:HD + (g + 1) * 64], qkt[:, par, 0, g, :],
                                      kvs[:, par, j, g, :], start=g == 0 and j == 0, stop=False,
                                      skip_group_check=True)
                    for i in range(HG):
                        pe.wait_ge(m["sdhi"], t * HG + i + 1)
                        pe.wait_ge(m["sdlo"], t * HG + i + 1)
                        for g in range(NG):
                            h = HG * g + i
                            last = three(pe, op[:, h * DH1:(h + 1) * DH1],
                                         lambda j: sds[:, j, i, g * P:(g + 1) * P],
                                         lambda j: vs[:, par, j, h * DH1:(h + 1) * DH1], False, i == HG - 1)
                    last.then_inc(m["out_full"], 1)
                    pe.wait_ge(m["anhi"], n)
                    pe.wait_ge(m["anlo"], n)
                    pe.wait_ge(m["kxt_r"], n + 1)
                    for j in range(2):
                        for kc in range(KC):
                            last = pe.transpose(tx[:, 1, j * KC + kc, :], ats[:, j, kc * P:(kc + 1) * P], ident[:])
                    last.then_inc(m["att_full"], 1)
                    pe.wait_ge(m["atthi"], n)
                    pe.wait_ge(m["vlo"], n + 1)
                    for kc in range(KC):
                        last = three(pe, vyp[:, D:2 * D], lambda i: att[:, i, kc, :],
                                     lambda j: w[:, j, kc, 3 * D:4 * D], kc == 0, kc == KC - 1)
                    last.then_inc(m["y_full"], 1)

                pe.wait_ge(m["w_lo"], 1)
                tiles(pe, a, b)

            @block.scalar
            def _(act):
                act.preload_act_table(ACT.Sqrt)
                act.wait_ge(m["in_"], n_in)
                act.activation(w[:, 0], w32[:], ACT.Copy, scale=WSCALE).then_inc(m["w_hi"], 1)

                def a1(n, par):
                    act.wait_ge(m["v_full"], n + 1)
                    act.activation(vs[:, par, 0, :], vyp[:, 0:D], ACT.Copy, scale=1 / WSCALE).then_inc(m["vhi"], 1)
                    act.wait_ge(m["r_ready"], n + 1)
                    act.activation(qks[:, :, 0, :], ra[:], ACT.Copy).then_inc(m["qkhi"], 1)

                def a2(n, par):
                    act.wait_ge(m["kd_ready"], n + 1)
                    act.activation(kd[:, par, 0], bcast(kd32[:].unsqueeze(2), P, H1, 2, DH1),
                                   ACT.Copy).then_inc(m["kdhi"], 1)
                    act.wait_ge(m["t_full"], n + 1)
                    act.activation(qkt[:, par], tqk[:], ACT.Copy).then_inc(m["qkt_r"], 1)

                def a(n, tile, pos, par):
                    a1(n, par)
                    a2(n, par)

                def b(batch, t, par, nxt):
                    n = t + 1
                    a1(n, 1 - par)
                    for i in range(HG):
                        act.wait_ge(m["sd_r"], t * HG + i + 1)
                        act.activation(sds[:, 0, i, :], sd[:, i, :], ACT.Copy).then_inc(m["sdhi"], 1)
                    a2(n, 1 - par)
                    act.wait_ge(m["kv_r"], n)
                    act.activation(kvs[:, 1 - par, 0], kv[:], ACT.Copy).then_inc(m["kvhi"], 1)
                    act.wait_ge(m["at_r"], n)
                    act.activation(sq[:], at[:], ACT.Square, accum_out=ss[:]).then_inc(m["ss_r"], 1)
                    act.wait_ge(m["ms_r"], n)
                    act.activation(std[:], ss[:], ACT.Sqrt).then_inc(m["std_r"], 1)
                    act.wait_ge(m["an_r"], n)
                    act.activation(ats[:, 0, :], at[:], ACT.Copy).then_inc(m["anhi"], 1)
                    act.wait_ge(m["att_full"], n)
                    act.activation(att[:].rearrange("p a k c -> p (a k) c"), tx[:, 1], ACT.Copy).then_inc(m["atthi"], 1)
                    act.wait_ge(m["y_full"], n)
                    act.activation(y[:, ds(t, 1), :], vyp[:, D:2 * D], ACT.Copy,
                                   scale=1 / WSCALE).then_inc(m["y_out"], 1)

                tiles(act, a, b)

            @block.gpsimd
            def _(pool):
                def a(n, tile, pos, par):
                    pool.wait_ge(m["ra_r"], n * 3 + 3)
                    pool.tensor_tensor(ra[:], ra[:], rb[:], ALU.add).then_inc(m["r_ready"], 1)
                    pool.wait_ge(m["r_ready"], n + 1)
                    pool.tensor_tensor(kd32[:], ra[:, H1:2 * H1, :], bcast(kdec[:].unsqueeze(2), P, H1, DH1),
                                       ALU.mult).then_inc(m["kd_ready"], 1)
                    pool.wait_ge(m["qklo"], n + 1)
                    pool.tensor_tensor(kx[:, :, 0, :], ra[:, H1:2 * H1, :], qks[:, H1:2 * H1, 0, :],
                                       ALU.subtract).then_inc(m["kxr"], 1)
                    pool.tensor_copy(kx[:, :, 1, :], qks[:, H1:2 * H1, 0, :]).then_inc(m["kxr"], 1)

                def b(batch, t, par, nxt):
                    nxt()
                    for i in range(HG):
                        pool.wait_ge(m["sdhi"], t * HG + i + 1)
                        pool.tensor_tensor(sds[:, 1, i, :], sd[:, i, :], sds[:, 0, i, :],
                                           ALU.subtract).then_inc(m["sdlo"], 1)

                pool.wait_ge(m["in_"], n_in)
                tiles(pool, a, b)

            @block.vector
            def _(v):
                done = [0]
                v.wait_ge(m["w_hi"], 1)
                v.scalar_tensor_tensor(w[:, 1].rearrange("p k c -> p (k c)"),
                                       w32[:].rearrange("p k c -> p (k c)"), WSCALE,
                                       w[:, 0].rearrange("p k c -> p (k c)"),
                                       ALU.mult, ALU.subtract).then_inc(m["w_lo"], 1)
                v.sem_inc(m["y_out"], 1)

                def a1(n, pos):
                    v.wait_ge(m["qk_full"], n + 1)
                    q = qkp[:].rearrange("p (h d) -> p h d", d=DH1)
                    half = DH1 // 2

                    def tab(tb, lo, hi):
                        return tb[:, ds(pos, 1), lo:hi].to_broadcast([P, 2 * H1, hi - lo])
                    v.tensor_tensor(ra[:], q, tab(cos, 0, DH1), ALU.mult).then_inc(m["ra_r"], 1)
                    v.tensor_tensor(rb[:, :, 0:half], q[:, :, half:], tab(sin, 0, half),
                                    ALU.mult).then_inc(m["ra_r"], 1)
                    v.tensor_tensor(rb[:, :, half:], q[:, :, 0:half], tab(sin, half, DH1),
                                    ALU.mult).then_inc(m["ra_r"], 1)

                def a2(n, par):
                    v.wait_ge(m["vhi"], n + 1)
                    v.scalar_tensor_tensor(vs[:, par, 1, :], vyp[:, 0:D], 1 / WSCALE, vs[:, par, 0, :],
                                           ALU.mult, ALU.subtract).then_inc(m["vlo"], 1)
                    v.wait_ge(m["qkhi"], n + 1)
                    v.tensor_tensor(qks[:, :, 1, :], ra[:], qks[:, :, 0, :], ALU.subtract).then_inc(m["qklo"], 1)
                    v.wait_ge(m["kdhi"], n + 1)
                    for rep in range(2):
                        ins = v.tensor_tensor(kd[:, par, 1, :, rep], kd32[:], kd[:, par, 0, :, rep], ALU.subtract)
                    ins.then_inc(m["kdlo"], 1)

                def a3(n, par):
                    v.wait_ge(m["tx_full"], n + 1)
                    v.tensor_copy(kxt[:, par], tx[:, 0]).then_inc(m["kxt_r"], 1)

                def a(n, tile, pos, par):
                    a1(n, pos)
                    a2(n, par)
                    a3(n, par)

                def reset(b):
                    v.memset(kv[:], 0.0).then_inc(m["kv_reset"], 1)
                    v.memset(kvs[:, 0, 0], 0.0).then_inc(m["kv_reset"], 1)
                    v.wait_ge(m["kv_reset"], b * 2 + 2)
                    v.memset(kvs[:, 0, 1], 0.0).then_inc(m["kvlo"], 1)

                def b(batch, t, par, nxt):
                    n = t + 1
                    a1(n, n % TPB)
                    for i in range(HG):
                        v.wait_ge(m["sc_full"], t * HG + i + 1)
                        v.tensor_tensor(sd[:, i, :], sp_[i][:], dmask[:, i, :], ALU.mult).then_inc(m["sd_r"], 1)
                    a2(n, 1 - par)
                    a3(n, 1 - par)
                    v.wait_ge(m["upd_full"], n)
                    v.tensor_tensor(kvu[:], upd[:, 0:HD].rearrange("p (g e) -> p g e", g=NG),
                                    bcast(kvmask[:].unsqueeze(1), P, NG, HG * DH1), ALU.mult).then_inc(m["dvo"], 1)
                    v.tensor_tensor(kv[:], kv[:], bcast(rc[:].unsqueeze(2), P, NG, HG * DH1),
                                    ALU.mult).then_inc(m["dvo"], 1)
                    v.wait_ge(m["dvo"], t * 4 + 2)
                    v.tensor_tensor(kv[:], kv[:], kvu[:], ALU.add).then_inc(m["kv_r"], 1)
                    v.wait_ge(m["out_full"], n)
                    v.tensor_tensor(at[:].rearrange("p (h e) -> p h e", h=H1),
                                    op[:, HD:].rearrange("p (h e) -> p h e", h=H1),
                                    bcast(qdec[:].unsqueeze(2), P, H1, DH1), ALU.mult).then_inc(m["dvo"], 1)
                    v.wait_ge(m["dvo"], t * 4 + 3)
                    v.tensor_tensor(at[:], at[:], op[:, 0:HD], ALU.add).then_inc(m["at_r"], 1)
                    v.wait_ge(m["kvhi"], n)
                    v.tensor_tensor(kvs[:, 1 - par, 1], kv[:], kvs[:, 1 - par, 0],
                                    ALU.subtract).then_inc(m["kvlo"], 1)
                    v.wait_ge(m["ss_r"], n)
                    v.tensor_scalar(ss[:], ss[:], 1.0 / HD, LN_EPS, ALU.mult, ALU.add).then_inc(m["ms_r"], 1)
                    v.wait_ge(m["std_r"], n)
                    v.reciprocal(rstd[:], std[:]).then_inc(m["dvo"], 1)
                    v.wait_ge(m["dvo"], t * 4 + 4)
                    v.scalar_tensor_tensor(at[:], at[:], rstd[:], rms_w[:], ALU.mult,
                                           ALU.mult).then_inc(m["an_r"], 1)
                    v.wait_ge(m["anhi"], n)
                    v.tensor_tensor(ats[:, 1, :], at[:], ats[:, 0, :], ALU.subtract).then_inc(m["anlo"], 1)

                tiles(v, a, b, reset)


def _pack_ffn(w1, w3, w2, ht_n):
    import numpy as np
    rows = ht_n * P
    out = np.zeros((ht_n, P, 2 * KC * P + D), np.float32)
    for n, w in enumerate((w1, w3)):
        full = np.zeros((rows, D), np.float32)
        full[:w.shape[0]] = w
        out[:, :, n * D:(n + 1) * D] = full.reshape(ht_n, P, KC, P).transpose(0, 3, 2, 1).reshape(ht_n, P, D)
    full = np.zeros((rows, D), np.float32)
    full[:w2.shape[0]] = w2
    out[:, :, 2 * D:] = full.reshape(ht_n, P, D)
    return out


def _by_kc(w):
    return w.reshape(KC, P, -1).transpose(1, 0, 2)


def _pack_attn0(wq, wk, wv):
    import numpy as np
    parts = [w.reshape(KC, P, GROUPS, HG * DH).transpose(2, 1, 0, 3).reshape(GROUPS, P, -1) for w in (wq, wk, wv)]
    return np.concatenate(parts, axis=2)


def _rows(v, ht_n):
    import numpy as np
    out = np.zeros(ht_n * P, np.float32)
    out[:v.shape[0]] = v
    return np.ascontiguousarray(out.reshape(ht_n, P).T)


def _expand():
    import numpy as np
    e = np.zeros((E0 + 1, HT0 * P), np.float16)
    for n in range(E0 + 1):
        e[n, n * HID0:(n + 1) * HID0] = 1
    return e


def _tables():
    import numpy as np
    f = np.float32
    quarter = DH1 // 4
    freq = np.concatenate([(f(1) / f(1024)) ** np.linspace(0, 1, quarter, dtype=f), np.zeros(quarter, f)])
    theta = (np.arange(S, dtype=f)[:, None] * freq[None, :]).astype(f)
    cos, sin = np.cos(theta), np.sin(theta)
    by_tile = lambda a: (a / WSCALE).reshape(TPB, P, DH1).transpose(1, 0, 2).astype(f)
    slopes = (2.0 ** -0.5) ** np.arange(1, H1 + 1)
    r = np.exp(-slopes)
    i = np.arange(CHUNK)
    head = np.arange(P)[:, None] // 32 + 4 * np.arange(4)[None, :]
    diff = i[None, :] - i[:, None]
    dm = np.where(diff[:, None] >= 0, r[None, :, None] ** np.maximum(diff, 0)[:, None], 0)
    return {
        "cos": by_tile(np.concatenate([cos, cos], 1)), "sin": by_tile(np.concatenate([sin, -sin], 1)),
        "qdec": (r[None] ** (i[:, None] + 1.0)).astype(f), "kdec": (r[None] ** (CHUNK - 1.0 - i[:, None])).astype(f),
        "rc": (r[head] ** CHUNK).astype(f),
        "kvmask": (np.arange(P)[:, None] // 32 == np.arange(64)[None, :] // DH1).astype(f),
        "dmask": dm.reshape(P, 4, 4, P).transpose(0, 2, 1, 3).reshape(P, 4, 4 * P).astype(f),
    }


def prepare(inputs):
    import numpy as np
    i = {k: np.asarray(v) for k, v in inputs.items()}
    a = {"x": i["L0_attn_x"]}
    a["eye"] = np.eye(P, dtype=np.float16)
    a["w_attn0"] = _pack_attn0(i["L0_attn_Wq"], i["L0_attn_Wk"], i["L0_attn_Wv"])
    a["wo_attn0"] = i["L0_attn_Wo"].reshape(H0, DH, D).transpose(1, 0, 2).reshape(P, H0 * D)
    a["betas"] = i["L0_attn_betas"].reshape(1, H0 * DH)
    flat = lambda w: w.reshape(-1, w.shape[-1])
    a["w_ffn0"] = _pack_ffn(np.concatenate([i["L0_ffn_sw1"], flat(i["L0_ffn_ew1"])]),
                            np.concatenate([i["L0_ffn_sw3"], flat(i["L0_ffn_ew3"])]),
                            np.concatenate([i["L0_ffn_sw2"].T, flat(i["L0_ffn_ew2"].transpose(0, 2, 1))]), HT0)
    a["wr"] = np.ascontiguousarray(_by_kc(i["L0_ffn_wr"].T))
    a["expand"] = _expand()
    a["w_ffn1"] = _pack_ffn(i["L1_ffn_gate_w"], i["L1_ffn_up_w"], i["L1_ffn_down_w"].T, HT1)
    a["gate_s"] = _rows(i["L1_ffn_gate_s"], HT1)
    a["up_s"] = _rows(i["L1_ffn_up_s"], HT1)
    a["down_s"] = i["L1_ffn_down_s"].reshape(1, D)
    a["w_attn1"] = np.concatenate([_by_kc(i["L1_attn_W" + n]) for n in "qkvo"], axis=2)
    a["mask"] = np.where(np.arange(SEG)[None] <= np.arange(P)[:, None] % SEG, 0, -1e30).astype(np.float32)
    a["rms_w"] = i["L1_attn_rms_w"].reshape(1, D)
    a.update(_tables())
    return {k: np.ascontiguousarray(v) for k, v in a.items()}


def network(nc, t, out):
    with ExitStack() as ctx:
        xt = ctx.enter_context(nc.sbuf_tensor("xt", [P, 2, KC, TOK], F16))
        ident = ctx.enter_context(nc.sbuf_tensor("ident", [P, P], F16))
        loaded = ctx.enter_context(nc.semaphore("ident_loaded"))
        with nc.Block() as block:
            @block.sync
            def _(sp):
                sp.dma_start(ident[:], t["eye"]).then_inc(loaded, 16)
                sp.wait_ge(loaded, 16)
        with ExitStack() as first:
            x = first.enter_context(nc.sbuf_tensor("x_first", [P, TILES, D], F32))
            norm_phase(nc, "n0", ident, x, None, xt, load_x=t["x"])
        y_dram = nc.dram_tensor("y_attn0", (B, S, D), F32, kind="Internal").ap()
        attn0_phase(nc, t["w_attn0"], t["wo_attn0"], t["betas"], t["mask"], xt, y_dram, ident)
        y = ctx.enter_context(nc.sbuf_tensor("y", [P, TILES, D], F32))
        x = ctx.enter_context(nc.sbuf_tensor("x_sb", [P, TILES, D], F32))
        norm_phase(nc, "n1", ident, x, y, xt, load_x=t["x"], load_y=y_dram)
        ffn_phase(nc, "f0", t["w_ffn0"], xt, y, HT0, ident, router=(t["wr"], t["expand"]))
        norm_phase(nc, "n2", ident, x, y, xt)
        attn1_phase(nc, t["w_attn1"], t, xt, y, ident)
        norm_phase(nc, "n3", ident, x, y, xt)
        ffn_phase(nc, "f1", t["w_ffn1"], xt, y, HT1, ident, scales=(t["gate_s"], t["up_s"], t["down_s"]))
        norm_phase(nc, "n4", ident, x, y, None, store=out)


def kernel(**inputs):
    import concourse.bacc as _bacc
    from concourse.bass_utils import run_bass_kernel_spmd as _run

    arrays = prepare(inputs)
    nc = _bacc.Bacc("TRN2", target_bir_lowering=False, num_devices=1)
    tensors = {name: nc.dram_tensor(name, a.shape, mybir.dt.from_np(a.dtype), kind="ExternalInput").ap()
               for name, a in arrays.items()}
    out = nc.dram_tensor("out", (B, S, D), F32, kind="ExternalOutput").ap()
    network(nc, tensors, out)
    r = _run(nc, [arrays], core_ids=[0])
    return r.results[0]["out"]
```

```python
from contextlib import ExitStack

import concourse.bass as bass
from concourse import mybir

ALU = mybir.AluOpType
ACT = mybir.ActivationFunctionType
AX = mybir.AxisListType
F32 = mybir.dt.float32
F16 = mybir.dt.float16
U32 = mybir.dt.uint32
ds = bass.ds

P = 128
B, S, D = 4, 512, 256
TOK = B * S
TILES = TOK // P
TPB = S // P
KC = D // P
WSCALE = 64.0
LN_EPS = 1e-5

H0, DH, SEG = 16, 128, 64
NSEG = S // SEG
HG = 4
GROUPS = H0 // HG
ROWS16 = H0
E0, HID0 = 8, D * 4 // 3
HT0 = -(-(E0 + 1) * HID0 // P)
INTER = 704
HT1 = -(-INTER // P)
H1, DH1, CHUNK = 16, 16, 128


class Phase:

    def __init__(self, nc, ctx, name):
        self.nc, self.ctx, self.name = nc, ctx, name
        self.sems = []
        ctx.callback(self.clear)

    def sb(self, name, shape, dt=F32):
        return self.ctx.enter_context(self.nc.sbuf_tensor(f"{self.name}_{name}", shape, dt))

    def ps(self, name, shape, dt=F32):
        return self.ctx.enter_context(self.nc.psum_tensor(f"{self.name}_{name}", shape, dt))

    def sem(self, name):
        self.sems.append(self.nc.alloc_semaphore(f"{self.name}_{name}"))
        return self.sems[-1]

    def clear(self):
        self.nc.clear_and_free_semaphores(self.sems)
        self.nc.all_engine_barrier()


def bcast(ap, *shape):
    return ap.to_broadcast(list(shape))


def norm_phase(nc, name, ident, x, y, xt, load_x=None, load_y=None, store=None):
    with ExitStack() as ctx:
        ph = Phase(nc, ctx, name)
        stats = ph.sb("stats", [P, 2, TILES, 6])
        mv = ph.sb("mv", [P, 2, TILES, 2])
        std = ph.sb("std", [P, 2, TILES])
        rstd = ph.sb("rstd", [P, 2, TILES])
        shift = ph.sb("shift", [P, 2, TILES])
        eps = ph.sb("eps", [P, 1])
        m = {n: ph.sem(n) for n in ("x_in x0_in y_in y0_in eps_r hi_ready lo_ready turned thi_out tlo_out xh_ready shifted"
                                    " x_done stored").split()}
        for k in "yx":
            for n in ("stats", "var", "std", "rstd", "shift"):
                m[n + k] = ph.sem(n + k)
        if store is None:
            xh = ph.sb("xh", [P, TPB, D])
            hi = ph.sb("hi", [P, TPB, D], F16)
            lo = ph.sb("lo", [P, TPB, D], F16)
            pt = [ph.ps(f"pt{i}", [P, KC, S], F16) for i in range(2)]
        kinds = ([0] if y is not None else []) + ([1] if store is None else [])

        Y_PARTS = ((0, TPB), (TPB, TILES))

        def tiles(a, b):
            return a[:, ds(b * TPB, TPB)]

        def batches(eng, body, ahead=1):
            for b in range(ahead):
                body(b, b)
            with eng.Fori(ahead, B) as b:
                body(b, ahead)

        with nc.Block() as block:
            @block.sync
            def _(sp):
                for b in range(B):
                    for dram, dst, sem in ((load_y, y, "y_in"), (load_x, x, "x_in")):
                        if dram is not None:
                            src = dram.rearrange("b (t p) d -> p b t d", p=P)
                            sp.dma_start(dst[:, b * TPB:(b + 1) * TPB, :],
                                         src[:, b]).then_inc(m[sem if b else sem.replace("_", "0_")], 16)
                if store is not None:
                    dst = store.rearrange("b (t p) d -> p b t d", p=P)
                    for b in range(B):
                        sp.wait_ge(m["x_done"], b * TPB + TPB)
                        sp.dma_start(dst[:, b], x[:, b * TPB:(b + 1) * TPB, :]).then_inc(m["stored"], 16)
                    sp.wait_ge(m["stored"], 16 * B)

            @block.vector
            def _(v):
                def y_statistics(part):
                    a, e = Y_PARTS[part]
                    for t in range(a, e):
                        last = v.bn_stats(stats[:, 0, t, :].unsqueeze(1), y[:, t:t + 1, :])
                    last.then_inc(m["statsy"], 1)
                    v.wait_ge(m["statsy"], part + 1)
                    for t in range(a, e):
                        last = v.bn_aggr(mv[:, 0, t, :], stats[:, 0, t, :])
                    last.then_inc(m["vary"], 1)

                def y_scale_shift(part):
                    a, e = Y_PARTS[part]
                    v.wait_ge(m["stdy"], part + 1)
                    v.reciprocal(rstd[:, 0, a:e], std[:, 0, a:e]).then_inc(m["rstdy"], 1)
                    v.wait_ge(m["rstdy"], part + 1)
                    v.scalar_tensor_tensor(shift[:, 0, a:e], mv[:, 0, a:e, 0], -1.0, rstd[:, 0, a:e],
                                           ALU.mult, ALU.mult).then_inc(m["shifty"], 1)

                def statistics(b):
                    for t in range(TPB):
                        last = v.bn_stats(stats[:, 1, t, :].unsqueeze(1), x[:, ds(b * TPB + t, 1), :])
                    last.then_inc(m["statsx"], 1)

                def variance():
                    for t in range(TPB):
                        last = v.bn_aggr(mv[:, 1, t, :], stats[:, 1, t, :])
                    last.then_inc(m["varx"], 1)

                def scale_shift(b):
                    v.wait_ge(m["stdx"], b + 1)
                    v.reciprocal(tiles(rstd[:, 1], b), tiles(std[:, 1], b)).then_inc(m["rstdx"], 1)
                    v.wait_ge(m["rstdx"], b + 1)
                    v.scalar_tensor_tensor(tiles(shift[:, 1], b), mv[:, 1, :TPB, 0], -1.0,
                                           tiles(rstd[:, 1], b), ALU.mult, ALU.mult).then_inc(m["shiftx"], 1)

                def low_out(b, kc):
                    v.wait_ge(m["turned"], b * 2 + 2)
                    v.tensor_copy(xt[:, 1, kc:kc + 1, ds(b * S, S)], pt[1][:, kc:kc + 1]).then_inc(m["tlo_out"], 1)

                def batch(b, before):
                    if y is not None:
                        v.wait_ge(m["shifted"], b + 1)
                        for t in range(TPB):
                            i = ds(b * TPB + t, 1)
                            v.scalar_tensor_tensor(x[:, i, :], y[:, i, :], rstd[:, 0, i], x[:, i, :], ALU.mult,
                                                   ALU.add).then_inc(m["x_done"], 1)
                        if store is None:
                            v.wait_ge(m["x_done"], b * TPB + TPB)
                    elif load_x is not None and before < 2:
                        v.wait_ge(m["x_in"] if before else m["x0_in"], 16 * (B - 1) if before else 16)
                    if store is None:
                        if before == 2:
                            low_out(b - 2, 0)
                        statistics(b)
                        v.wait_ge(m["statsx"], b + 1)
                        if before == 2:
                            low_out(b - 2, 1)
                        variance()
                        scale_shift(b)

                v.memset(eps[:], LN_EPS).then_inc(m["eps_r"], 1)
                if y is not None:
                    if load_y is not None:
                        v.wait_ge(m["y0_in"], 16)
                    y_statistics(0)
                    y_scale_shift(0)
                    if load_y is not None:
                        v.wait_ge(m["y_in"], 16 * (B - 1))
                    y_statistics(1)
                    y_scale_shift(1)
                batches(v, batch, 2)
                if store is None:
                    for b in (B - 2, B - 1):
                        for kc in range(KC):
                            low_out(b, kc)

            @block.scalar
            def _(act):
                def y_deviation(part):
                    a, e = Y_PARTS[part]
                    act.wait_ge(m["vary"], part + 1)
                    act.activation(std[:, 0, a:e], mv[:, 0, a:e, 1], ACT.Sqrt, bias=eps[:]).then_inc(m["stdy"], 1)

                def deviation(b):
                    act.wait_ge(m["varx"], b + 1)
                    act.activation(tiles(std[:, 1], b), mv[:, 1, :TPB, 1], ACT.Sqrt,
                                   bias=eps[:]).then_inc(m["stdx"], 1)

                def high_out(b):
                    act.wait_ge(m["turned"], b * 2 + 1)
                    act.activation(xt[:, 0, :, ds(b * S, S)], pt[0][:], ACT.Copy).then_inc(m["thi_out"], 1)

                def normalise(b, later):
                    act.wait_ge(m["shiftx"], b + 1)
                    if later:
                        act.wait_ge(m["lo_ready"], b)
                    for dst, done in ((xh, "xh_ready"), (hi, "hi_ready")):
                        for t in range(TPB):
                            i = ds(b * TPB + t, 1)
                            last = act.activation(dst[:, t:t + 1, :], x[:, i, :], ACT.Identity,
                                                  bias=shift[:, 1, i], scale=rstd[:, 1, i])
                        last.then_inc(m[done], 1)

                def batch(b, before):
                    if store is None:
                        if before == 2:
                            high_out(b - 2)
                        if before:
                            normalise(b - 1, before == 2)
                        deviation(b)

                act.preload_act_table(ACT.Sqrt)
                act.wait_ge(m["eps_r"], 1)
                if y is not None:
                    for part in range(len(Y_PARTS)):
                        y_deviation(part)
                batches(act, batch, 2)
                if store is None:
                    high_out(B - 2)
                    normalise(B - 1, True)
                    high_out(B - 1)

            @block.gpsimd
            def _(pool):
                def low(b, later):
                    pool.wait_ge(m["hi_ready"], b + 1)
                    if later:
                        pool.wait_ge(m["turned"], b * 2)
                    pool.tensor_tensor(lo[:], xh[:], hi[:], ALU.subtract).then_inc(m["lo_ready"], 1)

                def shifted(b, before):
                    if before < 2:
                        pool.wait_ge(m["shifty"], before + 1)
                        if load_x is not None:
                            pool.wait_ge(m["x_in"] if before else m["x0_in"], 16 * (B - 1) if before else 16)
                    pool.tensor_tensor(tiles(x, b), tiles(x, b), bcast(tiles(shift[:, 0], b).unsqueeze(2), P, TPB, D),
                                       ALU.add).then_inc(m["shifted"], 1)

                if y is not None:
                    batches(pool, shifted, 2)
                if store is None:
                    batches(pool, low)

            if store is None:
                @block.tensor
                def _(pe):
                    def batch(b, later):
                        for part, (src, ready, out) in enumerate(((hi, "hi_ready", "thi_out"),
                                                                  (lo, "lo_ready", "tlo_out"))):
                            pe.wait_ge(m[ready], b + 1)
                            if later:
                                pe.wait_ge(m[out], b * (part + 1))
                            for kc in range(KC):
                                for t in range(TPB):
                                    last = pe.transpose(pt[part][:, kc, t * P:(t + 1) * P],
                                                        src[:, t, kc * P:(kc + 1) * P], ident[:])
                            last.then_inc(m["turned"], 1)
                    batches(pe, batch)


def ffn_phase(nc, name, w_dram, xt, y, ht_n, ident, router=None, scales=None):
    WC = 2 * KC * P + D
    with ExitStack() as ctx:
        ph = Phase(nc, ctx, name)
        wst = ph.sb("wst", [P, 2, WC])
        wsc = ph.sb("wsc", [P, 2])
        w = ph.sb("w", [P, 2, ht_n, WC], F16)
        sil = ph.sb("sil", [P, 2, S])
        hv = ph.sb("hv", [P, 2, S])
        hh = ph.sb("hh", [P, 2, S], F16)
        hl = ph.sb("hl", [P, 2, S], F16)
        zero = ph.sb("zero", [P, S], F16)
        up = [ph.ps(f"up{i}", [P, 512]) for i in range(2)]
        vp = [ph.ps(f"vp{i}", [P, 512]) for i in range(2)]
        gp = [ph.ps(f"gp{i}", [P, 512]) for i in range(2)]
        yp = [ph.ps(f"yp{i}", [P, 2, D]) for i in range(2)]
        w_in = [ph.sem(f"w_in{i}") for i in range(2)]
        w_const = ph.sem("w_const")
        w_scaled = ph.sem("w_scaled")
        w_hi = ph.sem("w_hi")
        w_ready = ph.sem("w_ready")
        const_in = ph.sem("const_in")
        zeroed = ph.sem("zeroed")
        uvg = ph.sem("uvg")
        sil_ready = ph.sem("sil_ready")
        sv = ph.sem("sv")
        h_ready = ph.sem("h_ready")
        hh_ready = ph.sem("hh_ready")
        hl_ready = ph.sem("hl_ready")
        y_part = ph.sem("y_part")
        y_out = ph.sem("y_out")
        if router is not None:
            wr_dram, expand_dram = router
            wr32 = ph.sb("wr32", [P, KC, E0])
            wrp = ph.sb("wrp", [P, 2, KC, E0], F16)
            expand = ph.sb("expand", [P, ht_n * P], F16)
            lg = ph.sb("lg", [P, TILES, E0])
            mx = ph.sb("mx", [P, TILES])
            top = ph.sb("top", [P, TILES, 8])
            topi = ph.sb("topi", [P, TILES, 8], U32)
            topf = ph.sb("topf", [P, TILES, 8])
            eid = ph.sb("eid", [P, E0])
            gates = ph.sb("gates", [P, TILES, 16])
            pick = ph.sb("pick", [P, TILES, E0])
            gt32 = ph.sb("gt32", [P, TILES, 16])
            gparts = ph.sb("gparts", [P, TILES, 2, 16], F16)
            gt = ph.sb("gt", [P, TOK], F16)
            wr_in = ph.sem("wr_in")
            rsem = ph.sem("rsem")
            r_logits = ph.sem("r_logits")
            r_sub = ph.sem("r_sub")
            r_exp = ph.sem("r_exp")
            r_gates = ph.sem("r_gates")
            r_ghi = ph.sem("r_ghi")
            r_glo = ph.sem("r_glo")
            r_t = ph.sem("r_t")
            r_tout = ph.sem("r_tout")
            r_w = ph.sem("r_w")
        if scales is not None:
            scaled = ph.sem("scaled")
            s1 = ph.sb("s1", [P, ht_n])
            s3 = ph.sb("s3", [P, ht_n])
            s2 = ph.sb("s2", [P, D])
        h_scale = WSCALE if scales is None else 1.0
        tg = [bank[:].bitcast(F16) for bank in vp]

        with nc.Block() as block:
            @block.sync
            def _(sp):
                if router is not None:
                    with nc.allow_non_contiguous_dma(reason="a small table"):
                        sp.dma_start(wr32[:], wr_dram).then_inc(wr_in, 16)
                    sp.wait_ge(rsem, 1)
                    sp.dma_start(expand[0:32, :], expand_dram).then_inc(const_in, 16)
                if scales is not None:
                    sp.dma_start(s1[:], scales[0]).then_inc(const_in, 16)
                    sp.dma_start(s3[:], scales[1]).then_inc(const_in, 16)
                    sp.dma_start(s2[:], scales[2].to_broadcast([P, D])).then_inc(const_in, 16)
                for t in range(2):
                    sp.dma_start(wst[:, t, :], w_dram[t]).then_inc(w_in[t], 16)
                with sp.Fori(1, ht_n // 2) as k:
                    for par in range(2):
                        sp.wait_ge(w_ready, k * 2 - 1 + par)
                        sp.dma_start(wst[:, par, :], w_dram[ds(k * 2 + par, 1)].rearrange(
                            "o p c -> p (o c)")).then_inc(w_in[par], 16)

            @block.gpsimd
            def _(pool):
                pool.memset(wsc[:, 0:1], WSCALE).then_inc(w_const, 1)
                pool.memset(wsc[:, 1:2], 1.0).then_inc(w_const, 1)
                pool.wait_ge(w_const, 2)
                with pool.Fori(0, ht_n // 2) as k:
                    for par in range(2):
                        pool.wait_ge(w_in[par], k * 16 + 16)
                        pool.tensor_tensor(wst[:, par, :], wst[:, par, :], bcast(wsc[:, 0:1], P, WC),
                                           ALU.mult).then_inc(w_scaled, 1)
                        pool.wait_ge(w_scaled, k * 2 + par + 1)
                        pool.tensor_tensor(w[:, 0, ds(k * 2 + par, 1), :], wst[:, par, :],
                                           bcast(wsc[:, 1:2], P, WC), ALU.mult).then_inc(w_hi, 1)
                        pool.wait_ge(w_hi, k * 2 + par + 1)
                        pool.tensor_tensor(w[:, 1, ds(k * 2 + par, 1), :], wst[:, par, :],
                                           w[:, 0, ds(k * 2 + par, 1), :],
                                           ALU.subtract).then_inc(w_ready, 1)

            def wcol(part, ht, col, n):
                return w[:, part, ds(ht, 1), col:col + n].rearrange("p o c -> p (o c)") \
                    if not isinstance(ht, int) else w[:, part, ht, col:col + n]

            @block.tensor
            def _(pe):
                def three(out, wa, xa, start, stop):
                    for n, (i, j) in enumerate(((0, 0), (0, 1), (1, 0))):
                        last = pe.matmul(out, wa(i), xa(j), start=start and n == 0,
                                         stop=stop and n == 2, skip_group_check=True)
                    return last

                if router is not None:
                    pe.wait_ge(r_w, 3)
                    for t in range(TILES):
                        for kc in range(KC):
                            last = three(up[0][:, t * E0:(t + 1) * E0],
                                         lambda i: xt[:, i, kc, t * P:(t + 1) * P],
                                         lambda j: wrp[:, j, kc, :],
                                         t == 0 and kc == 0, t == TILES - 1 and kc == KC - 1)
                    last.then_inc(r_logits, 1)
                    pe.wait_ge(r_ghi, 1)
                    pe.wait_ge(r_glo, 1)
                    for t in range(TILES):
                        last = pe.transpose(tg[t // 8][0:32, (t % 8) * P:(t % 8 + 1) * P],
                                            gparts[:, t].rearrange("p a e -> p (a e)"), ident[:])
                    last.then_inc(r_t, 1)
                    pe.wait_ge(r_tout, 2)

                def products(b, ht, par):
                    for dst, col in ((up, 0), (vp, KC * P)):
                        for kc in range(KC):
                            last = three(dst[par][:], lambda i: wcol(i, ht, col + kc * P, P),
                                         lambda j: xt[:, j, kc, ds(b * S, S)], kc == 0, kc == KC - 1)
                    if router is not None:
                        last = pe.matmul(gp[par][:], expand[:, ds(ht * P, P)], gt[:, ds(b * S, S)],
                                         start=True, stop=True)
                    last.then_inc(uvg, 1)

                def down(s, ht, par):
                    pe.wait_ge(hh_ready, s + 1)
                    pe.wait_ge(hl_ready, s + 1)
                    for t in range(TPB):
                        src = (hh, hl)
                        last = three(yp[t // 2][:, t % 2, :],
                                     lambda i: src[i][:, par, t * P:(t + 1) * P],
                                     lambda j: wcol(j, ht, 2 * KC * P, D), False, False)
                    last.then_inc(y_part, 1)

                pe.wait_ge(zeroed, 1)
                def step(b, ht, par, wrap=False):
                    pe.wait_ge(h_ready, b * ht_n + ht + 1)
                    pe.wait_ge(w_ready, ht + 1)
                    products(b % B if wrap else b, ht, par)

                def open_banks(b):
                    pe.wait_ge(y_out, b * 2 + 1)
                    for bank in yp:
                        pe.matmul(bank[:].rearrange("p a d -> p (a d)"), zero[:, 0:P], zero[:],
                                  start=True, stop=False, skip_group_check=True)

                step(0, 0, 0)
                with pe.Fori(0, B) as b:
                    s0 = b * ht_n
                    step(b, 1, 1)
                    open_banks(b)
                    down(s0, 0, 0)
                    step(b, 2, 0)
                    down(s0 + 1, 1, 1)
                    with pe.Fori(1, ht_n // 2 - 1) as k:
                        step(b, k * 2 + 1, 1)
                        down(s0 + k * 2, k * 2, 0)
                        step(b, k * 2 + 2, 0)
                        down(s0 + k * 2 + 1, k * 2 + 1, 1)
                    step(b, ht_n - 1, 1)
                    down(s0 + ht_n - 2, ht_n - 2, 0)
                    step(b + 1, 0, 0, wrap=True)
                    down(s0 + ht_n - 1, ht_n - 1, 1)

            @block.scalar
            def _(act):
                if router is not None:
                    act.preload_act_table(ACT.Exp)
                    act.wait_ge(wr_in, 16)
                    act.activation(wrp[:, 0], wr32[:], ACT.Copy, scale=WSCALE).then_inc(r_w, 1)
                    act.wait_ge(r_sub, 1)
                    act.activation(lg[:], lg[:], ACT.Exp).then_inc(r_exp, 1)
                    act.wait_ge(r_gates, 1)
                    act.activation(gparts[:, :, 0], gt32[:], ACT.Copy).then_inc(r_ghi, 1)
                    act.wait_ge(r_t, 1)
                    for i in range(2):
                        act.activation(gt[0:32, i * 1024:(i + 1) * 1024], tg[i][0:32, :],
                                       ACT.Copy).then_inc(r_tout, 1)
                act.preload_act_table(ACT.Silu)
                if scales is not None:
                    act.wait_ge(scaled, 2)
                def silu(s, ht, par):
                    act.wait_ge(uvg, s + 1)
                    sc = 1.0 / WSCALE if scales is None else s1[:, ht:ht + 1] if isinstance(ht, int) else s1[:, ds(ht, 1)]
                    act.activation(sil[:, par], up[par][:], ACT.Silu, scale=sc).then_inc(sil_ready, 1)

                def hidden_hi(s, par):
                    act.wait_ge(h_ready, s + 3)
                    act.wait_ge(y_part, s + 1)
                    act.activation(hh[:, par], hv[:, par], ACT.Copy).then_inc(hh_ready, 1)

                def output(b):
                    act.wait_ge(y_part, b * ht_n + ht_n + 2)
                    for i in range(2):
                        act.activation(y[:, ds(b * TPB + i * 2, 2), :], yp[i][:], ACT.Copy,
                                       scale=1.0 / (WSCALE * h_scale)).then_inc(y_out, 1)

                def batch(b, later):
                    s0 = b * ht_n
                    silu(s0, 0, 0)
                    if later:
                        output(b - 1)
                    hidden_hi(s0, 0)
                    silu(s0 + 1, 1, 1)
                    hidden_hi(s0 + 1, 1)
                    with act.Fori(1, ht_n // 2) as k:
                        for par in range(2):
                            silu(s0 + k * 2 + par, k * 2 + par, par)
                            hidden_hi(s0 + k * 2 + par, par)

                batch(0, False)
                with act.Fori(1, B) as b:
                    batch(b, True)
                output(B - 1)

            @block.vector
            def _(v):
                done = [0]
                own_sem = rsem if router is not None else zeroed

                def own(ins):
                    ins.then_inc(own_sem, 1)
                    done[0] += 1
                    v.wait_ge(own_sem, done[0])

                if router is not None:
                    own(v.memset(expand[:], 0.0))
                    own(v.memset(gt[:], 0.0))
                    own(v.memset(gt32[:], 0.0))
                v.memset(zero[:], 0.0).then_inc(zeroed, 1)
                if router is None:
                    done[0] += 1
                if router is not None:
                    for e in range(E0):
                        own(v.memset(eid[:, e:e + 1], float(e)))
                    v.wait_ge(r_w, 1)
                    v.scalar_tensor_tensor(wrp[:, 1], wr32[:], WSCALE, wrp[:, 0], ALU.mult,
                                           ALU.subtract).then_inc(r_w, 1)
                    v.wait_ge(const_in, 16)
                    v.sem_inc(r_w, 1)
                    v.wait_ge(r_logits, 1)
                    flat = up[0][:, 0:TILES * E0].rearrange("p (t e) -> p t e", e=E0)
                    own(v.tensor_scalar(lg[:], flat, 1.0 / WSCALE, None, ALU.mult))
                    own(v.tensor_reduce(mx[:], lg[:], AX.X, ALU.max))
                    v.tensor_tensor(lg[:], lg[:], bcast(mx[:].unsqueeze(2), P, TILES, E0),
                                    ALU.subtract).then_inc(r_sub, 1)
                    v.wait_ge(r_exp, 1)
                    own(v.tensor_reduce(mx[:], lg[:], AX.X, ALU.add))
                    own(v.reciprocal(mx[:], mx[:]))
                    own(v.tensor_tensor(lg[:], lg[:], bcast(mx[:].unsqueeze(2), P, TILES, E0), ALU.mult))
                    for t in range(TILES):
                        own(v.max(top[:, t, :], lg[:, t, :]))
                        own(v.max_index(topi[:, t, :], top[:, t, :], lg[:, t, :]))
                    own(v.tensor_copy(topf[:], topi[:]))
                    own(v.tensor_tensor(mx[:], top[:, :, 0], top[:, :, 1], ALU.add))
                    own(v.reciprocal(mx[:], mx[:]))
                    own(v.tensor_tensor(top[:, :, 0:2], top[:, :, 0:2],
                                        bcast(mx[:].unsqueeze(2), P, TILES, 2), ALU.mult))
                    ids = bcast(eid[:].unsqueeze(1), P, TILES, E0)
                    for r in range(2):
                        own(v.tensor_tensor(pick[:], bcast(topf[:, :, r:r + 1], P, TILES, E0), ids,
                                            ALU.is_equal))
                        own(v.tensor_tensor(pick[:], pick[:], bcast(top[:, :, r:r + 1], P, TILES, E0),
                                            ALU.mult))
                        own(v.tensor_tensor(gt32[:, :, 1:1 + E0], gt32[:, :, 1:1 + E0], pick[:], ALU.add))
                    v.memset(gt32[:, :, 0:1], 1.0).then_inc(r_gates, 1)
                    v.wait_ge(r_ghi, 1)
                    v.tensor_tensor(gparts[:, :, 1], gt32[:], gparts[:, :, 0], ALU.subtract).then_inc(r_glo, 1)
                for n in range(2):
                    v.sem_inc(h_ready, 1)
                    v.sem_inc(y_part, 1)
                v.sem_inc(y_out, 1)
                if scales is not None:
                    v.wait_ge(const_in, 48)
                    v.tensor_scalar(s1[:], s1[:], 1.0 / WSCALE, None, ALU.mult).then_inc(scaled, 1)
                    v.tensor_scalar(s3[:], s3[:], 1.0 / WSCALE, None, ALU.mult).then_inc(scaled, 1)
                    v.wait_ge(scaled, 2)
                with v.Fori(0, B) as b:
                    with v.Fori(0, ht_n // 2) as k:
                        for par in range(2):
                            s = b * ht_n + k * 2 + par
                            v.wait_ge(uvg, s + 1)
                            v.wait_ge(sil_ready, s + 1)
                            if router is not None:
                                v.tensor_tensor(hv[:, par], vp[par][:], sil[:, par],
                                                ALU.mult).then_inc(sv, 1)
                                v.wait_ge(sv, s + 1)
                                v.tensor_tensor(hv[:, par], hv[:, par], gp[par][:],
                                                ALU.mult).then_inc(h_ready, 1)
                            else:
                                v.scalar_tensor_tensor(hv[:, par], vp[par][:], s3[:, ds(k * 2 + par, 1)],
                                                       sil[:, par], ALU.mult,
                                                       ALU.mult).then_inc(h_ready, 1)
                            v.wait_ge(hh_ready, s + 1)
                            v.tensor_tensor(hl[:, par], hv[:, par], hh[:, par],
                                            ALU.subtract).then_inc(hl_ready, 1)
                if scales is not None:
                    v.wait_ge(y_out, B * 2 + 1)
                    v.tensor_tensor(y[:], y[:], bcast(s2[:].unsqueeze(1), P, TILES, D), ALU.mult)


BESIDE = (
    (("load_weights 0", "own_dot 0", "project 0 0", "past_att_hi 3", "past_att_lo 3", "own_exponent 1"),
     ("own_dot_out 0", "project 0 1", "past_att_turn 3"),
     ("own_row_sum 1", "own_normalise 1", "split 0 0", "past_att_out 3", "own_prob_hi 1", "low 0 0",
      "own_prob_lo 1")),
    (("past_output 0", "split 0 1", "low 0 1"),
     ("past_output 1", "sigma 0 0"),
     ("past_output_out", "sigma_hi 0 0", "sigma_lo 0 0", "sigma 0 1", "sigma_hi 0 1", "sigma_lo 0 1", "weights 0",
      "load_weights 1", "past_output_store")),
    (("project 0 2", "own_prob_turn 1"),
     ("split 0 2", "low 0 2", "project 0 3", "own_pt_lo 1"),
     ("own_pt_hi 1", "split 0 3", "low 0 3", "sigma 0 2", "weights 1")),
    (("own_dot 1", "value 0 0"),
     ("sigma_hi 0 2", "sigma_lo 0 2", "value 0 1", "sigma 0 3"),
     ("own_dot_out 1", "own_add 0", "sigma_hi 0 3", "sigma_lo 0 3", "value_out 0 0", "value_lo 0 0")),
    (("score 0", "own_att_hi 0", "own_att_lo 0", "value_out 0 1", "value_lo 0 1"),
     ("project 1 0", "own_att_turn 0", "row_max 0"),
     ("own_att_out 0", "subtract_max 0", "split 1 0", "low 1 0", "own_add 1")),
    (("key_turn 0", "exponent 0"),
     ("own_att_hi 1", "own_att_lo 1", "project 1 1", "key_lo 0", "sigma 1 0"),
     ("own_att_turn 1", "row_sum 0", "normalise 0", "key_hi 0", "sigma_hi 1 0", "sigma_lo 1 0", "split 1 1",
      "low 1 1", "prob_hi 0", "prob_lo 0")),
    (("project 1 2", "project 1 3", "own_att_out 1", "own_add 2"),
     ("split 1 2", "low 1 2", "prob_turn 0", "sigma 1 1"),
     ("sigma_hi 1 1", "sigma_lo 1 1", "pt_hi 0", "own_att_hi 2", "own_att_lo 2", "split 1 3", "low 1 3")),
    (("value 1 0", "sigma 1 2", "sigma_hi 1 2", "sigma_lo 1 2", "sigma 1 3", "sigma_hi 1 3", "sigma_lo 1 3",
      "pt_lo 0", "score 1", "value 1 1"),
     ("row_max 1", "own_att_turn 2", "subtract_max 1"),
     ("key_turn 1", "value_out 1 0", "value_lo 1 0", "own_att_out 2", "value_out 1 1", "value_lo 1 1",
      "own_add 3", "key_hi 1", "key_lo 1")),
)


class Unit:

    def __init__(self, n, par):
        self.n, self.par = n, par
        self.b, self.k = n % B, (n // B) % GROUPS


def attn0_phase(nc, w_dram, wo_dram, betas, mask_dram, xt, y_dram, ident):
    KQV = 2 * HG * DH
    WC = 3 * KQV
    EIGHTH = WC // 8
    HALF = ((slice(0, SEG), slice(SEG, P)), (slice(SEG, P), slice(0, SEG)))
    with ExitStack() as ctx:
        ph = Phase(nc, ctx, "a0")
        w = ph.sb("w", [P, 2, 2, WC], F16)
        wo = ph.sb("wo", [P, 2, H0 * D], F16)
        wst = ph.sb("wst", [P, EIGHTH])
        wsc = ph.sb("wsc", [P, 2])
        beta = ph.sb("beta", [P, H0 * DH])
        omb = ph.sb("omb", [P, HG * DH])
        mask = ph.sb("mask", [P, SEG])
        qs = ph.sb("qs", [P, 2, 2, S], F16)
        ks = ph.sb("ks", [P, 2, 2, S], F16)
        x32 = ph.sb("x32", [P, 2, S])
        ee = ph.sb("ee", [P, 2, S])
        sg = ph.sb("sg", [P, 2, 2, HG, TPB, 4, SEG], F16)
        skr = ph.sb("skr", [P, 2, 2, HG, TPB, P], F16)
        v32 = ph.sb("v32", [P, 2, TPB, HG * DH])
        vs = ph.sb("vs", [P, 2, TPB, HG * DH], F16)
        sm = ph.sb("sm", [P, 2 * TPB, SEG])
        red = ph.sb("red", [P, 2, 2 * TPB])
        ps = ph.sb("ps", [P, 2, 2 * TPB, SEG], F16)
        ptb = ph.sb("ptb", [P, 2, 2, TPB, P], F16)
        ms = ph.sb("ms", [P, 2, 2, HG, DH + 2], F16)
        ms0 = ph.sb("ms0", [P, 2, DH + 2], F16)
        dd = ph.sb("dd", [P, 2, 2, HG, DH + 2], F16)
        rd = ph.sb("rd", [P, HG])
        d32 = ph.sb("d32", [P, HG, DH])
        am = ph.sb("am", [P, 2, HG * DH])
        at = ph.sb("at", [P, 2, TPB, HG * DH])
        ats = ph.sb("ats", [P, 2, HG * DH], F16)
        att = ph.sb("att", [P, 2, ROWS16, P], F16)
        yst = ph.sb("yst", [P, D])
        mem = ph.ps("mem", [P, HG, 256])
        num = ph.ps("num", [P, HG, 256])
        pj = [ph.ps(f"pj{i}", [P, S]) for i in range(2)]
        tr = [ph.ps(f"tr{i}", [P, S]) for i in range(2)]
        tr16 = [t[:].bitcast(F16) for t in tr]

        names = ("wo_in w0_hi w0_lo wo_hi wo_lo w_in w_sc w_hi w_ready const_in beta_r init pj_full x32_r"
                 " hi_r ex_r e1_r lo_r sg_r sghi sglo skr_full skrhi skrlo v_r omb_r vlo s_full sm_r mx_r"
                 " sd_r pex_r sum_r ri_r pn_r phi plo pt_full pthi ptlo num_full rd_r d_r dhi dlo am_r"
                 " mem_full mhi mlo dot_full dot_r at_r ahi alo att_full att_r y_full y_out y_stored yst_free").split()
        m = {n: ph.sem(n) for n in names}
        w0_in = [ph.sem(f"w0_in{i}") for i in range(3)]

        def three(pe, out, wa, xa, start=False, stop=False):
            for n, (i, j) in enumerate(((0, 0), (0, 1), (1, 0))):
                last = pe.matmul(out, wa(i), xa(j), start=start and n == 0, stop=stop and n == 2,
                                 skip_group_check=True)
            return last

        def units(eng, steps, retrieve, update, split):
            def beside(names, plain, own, past):
                for text in names:
                    name, *args = text.split()
                    unit = {"own": own, "past": past}.get(name.split("_")[0], plain)
                    name = name.removeprefix("own_").removeprefix("past_")
                    if unit is not None and name in steps:
                        steps[name](unit, *[int(a) for a in args])

            def segment(j, plain, own, past):
                retrieve(own, j)
                beside(BESIDE[j][0], plain, own, past)
                if j < NSEG - 1:
                    update(own, j)
                beside(BESIDE[j][1], plain, own, past)
                if j < NSEG - 1:
                    split(own, j)
                beside(BESIDE[j][2], plain, own, past)

            for row in BESIDE:
                for names in row:
                    beside(names, Unit(0, 0), None, None)
            for j in range(2):
                segment(j, Unit(1, 1), Unit(0, 0), None)
            with eng.Fori(0, GROUPS) as k:
                with eng.Fori(0, B // 2) as bb:
                    for par in range(2):
                        n = k * B + bb * 2 + par
                        cur, new, after = Unit(n, par), Unit(n + 1, 1 - par), Unit(n + 2, par)
                        for j in range(2, NSEG):
                            segment(j, new, cur, None)
                        for j in range(2):
                            segment(j, after, new, cur)

        def later(unit):
            return not isinstance(unit.n, int) or unit.n > 0

        def keys(par, part, c):
            return sg[:, par, part, c, :, 0::3, :]

        def queries(par, part, c):
            return sg[:, par, part, c, :, 1:3, :]

        def probs_t(part, odd):
            return tr16[part][0:SEG, :].rearrange("p (c t o s) -> p c t o s", c=2, t=TPB, o=2)[:, :, :, odd, :]

        with nc.Block() as block:
            @block.sync
            def _(sp):
                for i in range(3):
                    cols = slice(i * KQV, (i + 1) * KQV)
                    sp.dma_start(v32[:].rearrange("p a t e -> p (a t e)")[:, cols],
                                 w_dram[0, :, cols]).then_inc(w0_in[i], 16)
                sp.dma_start(mask[:], mask_dram).then_inc(m["const_in"], 16)
                sp.dma_start(beta[:], betas.to_broadcast([P, H0 * DH])).then_inc(m["const_in"], 16)
                sp.dma_start(at[:].rearrange("p a t e -> p (a t e)"), wo_dram).then_inc(m["wo_in"], 16)

                def load_weights(new, half):
                    if later(new) or half:
                        sp.wait_ge(m["w_ready"], new.n * 2 + half)
                    grp, e = (new.n // B + 1) % GROUPS, new.b * 2 + half
                    src = w_dram.rearrange("g p (e c) -> g e p c", e=8)[ds(grp, 1), ds(e, 1)]
                    sp.dma_start(wst[:], src.rearrange("g e p c -> p (g e c)")).then_inc(m["w_in"], 16)

                def output_store(u):
                    sp.wait_ge(m["y_out"], u.n + 1)
                    rows = y_dram.rearrange("b (s k m) d -> b k s m d", s=NSEG, k=GROUPS)[ds(u.b, 1), ds(u.k, 1)]
                    for s in range(NSEG):
                        sp.dma_start(rows[:, :, s].rearrange("x y m d -> (x y m) d"),
                                     yst[s * 16:(s + 1) * 16, :]).then_inc(m["y_stored"], 16)
                    sp.wait_ge(m["y_stored"], (u.n + 1) * NSEG * 16)
                    sp.sem_inc(m["yst_free"], 1)

                sp.sem_inc(m["yst_free"], 1)

                def nothing(u, j):
                    pass
                units(sp, dict(load_weights=load_weights, output_store=output_store), nothing, nothing, nothing)

            @block.gpsimd
            def _(pool):
                def weights(new, half):
                    n = new.n * 2 + half
                    if later(new):
                        pool.wait_ge(m["pj_full"], new.n * 12)
                    pool.wait_ge(m["w_in"], n * 16 + 16)
                    pool.tensor_tensor(wst[:], wst[:], bcast(wsc[:, 0:1], P, EIGHTH), ALU.mult).then_inc(m["w_sc"], 1)
                    pool.wait_ge(m["w_sc"], n + 3)
                    buf, cols = (new.n // B + 1) % 2, (new.b * 2 + half) * EIGHTH

                    def to(part):
                        return w[:].rearrange("p a q c -> p (a q c)")[:, ds(buf * (2 * WC) + part * WC + cols, EIGHTH)]
                    pool.tensor_tensor(to(0), wst[:], bcast(wsc[:, 1:2], P, EIGHTH), ALU.mult).then_inc(m["w_hi"], 1)
                    pool.wait_ge(m["w_hi"], n + 1)
                    pool.tensor_tensor(to(1), wst[:], to(0), ALU.subtract).then_inc(m["w_ready"], 1)

                def low(new, h, ci):
                    c, dst = ci % 2, (qs, ks)[ci // 2]
                    pool.wait_ge(m["hi_r"], (new.n * 2 + h) * 4 + ci + 1)
                    pool.tensor_tensor(dst[:, 1, c, :], x32[:, c, :], dst[:, 0, c, :], ALU.subtract).then_inc(m["lo_r"], 1)

                def sigma_lo(new, h, ci):
                    c, to = ci % 2, (queries, keys)[ci // 2]
                    pool.wait_ge(m["sghi"], (new.n * 2 + h) * 4 + ci + 1)
                    head = h * 2 + c
                    pool.tensor_tensor(to(new.par, 1, head), ee[:, c, :].rearrange("p (t o s) -> p t o s", t=TPB, o=2),
                                       to(new.par, 0, head), ALU.subtract).then_inc(m["sglo"], 1)

                def value_lo(new, h, i):
                    cols = slice(h * 2 * DH, (h + 1) * 2 * DH)
                    pool.wait_ge(m["v_r"], (new.n * 2 + h) * 2 + i + 1)
                    pool.tensor_tensor(vs[:, 1, i * 2:i * 2 + 2, cols], v32[:, new.par, i * 2:i * 2 + 2, cols],
                                       vs[:, 0, i * 2:i * 2 + 2, cols], ALU.subtract).then_inc(m["vlo"], 1)

                def subtract_max(new, h):
                    pool.wait_ge(m["mx_r"], new.n * 2 + h + 1)
                    pool.tensor_tensor(sm[:], sm[:], bcast(red[:, 0].unsqueeze(2), P, 2 * TPB, SEG),
                                       ALU.subtract).then_inc(m["sd_r"], 1)

                def normalise(new, h):
                    pool.wait_ge(m["ri_r"], new.n * 2 + h + 1)
                    pool.tensor_tensor(sm[:], sm[:], bcast(red[:, 1].unsqueeze(2), P, 2 * TPB, SEG),
                                       ALU.mult).then_inc(m["pn_r"], 1)

                def prob_lo(new, h):
                    pool.wait_ge(m["phi"], new.n * 2 + h + 1)
                    pool.tensor_tensor(ps[:, 1], sm[:], ps[:, 0], ALU.subtract).then_inc(m["plo"], 1)

                def add(u, t):
                    pool.wait_ge(m["dot_r"], u.n * 4 + 4)
                    pool.wait_ge(m["am_r"], u.n * NSEG + 2 * t + 2)
                    pool.tensor_tensor(at[:, u.par, t], at[:, u.par, t], am[:, t % 2], ALU.add).then_inc(m["at_r"], 1)

                def att_lo(u, t):
                    pool.wait_ge(m["ahi"], u.n * TPB + t + 1)
                    pool.tensor_tensor(ats[:, 1], at[:, u.par, t], ats[:, 0], ALU.subtract).then_inc(m["alo"], 1)

                def nothing(u, j):
                    pass

                pool.memset(wsc[:, 0:1], WSCALE).then_inc(m["w_sc"], 1)
                pool.memset(wsc[:, 1:2], 1.0).then_inc(m["w_sc"], 1)
                pool.wait_ge(m["w_sc"], 2)
                units(pool, dict(weights=weights, low=low, sigma_lo=sigma_lo, value_lo=value_lo,
                                 subtract_max=subtract_max, normalise=normalise, prob_lo=prob_lo, add=add,
                                 att_lo=att_lo), nothing, nothing, nothing)

            @block.tensor
            def _(pe):
                def wcol(part, k, col, n):
                    if isinstance(k, int):
                        return w[:, k % 2, part, col:col + n]
                    return w[:].rearrange("p a q c -> p (a q c)")[:, ds((k % 2) * (2 * WC) + (part * WC + col), n)]

                def project(new, h, ci):
                    i = new.n * 2 + h
                    kind, c = ci // 2, ci % 2
                    if ci == 0 and h == 0:
                        if later(new):
                            pe.wait_ge(m["w_ready"], new.n * 2)
                        else:
                            pe.wait_ge(m["w0_lo"], 3)
                    if ci >= 2:
                        pe.wait_ge(m["ex_r"], i * 4 + ci - 1)
                    elif later(new) or h:
                        pe.wait_ge(m["v_r"], i * 2 + ci - 1)
                    for kc in range(KC):
                        last = three(pe, pj[c][:],
                                     lambda p: wcol(p, new.k, kind * KQV + kc * HG * DH + (h * 2 + c) * DH, DH),
                                     lambda p: xt[:, p, kc, ds(new.b * S, S)], kc == 0, kc == KC - 1)
                    last.then_inc(m["pj_full"], 1)

                def value(new, h, i):
                    pe.wait_ge(m["ex_r"], (new.n * 2 + h) * 4 + 3 + i)
                    for t in range(2):
                        for kc in range(KC):
                            last = three(pe, pj[i][:, t * D:(t + 1) * D],
                                         lambda p: xt[:, p, kc, ds(new.b * S + (i * 2 + t) * P, P)],
                                         lambda p: wcol(p, new.k, 2 * KQV + kc * HG * DH + h * 2 * DH, 2 * DH),
                                         t == 0 and kc == 0, t == 1 and kc == KC - 1)
                    last.then_inc(m["pj_full"], 1)

                def score(new, h):
                    i = new.n * 2 + h
                    if h:
                        pe.wait_ge(m["pthi"], new.n * 2 + 1)
                    elif later(new):
                        pe.wait_ge(m["dot_r"], new.n * 4)
                    pe.wait_ge(m["lo_r"], i * 4 + 4)
                    for c in range(2):
                        for t in range(TPB):
                            for odd in range(2):
                                rows = slice(odd * SEG, odd * SEG + SEG)
                                s0 = (2 * t + odd) * SEG
                                col = (c * TPB + t) * SEG
                                last = three(pe, tr[0][rows, col:col + SEG],
                                             lambda p: qs[:, p, c, s0:s0 + SEG],
                                             lambda p: ks[:, p, c, s0:s0 + SEG],
                                             c == 0 and t == 0, c == 1 and t == TPB - 1)
                    last.then_inc(m["s_full"], 1)

                def key_turn(new, h):
                    i = new.n * 2 + h
                    pe.wait_ge(m["sglo"], i * 4 + 4)
                    for part in range(2):
                        if part == 0:
                            pe.wait_ge(m["sm_r"], new.n * 2 + 1 + h)
                        elif later(new):
                            pe.wait_ge(m["att_r"], new.n * 4 - 3 + 2 * h)
                        elif h:
                            pe.wait_ge(m["ptlo"], 1)
                        for c in range(2):
                            for t in range(TPB):
                                q = (c * TPB + t) * P
                                pe.transpose(tr16[part][:, q:q + P],
                                             sg[:, new.par, part, h * 2 + c, t, 2:4, :].rearrange("p a s -> p (a s)"),
                                             ident[:])
                                last = pe.transpose(tr16[part][0:SEG, q:q + P],
                                                    sg[:, new.par, part, h * 2 + c, t, 0, :], ident[:])
                        last.then_inc(m["skr_full"], 1)

                def prob_turn(new, h):
                    i = new.n * 2 + h
                    for part, ready in enumerate(("phi", "plo")):
                        pe.wait_ge(m[ready], i + 1)
                        if h == 0 and part == 0:
                            pe.wait_ge(m["skrhi"], new.n * 2 + 1)
                        elif later(new):
                            if part == 0:
                                pe.wait_ge(m["y_out"], new.n)
                            else:
                                pe.wait_ge(m["att_r"], new.n * 4 - 2 + 2 * h)
                        else:
                            pe.wait_ge(m["dot_r" if h else "skrlo"], 2 if h else 1)
                        pe.transpose(tr16[part][:, 0:P], ps[:, part, 0:2, :].rearrange("p a s -> p (a s)"), ident[:])
                        for ct in range(1, 2 * TPB):
                            last = pe.transpose(tr16[part][0:SEG, ct * P:(ct + 1) * P], ps[:, part, ct, :], ident[:])
                        last.then_inc(m["pt_full"], 1)

                def dot(new, h):
                    i = new.n * 2 + h
                    pe.wait_ge(m["pthi"], i + 1)
                    pe.wait_ge(m["ptlo"], i + 1)
                    pe.wait_ge(m["vlo"], i * 2 + 2)
                    for half in range(2):
                        if h == 0:
                            pe.wait_ge(m[("skrhi", "skrlo")[half]], new.n * 2 + 2)
                        for t in range(2):
                            for c in range(2):
                                cols = slice((h * 2 + c) * DH, (h * 2 + c + 1) * DH)
                                last = three(pe, tr[half][:, (t * 2 + c) * DH:(t * 2 + c + 1) * DH],
                                             lambda p: ptb[:, p, c, half * 2 + t, :],
                                             lambda p: vs[:, p, half * 2 + t, cols],
                                             t == 0 and c == 0, t == 1 and c == 1)
                        last.then_inc(m["dot_full"], 1)

                def retrieve(u, j):
                    t, odd = j // 2, j % 2
                    if j == 0:
                        pe.wait_ge(m["sglo"], u.n * 8 + 8)
                        if later(u):
                            pe.wait_ge(m["am_r"], u.n * NSEG)
                        for c in range(HG):
                            pe.matmul(mem[:, c, 0:DH + 1], ident[:], ms0[:, 0, 0:DH + 1], start=c % 2 == 0, stop=False,
                                      skip_group_check=True)
                    for bank in range(2):
                        if j:
                            pe.wait_ge(m["mlo"], (u.n * 7 + j) * 2 - 1 + bank)
                        for c in (2 * bank, 2 * bank + 1):
                            last = three(pe, num[:, c, 0:DH + 1],
                                         lambda p: sg[:, u.par, p, c, t, 2 * odd:2 * odd + 2, :].rearrange(
                                             "p a s -> p (a s)"),
                                         lambda p: ms0[:, p, 0:DH + 1] if j == 0 else ms[:, j % 2, p, c, 0:DH + 1],
                                         c % 2 == 0, c % 2 == 1)
                        last.then_inc(m["num_full"], 1)

                def update(u, j):
                    t, odd = j // 2, j % 2
                    if j == 0:
                        pe.wait_ge(m["skrhi"], u.n * 2 + 2)
                        pe.wait_ge(m["skrlo"], u.n * 2 + 2)
                    for bank in range(2):
                        pe.wait_ge(m["dlo"], (u.n * 7 + j) * 2 + bank + 1)
                        for c in (2 * bank, 2 * bank + 1):
                            last = three(pe, mem[:, c, 0:DH + 1], lambda p: skr[:, u.par, p, c, t, :],
                                         lambda p: dd[:, odd, p, c, 0:DH + 1])
                        last.then_inc(m["mem_full"], 1)

                def split(u, j):
                    pass

                def att_turn(u, t):
                    n = u.n + 1
                    pe.wait_ge(m["alo"], u.n * TPB + t + 1)
                    if t == 0:
                        pe.wait_ge(m["dot_r"], u.n * 4 + 4)
                    elif t < 3:
                        pe.wait_ge(m[("skrlo", "ptlo")[t - 1]], n * 2 + 1)
                    else:
                        pe.wait_ge(m["dot_r"], n * 4 + 2)
                    for part in range(2):
                        for c in range(HG):
                            q = (part * HG + c) * P
                            last = pe.transpose(tr16[1][:, q:q + P], ats[:, part, c * DH:(c + 1) * DH], ident[:])
                    last.then_inc(m["att_full"], 1)

                def output(u, part):
                    if part == 0:
                        pe.wait_ge(m["wo_lo"], 4)
                        pe.wait_ge(m["att_r"], u.n * TPB + TPB)
                        pe.wait_ge(m["dot_r"], u.n * 4 + 6)
                    for r in range(part * 8, part * 8 + 8):
                        last = three(pe, tr[0][:, 0:D], lambda p: att[:, p, r, :],
                                     lambda p: wo[:, p, r * D:(r + 1) * D], r == 0, r == ROWS16 - 1)
                    if part:
                        last.then_inc(m["y_full"], 1)

                pe.wait_ge(m["init"], 9)
                units(pe, dict(project=project, value=value, score=score, key_turn=key_turn, prob_turn=prob_turn,
                               dot=dot, att_turn=att_turn, output=output), retrieve, update, split)

            @block.scalar
            def _(act):
                for i in range(3):
                    act.wait_ge(w0_in[i], 16)
                    act.activation(w[:, 0, 0, i * KQV:(i + 1) * KQV],
                                   v32[:].rearrange("p a t e -> p (a t e)")[:, i * KQV:(i + 1) * KQV], ACT.Copy,
                                   scale=WSCALE).then_inc(m["w0_hi"], 1)
                act.wait_ge(m["const_in"], 32)
                act.activation(beta[:], beta[:], ACT.Sigmoid).then_inc(m["beta_r"], 1)
                act.preload_act_table(ACT.Exp)
                act.wait_ge(m["wo_in"], 16)
                for i in range(4):
                    act.activation(wo[:, 0, i * 1024:(i + 1) * 1024],
                                   at[:].rearrange("p a t e -> p (a t e)")[:, i * 1024:(i + 1) * 1024], ACT.Copy,
                                   scale=WSCALE).then_inc(m["wo_hi"], 1)

                def split(new, h, ci):
                    c, dst = ci % 2, (qs, ks)[ci // 2]
                    i = new.n * 2 + h
                    act.wait_ge(m["pj_full"], i * 6 + ci + 1)
                    if later(new) or h or ci >= 2:
                        act.wait_ge(m["sglo"], i * 4 + ci - 1)
                    if ci == 0 and (later(new) or h):
                        act.wait_ge(m["s_full"], i)
                    act.activation(x32[:, c, :], pj[c][:], ACT.Copy, scale=1 / WSCALE).then_inc(m["x32_r"], 1)
                    act.activation(dst[:, 0, c, :], pj[c][:], ACT.Copy, scale=1 / WSCALE).then_inc(m["hi_r"], 1)
                    act.activation(ee[:, c, :], pj[c][:], ACT.Exp, scale=1 / WSCALE).then_inc(m["ex_r"], 1)

                def sigma_hi(new, h, ci):
                    c, to = ci % 2, (queries, keys)[ci // 2]
                    act.wait_ge(m["sg_r"], (new.n * 2 + h) * 4 + ci + 1)
                    act.activation(to(new.par, 0, h * 2 + c), ee[:, c, :].rearrange("p (t o s) -> p t o s", t=TPB, o=2),
                                   ACT.Copy).then_inc(m["sghi"], 1)

                def value_out(new, h, i):
                    cols = slice(h * 2 * DH, (h + 1) * 2 * DH)
                    src = pj[i][:].rearrange("p (t e) -> p t e", t=2)
                    act.wait_ge(m["pj_full"], (new.n * 2 + h) * 6 + 5 + i)
                    act.activation(vs[:, 0, i * 2:i * 2 + 2, cols], src, ACT.Copy, scale=1 / WSCALE)
                    act.activation(v32[:, new.par, i * 2:i * 2 + 2, cols], src, ACT.Copy,
                                   scale=1 / WSCALE).then_inc(m["v_r"], 1)

                def key_hi(new, h):
                    act.wait_ge(m["skr_full"], (new.n * 2 + h) * 2 + 1)
                    act.activation(skr[:, new.par, 0, h * 2:h * 2 + 2].rearrange("p c t d -> p (c t d)"), tr16[0],
                                   ACT.Copy).then_inc(m["skrhi"], 1)

                def exponent(new, h):
                    act.wait_ge(m["sd_r"], new.n * 2 + h + 1)
                    act.activation(sm[:], sm[:], ACT.Exp, scale=float(DH) ** -0.5).then_inc(m["pex_r"], 1)

                def prob_hi(new, h):
                    act.wait_ge(m["pn_r"], new.n * 2 + h + 1)
                    act.activation(ps[:, 0], sm[:], ACT.Copy).then_inc(m["phi"], 1)

                def pt_hi(new, h):
                    act.wait_ge(m["pt_full"], (new.n * 2 + h) * 2 + 1)
                    for odd in range(2):
                        kr, qr = HALF[odd]
                        last = act.activation(ptb[kr, 0, :, :, qr], probs_t(0, odd), ACT.Copy)
                    last.then_inc(m["pthi"], 1)

                def retrieve(u, j):
                    if j == NSEG - 1:
                        return
                    kr, odd = HALF[j % 2][0], j % 2
                    for bank in range(2):
                        c = slice(2 * bank, 2 * bank + 2)
                        act.wait_ge(m["d_r"], (u.n * 7 + j) * 2 + bank + 1)
                        act.activation(dd[kr, odd, 0, c, 0:DH], d32[kr, c], ACT.Copy).then_inc(m["dhi"], 1)

                def update(u, j):
                    pass

                def split_mem(u, j):
                    for bank in range(2):
                        c = slice(2 * bank, 2 * bank + 2)
                        act.wait_ge(m["mem_full"], (u.n * 7 + j) * 2 + bank + 1)
                        act.activation(ms[:, (j + 1) % 2, 0, c, 0:DH + 1], mem[:, c, 0:DH + 1],
                                       ACT.Copy).then_inc(m["mhi"], 1)

                def att_hi(u, t):
                    act.wait_ge(m["at_r"], u.n * TPB + t + 1)
                    act.activation(ats[:, 0], at[:, u.par, t], ACT.Copy).then_inc(m["ahi"], 1)

                def att_out(u, t):
                    act.wait_ge(m["att_full"], u.n * TPB + t + 1)
                    for part in range(2):
                        src = tr16[1][:, part * 512:(part + 1) * 512].rearrange("p (c o a r) -> p c o a r", c=HG, o=2,
                                                                               r=ROWS16)
                        for blk in range(2):
                            m0 = (2 * t + 1 - blk) * 16
                            dst = att[:, part, :, m0:m0 + 16].rearrange("p r (c a) -> p c a r", c=HG)
                            last = act.activation(dst, src[:, :, blk], ACT.Copy)
                    last.then_inc(m["att_r"], 1)

                def output_out(u):
                    act.wait_ge(m["yst_free"], u.n + 1)
                    act.wait_ge(m["y_full"], u.n + 1)
                    act.activation(yst[:], tr[0][:, 0:D], ACT.Copy, scale=1 / WSCALE).then_inc(m["y_out"], 1)

                act.wait_ge(m["w0_lo"], 3)
                act.wait_ge(m["wo_lo"], 4)
                act.wait_ge(m["init"], 9)
                units(act, dict(split=split, sigma_hi=sigma_hi, value_out=value_out, key_hi=key_hi, exponent=exponent,
                                prob_hi=prob_hi, pt_hi=pt_hi, att_hi=att_hi, att_out=att_out, output_out=output_out),
                      retrieve, update, split_mem)

            @block.vector
            def _(v):
                v.memset(ptb[:], 0.0).then_inc(m["init"], 1)
                v.memset(dd[:], 0.0).then_inc(m["init"], 1)
                v.memset(ms0[:], 0.0).then_inc(m["init"], 1)
                v.memset(rd[:], 0.0).then_inc(m["init"], 1)
                v.memset(red[:], 0.0).then_inc(m["init"], 1)
                v.memset(am[:], 0.0).then_inc(m["init"], 1)
                v.wait_ge(m["init"], 6)
                v.memset(dd[0:SEG, 0, 0, :, DH:DH + 1], 1.0).then_inc(m["init"], 1)
                v.memset(dd[SEG:P, 1, 0, :, DH:DH + 1], 1.0).then_inc(m["init"], 1)
                v.memset(ms0[:, 0, DH:DH + 1], 1.0 / DH).then_inc(m["init"], 1)
                v.wait_ge(m["init"], 9)
                for i in range(3):
                    cols = slice(i * KQV, (i + 1) * KQV)
                    v.wait_ge(m["w0_hi"], i + 1)
                    v.scalar_tensor_tensor(w[:, 0, 1, cols], v32[:].rearrange("p a t e -> p (a t e)")[:, cols], WSCALE,
                                           w[:, 0, 0, cols], ALU.mult, ALU.subtract).then_inc(m["w0_lo"], 1)
                for i in range(4):
                    cols = slice(i * 1024, (i + 1) * 1024)
                    v.wait_ge(m["wo_hi"], i + 1)
                    v.scalar_tensor_tensor(wo[:, 1, cols], at[:].rearrange("p a t e -> p (a t e)")[:, cols], WSCALE,
                                           wo[:, 0, cols], ALU.mult, ALU.subtract).then_inc(m["wo_lo"], 1)

                def sigma(new, h, ci):
                    c = ci % 2
                    i = (new.n * 2 + h) * 4 + ci + 1
                    v.wait_ge(m["ex_r"], i)
                    v.tensor_scalar(ee[:, c, :], ee[:, c, :], 1.0, None, ALU.min).then_inc(m["e1_r"], 1)
                    v.wait_ge(m["e1_r"], i)
                    v.scalar_tensor_tensor(ee[:, c, :], x32[:, c, :], 0.0, ee[:, c, :], ALU.max,
                                           ALU.add).then_inc(m["sg_r"], 1)

                def key_lo(new, h):
                    v.wait_ge(m["skr_full"], (new.n * 2 + h) * 2 + 2)
                    v.tensor_copy(skr[:, new.par, 1, h * 2:h * 2 + 2].rearrange("p c t d -> p (c t d)"),
                                  tr16[1]).then_inc(m["skrlo"], 1)

                def row_max(new, h):
                    i = new.n * 2 + h
                    v.wait_ge(m["s_full"], i + 1)
                    if later(new) or h:
                        v.wait_ge(m["plo"], i)
                    v.tensor_tensor(sm[:], tr[0][:].rearrange("p (x s) -> p x s", s=SEG),
                                    bcast(mask[:].unsqueeze(1), P, 2 * TPB, SEG), ALU.add).then_inc(m["sm_r"], 1)
                    v.wait_ge(m["sm_r"], i + 1)
                    v.tensor_reduce(red[:, 0], sm[:], AX.X, ALU.max).then_inc(m["mx_r"], 1)

                def row_sum(new, h):
                    i = new.n * 2 + h
                    v.wait_ge(m["pex_r"], i + 1)
                    v.tensor_reduce(red[:, 1], sm[:], AX.X, ALU.add).then_inc(m["sum_r"], 1)
                    v.wait_ge(m["sum_r"], i + 1)
                    v.reciprocal(red[:, 1], red[:, 1]).then_inc(m["ri_r"], 1)

                def pt_lo(new, h):
                    v.wait_ge(m["pt_full"], (new.n * 2 + h) * 2 + 2)
                    for odd in range(2):
                        kr, qr = HALF[odd]
                        last = v.tensor_copy(ptb[kr, 1, :, :, qr], probs_t(1, odd))
                    last.then_inc(m["ptlo"], 1)

                def dot_out(new, h):
                    i = new.n * 2 + h
                    if h == 0:
                        v.tensor_scalar(omb[:], beta[:, ds(new.k * (HG * DH), HG * DH)], -1.0, 1.0, ALU.mult,
                                        ALU.add).then_inc(m["omb_r"], 1)
                        v.wait_ge(m["omb_r"], new.n + 1)
                    for half in range(2):
                        cols = slice(h * 2 * DH, (h + 1) * 2 * DH)
                        v.wait_ge(m["dot_full"], i * 2 + half + 1)
                        v.tensor_tensor(at[:, new.par, half * 2:half * 2 + 2, cols],
                                        tr[half][:].rearrange("p (t e) -> p t e", t=2),
                                        bcast(omb[:, cols].unsqueeze(1), P, 2, 2 * DH), ALU.mult).then_inc(m["dot_r"], 1)

                def retrieve(u, j):
                    t, odd = j // 2, j % 2
                    kr = HALF[odd][0]
                    if j == 0:
                        v.wait_ge(m["v_r"], u.n * 4 + 4)
                    for bank in range(2):
                        i = (u.n * NSEG + j) * 2 + bank + 1
                        v.wait_ge(m["num_full"], i)
                        v.reciprocal(rd[:, 2 * bank:2 * bank + 2], num[:, 2 * bank:2 * bank + 2, DH]).then_inc(m["rd_r"], 1)
                    for bank in range(2):
                        v.wait_ge(m["rd_r"], (u.n * NSEG + j) * 2 + bank + 1)
                        if j == NSEG - 1:
                            continue
                        for c in (2 * bank, 2 * bank + 1):
                            last = v.scalar_tensor_tensor(d32[kr, c], num[kr, c, 0:DH], rd[kr, c:c + 1],
                                                          v32[kr, u.par, t, c * DH:(c + 1) * DH], ALU.mult,
                                                          ALU.subtract, reverse1=True)
                        last.then_inc(m["d_r"], 1)
                    if j not in (4, 6):
                        attend(u, j, 0)
                    if j == NSEG - 1:
                        attend(u, j, 1)

                def attend(u, j, bank):
                    t, odd = j // 2, j % 2
                    qr = HALF[odd][1]
                    if bank == 0 and (j in (4, 6) or (j == 0 and later(u))):
                        v.wait_ge(m["at_r"], u.n * TPB + t - 1)
                    for c in (2 * bank, 2 * bank + 1):
                        last = v.scalar_tensor_tensor(am[qr, t % 2, c * DH:(c + 1) * DH], num[qr, c, 0:DH],
                                                      rd[qr, c:c + 1], beta[qr, ds(u.k * (HG * DH) + c * DH, DH)],
                                                      ALU.mult, ALU.mult)
                    if bank:
                        last.then_inc(m["am_r"], 1)

                def update(u, j):
                    kr, odd = HALF[j % 2][0], j % 2
                    for bank in range(2):
                        c = slice(2 * bank, 2 * bank + 2)
                        v.wait_ge(m["dhi"], (u.n * 7 + j) * 2 + bank + 1)
                        v.tensor_tensor(dd[kr, odd, 1, c, 0:DH], d32[kr, c], dd[kr, odd, 0, c, 0:DH],
                                        ALU.subtract).then_inc(m["dlo"], 1)
                    if j in (4, 6):
                        attend(u, j, 0)
                    attend(u, j, 1)

                def split(u, j):
                    for bank in range(2):
                        c = slice(2 * bank, 2 * bank + 2)
                        v.wait_ge(m["mhi"], (u.n * 7 + j) * 2 + bank + 1)
                        v.tensor_tensor(ms[:, (j + 1) % 2, 1, c, 0:DH + 1], mem[:, c, 0:DH + 1],
                                        ms[:, (j + 1) % 2, 0, c, 0:DH + 1], ALU.subtract).then_inc(m["mlo"], 1)

                v.wait_ge(m["const_in"], 32)
                v.wait_ge(m["beta_r"], 1)
                units(v, dict(sigma=sigma, key_lo=key_lo, row_max=row_max, row_sum=row_sum, pt_lo=pt_lo,
                              dot_out=dot_out), retrieve, update, split)


def attn1_phase(nc, w_dram, tabs, xt, y, ident):
    NG, HG = 4, 4
    HD = H1 * DH1
    with ExitStack() as ctx:
        ph = Phase(nc, ctx, "a1")
        w32 = ph.sb("w32", [P, KC, 4 * D])
        w = ph.sb("w", [P, 2, KC, 4 * D], F16)
        cos = ph.sb("cos", [P, TPB, DH1])
        sin = ph.sb("sin", [P, TPB, DH1])
        qdec = ph.sb("qdec", [P, H1])
        kdec = ph.sb("kdec", [P, H1])
        rc = ph.sb("rc", [P, NG])
        kvmask = ph.sb("kvmask", [P, HG * DH1])
        dmask = ph.sb("dmask", [P, HG, NG * P])
        rms_w = ph.sb("rms_w", [P, D])
        ra = ph.sb("ra", [P, 2 * H1, DH1])
        rb = ph.sb("rb", [P, 2 * H1, DH1])
        qks = ph.sb("qks", [P, 2 * H1, 2, DH1], F16)
        kx = ph.sb("kx", [P, H1, 2, DH1], F16)
        kd32 = ph.sb("kd32", [P, H1, DH1])
        kd = ph.sb("kd", [P, 2, 2, H1, 2, DH1], F16)
        vs = ph.sb("vs", [P, 2, 2, D], F16)
        qkt = ph.sb("qkt", [P, 2, 2, NG, P], F16)
        kxt = ph.sb("kxt", [P, 2, NG, P], F16)
        sd = ph.sb("sd", [P, HG, NG * P])
        sds = ph.sb("sds", [P, 2, HG, NG * P], F16)
        kv = ph.sb("kv", [P, NG, HG * DH1])
        kvu = ph.sb("kvu", [P, NG, HG * DH1])
        kvs = ph.sb("kvs", [P, 2, 2, NG, HG * DH1], F16)
        at = ph.sb("at", [P, HD])
        sq = ph.sb("sq", [P, HD])
        ss = ph.sb("ss", [P, 1])
        std = ph.sb("std", [P, 1])
        rstd = ph.sb("rstd", [P, 1])
        ats = ph.sb("ats", [P, 2, HD], F16)
        att = ph.sb("att", [P, 2, KC, P], F16)
        qkp = ph.ps("qkp", [P, 2 * D])
        vyp = ph.ps("vyp", [P, 2 * D])
        tqk = ph.ps("tqk", [P, 2, NG, P], F16)
        tx = ph.ps("tx", [P, 2, NG, P], F16)
        sp_ = [ph.ps(f"sc{i}", [P, NG * P]) for i in range(HG)]
        op, upd = sp_[0], sp_[1]

        names = ("in_ w_hi w_lo init qk_full v_full a_rot a_rb r_ready qkhi qklo kxr kxc kd_ready kdhi kdlo vhi vlo"
                 " t_full tx_full qkt_r kxt_r sc_full sd_r sdhi sdlo sdlov out_full upd_full sc_free kvu_r kv_r"
                 " kvhi kvlo kv_reset ra_r at_r ss_r ms_r std_r rstd_r an_r anhi anlo att_full atthi attlo"
                 " y_full y_out dvo").split()
        m = {n: ph.sem(n) for n in names}

        def three(pe, out, wa, xa, start, stop):
            for n, (i, j) in enumerate(((0, 0), (0, 1), (1, 0))):
                last = pe.matmul(out, wa(i), xa(j), start=start and n == 0, stop=stop and n == 2,
                                 skip_group_check=True)
            return last

        def tiles(eng, a, begin, rest, reset=None):
            a(0, 0, 0, 0)
            begin(0, 0, None)
            with eng.Fori(0, B) as b:
                if reset is not None:
                    reset(b)
                with eng.Fori(0, TPB // 2) as k:
                    for par in range(2):
                        t = b * TPB + k * 2 + par
                        rest(b, t, par)
                        begin(t + 1, 1 - par, t)

        with nc.Block() as block:
            @block.sync
            def _(sp):
                sp.dma_start(w32[:], w_dram).then_inc(m["in_"], 16)
                for n, dst in (("cos", cos), ("sin", sin), ("qdec", qdec), ("kdec", kdec), ("rc", rc),
                               ("kvmask", kvmask), ("dmask", dmask)):
                    sp.dma_start(dst[:], tabs[n]).then_inc(m["in_"], 16)
                sp.dma_start(rms_w[:], tabs["rms_w"].to_broadcast([P, D])).then_inc(m["in_"], 16)
            n_in = 16 * 9

            @block.tensor
            def _(pe):
                def stage_qk(tile):
                    for kc in range(KC):
                        last = three(pe, qkp[:], lambda i: xt[:, i, kc, ds(tile * P, P)],
                                     lambda j: w[:, j, kc, 0:2 * D], kc == 0, kc == KC - 1)
                    last.then_inc(m["qk_full"], 1)

                def stage_v(tile):
                    for kc in range(KC):
                        last = three(pe, vyp[:, 0:D], lambda i: xt[:, i, kc, ds(tile * P, P)],
                                     lambda j: w[:, j, kc, 2 * D:3 * D], kc == 0, kc == KC - 1)
                    last.then_inc(m["v_full"], 1)

                def stage_a2(n):
                    pe.wait_ge(m["qkhi"], n + 1)
                    pe.wait_ge(m["qklo"], n + 1)
                    flat = qks[:].rearrange("p h s d -> p (h s d)")
                    for c in range(2 * NG):
                        last = pe.transpose(tqk[:, c // NG, c % NG, :], flat[:, c * P:(c + 1) * P], ident[:])
                    last.then_inc(m["t_full"], 1)
                    pe.wait_ge(m["kxr"], n + 1)
                    pe.wait_ge(m["kxc"], n + 1)
                    flat = kx[:].rearrange("p h s d -> p (h s d)")
                    for c in range(NG):
                        last = pe.transpose(tx[:, 0, c, :], flat[:, c * P:(c + 1) * P], ident[:])
                    last.then_inc(m["tx_full"], 1)

                def a(n, tile, pos, par):
                    stage_qk(tile)
                    stage_v(tile)
                    stage_a2(n)

                def rest(batch, t, par):
                    n = t + 1
                    pe.wait_ge(m["vlo"], n)
                    pe.wait_ge(m["y_out"], n)
                    stage_v(n % TILES)
                    pe.wait_ge(m["kdhi"], n)
                    pe.wait_ge(m["kdlo"], n)
                    pe.wait_ge(m["sd_r"], n * HG)
                    for g in range(NG):
                        last = three(pe, upd[:, g * HG * DH1:(g + 1) * HG * DH1],
                                     lambda i: kd[:, par, i, g * HG:(g + 1) * HG].rearrange(
                                         "p h s d -> p (h s d)"),
                                     lambda j: vs[:, par, j, g * HG * DH1:(g + 1) * HG * DH1],
                                     g == 0, g == NG - 1)
                    last.then_inc(m["upd_full"], 1)
                    pe.wait_ge(m["kvlo"], n + batch)
                    for g in range(NG):
                        for j in range(2):
                            pe.matmul(op[:, HD + g * 64:HD + (g + 1) * 64], qkt[:, par, 0, g, :],
                                      kvs[:, par, j, g, :], start=g == 0 and j == 0, stop=False,
                                      skip_group_check=True)
                    for i in range(HG):
                        pe.wait_ge(m["sdhi"], t * HG + i + 1)
                        if i < HG - 1:
                            pe.wait_ge(m["sdlo"], t * (HG - 1) + i + 1)
                        else:
                            pe.wait_ge(m["sdlov"], n)
                        for g in range(NG):
                            h = HG * g + i
                            last = three(pe, op[:, h * DH1:(h + 1) * DH1],
                                         lambda j: sds[:, j, i, g * P:(g + 1) * P],
                                         lambda j: vs[:, par, j, h * DH1:(h + 1) * DH1], False, i == HG - 1)
                    last.then_inc(m["out_full"], 1)
                    stage_a2(n)

                def begin(n, par, t):
                    pe.wait_ge(m["qkt_r"], n + 1)
                    pe.wait_ge(m["kxt_r"], n + 1)
                    if t is not None:
                        pe.wait_ge(m["at_r"], n)
                        pe.wait_ge(m["kv_r"], n)
                    for g in range(NG):
                        for i in range(HG):
                            rows = slice(32 * i, 32 * i + 32)
                            pe.matmul(sp_[i][:, g * P:(g + 1) * P], qkt[rows, par, 1, g, :],
                                      qkt[rows, par, 0, g, :], start=g == 0, stop=False,
                                      skip_group_check=True)
                            last = pe.matmul(sp_[i][:, g * P:(g + 1) * P], kxt[rows, par, g, :],
                                             qkt[rows, par, 0, g, :], start=False, stop=g == NG - 1,
                                             skip_group_check=True)
                            if g == NG - 1:
                                last.then_inc(m["sc_full"], 1)
                    pe.wait_ge(m["ra_r"], n * 3 + 3)
                    stage_qk((n + 1) % TILES)
                    if t is None:
                        return
                    pe.wait_ge(m["anhi"], n)
                    pe.wait_ge(m["anlo"], n)
                    for j in range(2):
                        for kc in range(KC):
                            last = pe.transpose(tx[:, 1, j * KC + kc, :], ats[:, j, kc * P:(kc + 1) * P], ident[:])
                    last.then_inc(m["att_full"], 1)
                    pe.wait_ge(m["atthi"], n)
                    pe.wait_ge(m["vlo"], n + 1)
                    for kc in range(KC):
                        last = three(pe, vyp[:, D:2 * D], lambda i: att[:, i, kc, :],
                                     lambda j: w[:, j, kc, 3 * D:4 * D], kc == 0, kc == KC - 1)
                    last.then_inc(m["y_full"], 1)

                pe.wait_ge(m["w_lo"], 1)
                tiles(pe, a, begin, rest)

            @block.scalar
            def _(act):
                act.preload_act_table(ACT.Sqrt)
                act.wait_ge(m["in_"], n_in)
                act.activation(w[:, 0], w32[:], ACT.Copy, scale=WSCALE).then_inc(m["w_hi"], 1)

                def a1(n, par):
                    act.wait_ge(m["v_full"], n + 1)
                    act.activation(vs[:, par, 0, :], vyp[:, 0:D], ACT.Copy, scale=1 / WSCALE).then_inc(m["vhi"], 1)
                    act.wait_ge(m["r_ready"], n + 1)
                    act.activation(qks[:, :, 0, :], ra[:], ACT.Copy).then_inc(m["qkhi"], 1)
                    act.activation(kx[:, :, 1, :], ra[:, H1:2 * H1, :], ACT.Copy).then_inc(m["kxc"], 1)

                def a2(n, par):
                    act.wait_ge(m["kd_ready"], n + 1)
                    act.activation(kd[:, par, 0], bcast(kd32[:].unsqueeze(2), P, H1, 2, DH1),
                                   ACT.Copy).then_inc(m["kdhi"], 1)
                    act.wait_ge(m["t_full"], n + 1)
                    act.activation(qkt[:, par], tqk[:], ACT.Copy).then_inc(m["qkt_r"], 1)

                def a(n, tile, pos, par):
                    a1(n, par)
                    a2(n, par)

                def rest(batch, t, par):
                    n = t + 1
                    a1(n, 1 - par)
                    act.wait_ge(m["kv_r"], n)
                    act.activation(kvs[:, 1 - par, 0], kv[:], ACT.Copy).then_inc(m["kvhi"], 1)
                    a2(n, 1 - par)
                    act.wait_ge(m["at_r"], n)
                    act.activation(sq[:], at[:], ACT.Square, accum_out=ss[:]).then_inc(m["ss_r"], 1)
                    act.wait_ge(m["ms_r"], n)
                    act.activation(std[:], ss[:], ACT.Sqrt).then_inc(m["std_r"], 1)

                def begin(n, par, t):
                    if t is not None:
                        act.wait_ge(m["an_r"], n)
                        act.activation(ats[:, 0, :], at[:], ACT.Copy).then_inc(m["anhi"], 1)
                    for i in range(HG):
                        act.wait_ge(m["sd_r"], n * HG + i + 1)
                        act.activation(sds[:, 0, i, :], sd[:, i, :], ACT.Copy).then_inc(m["sdhi"], 1)
                    if t is not None:
                        act.wait_ge(m["att_full"], n)
                        act.activation(att[:].rearrange("p a k c -> p (a k) c"), tx[:, 1], ACT.Copy).then_inc(m["atthi"], 1)
                        act.wait_ge(m["y_full"], n)
                        act.activation(y[:, ds(t, 1), :], vyp[:, D:2 * D], ACT.Copy,
                                       scale=1 / WSCALE).then_inc(m["y_out"], 1)

                tiles(act, a, begin, rest)

            @block.gpsimd
            def _(pool):
                def a(n, tile, pos, par):
                    pool.wait_ge(m["ra_r"], n * 3 + 3)
                    pool.tensor_tensor(ra[:], ra[:], rb[:], ALU.add).then_inc(m["r_ready"], 1)
                    pool.wait_ge(m["r_ready"], n + 1)
                    pool.tensor_tensor(kd32[:], ra[:, H1:2 * H1, :], bcast(kdec[:].unsqueeze(2), P, H1, DH1),
                                       ALU.mult).then_inc(m["kd_ready"], 1)
                    pool.wait_ge(m["qklo"], n + 1)
                    pool.tensor_tensor(kx[:, :, 0, :], ra[:, H1:2 * H1, :], qks[:, H1:2 * H1, 0, :],
                                       ALU.subtract).then_inc(m["kxr"], 1)

                def rest(batch, t, par):
                    a(t + 1, 0, 0, 1 - par)

                def begin(n, par, t):
                    for i in range(HG - 1):
                        pool.wait_ge(m["sdhi"], n * HG + i + 1)
                        pool.tensor_tensor(sds[:, 1, i, :], sd[:, i, :], sds[:, 0, i, :],
                                           ALU.subtract).then_inc(m["sdlo"], 1)

                pool.wait_ge(m["in_"], n_in)
                tiles(pool, a, begin, rest)

            @block.vector
            def _(v):
                done = [0]
                v.wait_ge(m["w_hi"], 1)
                v.scalar_tensor_tensor(w[:, 1].rearrange("p k c -> p (k c)"),
                                       w32[:].rearrange("p k c -> p (k c)"), WSCALE,
                                       w[:, 0].rearrange("p k c -> p (k c)"),
                                       ALU.mult, ALU.subtract).then_inc(m["w_lo"], 1)
                v.sem_inc(m["y_out"], 1)

                def a1(n, pos):
                    v.wait_ge(m["qk_full"], n + 1)
                    q = qkp[:].rearrange("p (h d) -> p h d", d=DH1)
                    half = DH1 // 2

                    def tab(tb, lo, hi):
                        return tb[:, ds(pos, 1), lo:hi].to_broadcast([P, 2 * H1, hi - lo])
                    v.tensor_tensor(ra[:], q, tab(cos, 0, DH1), ALU.mult).then_inc(m["ra_r"], 1)
                    v.tensor_tensor(rb[:, :, 0:half], q[:, :, half:], tab(sin, 0, half),
                                    ALU.mult).then_inc(m["ra_r"], 1)
                    v.tensor_tensor(rb[:, :, half:], q[:, :, 0:half], tab(sin, half, DH1),
                                    ALU.mult).then_inc(m["ra_r"], 1)

                def a2(n, par):
                    v.wait_ge(m["vhi"], n + 1)
                    v.scalar_tensor_tensor(vs[:, par, 1, :], vyp[:, 0:D], 1 / WSCALE, vs[:, par, 0, :],
                                           ALU.mult, ALU.subtract).then_inc(m["vlo"], 1)
                    v.wait_ge(m["qkhi"], n + 1)
                    v.tensor_tensor(qks[:, :, 1, :], ra[:], qks[:, :, 0, :], ALU.subtract).then_inc(m["qklo"], 1)
                    v.wait_ge(m["kdhi"], n + 1)
                    for rep in range(2):
                        ins = v.tensor_tensor(kd[:, par, 1, :, rep], kd32[:], kd[:, par, 0, :, rep], ALU.subtract)
                    ins.then_inc(m["kdlo"], 1)

                def a3(n, par):
                    v.wait_ge(m["tx_full"], n + 1)
                    v.tensor_copy(kxt[:, par], tx[:, 0]).then_inc(m["kxt_r"], 1)

                def a(n, tile, pos, par):
                    a1(n, pos)
                    a2(n, par)
                    a3(n, par)

                def reset(b):
                    v.memset(kv[:], 0.0).then_inc(m["kv_reset"], 1)
                    v.memset(kvs[:, 0, 0], 0.0).then_inc(m["kv_reset"], 1)
                    v.wait_ge(m["kv_reset"], b * 2 + 2)
                    v.memset(kvs[:, 0, 1], 0.0).then_inc(m["kvlo"], 1)

                def rest(batch, t, par):
                    n = t + 1
                    v.wait_ge(m["upd_full"], n)
                    v.tensor_tensor(kvu[:], upd[:, 0:HD].rearrange("p (g e) -> p g e", g=NG),
                                    bcast(kvmask[:].unsqueeze(1), P, NG, HG * DH1), ALU.mult).then_inc(m["dvo"], 1)
                    v.tensor_tensor(kv[:], kv[:], bcast(rc[:].unsqueeze(2), P, NG, HG * DH1),
                                    ALU.mult).then_inc(m["dvo"], 1)
                    v.wait_ge(m["dvo"], t * 4 + 2)
                    v.tensor_tensor(kv[:], kv[:], kvu[:], ALU.add).then_inc(m["kv_r"], 1)
                    a2(n, 1 - par)
                    v.wait_ge(m["kvhi"], n)
                    v.tensor_tensor(kvs[:, 1 - par, 1], kv[:], kvs[:, 1 - par, 0],
                                    ALU.subtract).then_inc(m["kvlo"], 1)
                    v.wait_ge(m["out_full"], n)
                    v.tensor_tensor(at[:].rearrange("p (h e) -> p h e", h=H1),
                                    op[:, HD:].rearrange("p (h e) -> p h e", h=H1),
                                    bcast(qdec[:].unsqueeze(2), P, H1, DH1), ALU.mult).then_inc(m["dvo"], 1)
                    v.wait_ge(m["dvo"], t * 4 + 3)
                    v.tensor_tensor(at[:], at[:], op[:, 0:HD], ALU.add).then_inc(m["at_r"], 1)
                    a3(n, 1 - par)
                    v.wait_ge(m["ss_r"], n)
                    v.tensor_scalar(ss[:], ss[:], 1.0 / HD, LN_EPS, ALU.mult, ALU.add).then_inc(m["ms_r"], 1)
                    v.wait_ge(m["std_r"], n)
                    v.reciprocal(rstd[:], std[:]).then_inc(m["dvo"], 1)
                    v.wait_ge(m["dvo"], t * 4 + 4)
                    v.scalar_tensor_tensor(at[:], at[:], rstd[:], rms_w[:], ALU.mult,
                                           ALU.mult).then_inc(m["an_r"], 1)

                def begin(n, par, t):
                    if t is not None:
                        v.wait_ge(m["anhi"], n)
                        v.tensor_tensor(ats[:, 1, :], at[:], ats[:, 0, :], ALU.subtract).then_inc(m["anlo"], 1)
                    for i in range(HG):
                        v.wait_ge(m["sc_full"], n * HG + i + 1)
                        v.tensor_tensor(sd[:, i, :], sp_[i][:], dmask[:, i, :], ALU.mult).then_inc(m["sd_r"], 1)
                    a1(n + 1, (n + 1) % TPB)
                    v.wait_ge(m["sdhi"], n * HG + HG)
                    v.tensor_tensor(sds[:, 1, HG - 1, :], sd[:, HG - 1, :], sds[:, 0, HG - 1, :],
                                    ALU.subtract).then_inc(m["sdlov"], 1)

                tiles(v, a, begin, rest, reset)


def _pack_ffn(w1, w3, w2, ht_n):
    import numpy as np
    rows = ht_n * P
    out = np.zeros((ht_n, P, 2 * KC * P + D), np.float32)
    for n, w in enumerate((w1, w3)):
        full = np.zeros((rows, D), np.float32)
        full[:w.shape[0]] = w
        out[:, :, n * D:(n + 1) * D] = full.reshape(ht_n, P, KC, P).transpose(0, 3, 2, 1).reshape(ht_n, P, D)
    full = np.zeros((rows, D), np.float32)
    full[:w2.shape[0]] = w2
    out[:, :, 2 * D:] = full.reshape(ht_n, P, D)
    return out


def _by_kc(w):
    return w.reshape(KC, P, -1).transpose(1, 0, 2)


def _pack_attn0(wq, wk, wv):
    import numpy as np
    parts = [w.reshape(KC, P, GROUPS, HG * DH).transpose(2, 1, 0, 3).reshape(GROUPS, P, -1) for w in (wq, wk, wv)]
    return np.concatenate(parts, axis=2)


def _rows(v, ht_n):
    import numpy as np
    out = np.zeros(ht_n * P, np.float32)
    out[:v.shape[0]] = v
    return np.ascontiguousarray(out.reshape(ht_n, P).T)


def _expand():
    import numpy as np
    e = np.zeros((32, HT0 * P), np.float16)
    for n in range(E0 + 1):
        e[[n, 16 + n], n * HID0:(n + 1) * HID0] = 1
    return e


def _tables():
    import numpy as np
    f = np.float32
    quarter = DH1 // 4
    freq = np.concatenate([(f(1) / f(1024)) ** np.linspace(0, 1, quarter, dtype=f), np.zeros(quarter, f)])
    theta = (np.arange(S, dtype=f)[:, None] * freq[None, :]).astype(f)
    cos, sin = np.cos(theta), np.sin(theta)
    by_tile = lambda a: (a / WSCALE).reshape(TPB, P, DH1).transpose(1, 0, 2).astype(f)
    slopes = (2.0 ** -0.5) ** np.arange(1, H1 + 1)
    r = np.exp(-slopes)
    i = np.arange(CHUNK)
    head = np.arange(P)[:, None] // 32 + 4 * np.arange(4)[None, :]
    diff = i[None, :] - i[:, None]
    dm = np.where(diff[:, None] >= 0, r[None, :, None] ** np.maximum(diff, 0)[:, None], 0)
    return {
        "cos": by_tile(np.concatenate([cos, cos], 1)), "sin": by_tile(np.concatenate([sin, -sin], 1)),
        "qdec": (r[None] ** (i[:, None] + 1.0)).astype(f), "kdec": (r[None] ** (CHUNK - 1.0 - i[:, None])).astype(f),
        "rc": (r[head] ** CHUNK).astype(f),
        "kvmask": (np.arange(P)[:, None] // 32 == np.arange(64)[None, :] // DH1).astype(f),
        "dmask": dm.reshape(P, 4, 4, P).transpose(0, 2, 1, 3).reshape(P, 4, 4 * P).astype(f),
    }


def prepare(inputs):
    import numpy as np
    i = {k: np.asarray(v) for k, v in inputs.items()}
    a = {"x": i["L0_attn_x"]}
    a["eye"] = np.eye(P, dtype=np.float16)
    a["w_attn0"] = _pack_attn0(i["L0_attn_Wq"], i["L0_attn_Wk"], i["L0_attn_Wv"])
    a["wo_attn0"] = i["L0_attn_Wo"].reshape(H0, DH, D).transpose(1, 0, 2).reshape(P, H0 * D)
    a["betas"] = i["L0_attn_betas"].reshape(1, H0 * DH)
    flat = lambda w: w.reshape(-1, w.shape[-1])
    a["w_ffn0"] = _pack_ffn(np.concatenate([i["L0_ffn_sw1"], flat(i["L0_ffn_ew1"])]),
                            np.concatenate([i["L0_ffn_sw3"], flat(i["L0_ffn_ew3"])]),
                            np.concatenate([i["L0_ffn_sw2"].T, flat(i["L0_ffn_ew2"].transpose(0, 2, 1))]), HT0)
    a["wr"] = np.ascontiguousarray(_by_kc(i["L0_ffn_wr"].T))
    a["expand"] = _expand()
    a["w_ffn1"] = _pack_ffn(i["L1_ffn_gate_w"], i["L1_ffn_up_w"], i["L1_ffn_down_w"].T, HT1)
    a["gate_s"] = _rows(i["L1_ffn_gate_s"], HT1)
    a["up_s"] = _rows(i["L1_ffn_up_s"], HT1)
    a["down_s"] = i["L1_ffn_down_s"].reshape(1, D)
    a["w_attn1"] = np.concatenate([_by_kc(i["L1_attn_W" + n]) for n in "qkvo"], axis=2)
    a["mask"] = np.where(np.arange(SEG)[None] <= np.arange(P)[:, None] % SEG, 0, -1e30).astype(np.float32)
    a["rms_w"] = i["L1_attn_rms_w"].reshape(1, D)
    a.update(_tables())
    return {k: np.ascontiguousarray(v) for k, v in a.items()}


def network(nc, t, out):
    with ExitStack() as ctx:
        xt = ctx.enter_context(nc.sbuf_tensor("xt", [P, 2, KC, TOK], F16))
        ident = ctx.enter_context(nc.sbuf_tensor("ident", [P, P], F16))
        loaded = ctx.enter_context(nc.semaphore("ident_loaded"))
        with nc.Block() as block:
            @block.sync
            def _(sp):
                sp.dma_start(ident[:], t["eye"]).then_inc(loaded, 16)
                sp.wait_ge(loaded, 16)
        with ExitStack() as first:
            x = first.enter_context(nc.sbuf_tensor("x_first", [P, TILES, D], F32))
            norm_phase(nc, "n0", ident, x, None, xt, load_x=t["x"])
        y_dram = nc.dram_tensor("y_attn0", (B, S, D), F32, kind="Internal").ap()
        attn0_phase(nc, t["w_attn0"], t["wo_attn0"], t["betas"], t["mask"], xt, y_dram, ident)
        y = ctx.enter_context(nc.sbuf_tensor("y", [P, TILES, D], F32))
        x = ctx.enter_context(nc.sbuf_tensor("x_sb", [P, TILES, D], F32))
        norm_phase(nc, "n1", ident, x, y, xt, load_x=t["x"], load_y=y_dram)
        ffn_phase(nc, "f0", t["w_ffn0"], xt, y, HT0, ident, router=(t["wr"], t["expand"]))
        norm_phase(nc, "n2", ident, x, y, xt)
        attn1_phase(nc, t["w_attn1"], t, xt, y, ident)
        norm_phase(nc, "n3", ident, x, y, xt)
        ffn_phase(nc, "f1", t["w_ffn1"], xt, y, HT1, ident, scales=(t["gate_s"], t["up_s"], t["down_s"]))
        norm_phase(nc, "n4", ident, x, y, None, store=out)


def kernel(**inputs):
    import concourse.bacc as _bacc
    from concourse.bass_utils import run_bass_kernel_spmd as _run

    arrays = prepare(inputs)
    nc = _bacc.Bacc("TRN2", target_bir_lowering=False, num_devices=1)
    tensors = {name: nc.dram_tensor(name, a.shape, mybir.dt.from_np(a.dtype), kind="ExternalInput").ap()
               for name, a in arrays.items()}
    out = nc.dram_tensor("out", (B, S, D), F32, kind="ExternalOutput").ap()
    network(nc, tensors, out)
    r = _run(nc, [arrays], core_ids=[0])
    return r.results[0]["out"]
```
